# Optimizing a Trainium2 kernel written in Bass

```python
import numpy as np
import jax
import jax.numpy as jnp

def _softmax(x, axis=-1):
    return jax.nn.softmax(x, axis=axis)

def _gelu(x):
    return jax.nn.gelu(x, approximate=True)

def _silu(x):
    return jax.nn.silu(x)

def _sigmoid(x):
    return jax.nn.sigmoid(x)

def _layernorm(x, axis=-1, eps=1e-05):
    m = jnp.mean(x, axis=axis, keepdims=True)
    v = jnp.var(x, axis=axis, keepdims=True)
    return (x - m) / jnp.sqrt(v + eps)

def _scatter_add(tgt, idx, src, axis=0):
    return tgt.at[idx].add(src)

def _segment_sum(src, seg, n):
    return jax.ops.segment_sum(src, seg, n)
kernel_name = 'mk_gnn_resnorm_d4_gnn_r8_be2068'

def setup_inputs(seed: int=0):
    np.random.seed(seed)
    _w = jnp.asarray

    def _rec_inputs():
        import jax
        import jax.numpy as jnp
        _gk = jax.random.key(seed)
        x = -6.985e-05 + 0.9998 * jax.random.normal(jax.random.fold_in(_gk, 1), (1250, 512), jnp.float32)
        src = jax.random.randint(jax.random.fold_in(_gk, 2), (20000,), 0, 1250, jnp.int32)
        dst = jax.random.randint(jax.random.fold_in(_gk, 3), (20000,), 0, 1250, jnp.int32)
        _o = jnp.argsort(dst, stable=True)
        src = src[_o]
        dst = dst[_o]
        node_vec1 = jax.random.uniform(jax.random.fold_in(_gk, 13), (1250, 1), jnp.float32, 0.0, 0.999957)
        return (x, src, dst, node_vec1)
    x, src, dst, node_vec1 = _rec_inputs()

    def _L0_gnn_setup():
        import jax, jax.numpy as jnp
        import numpy as np
        B = 32
        MAXN = 256
        HEADS = 8
        DH = 64
        M = 256
        D = 512
        EPS = 1e-05
        KEPS = 1e-06

        def _batchnorm(x, g, b):
            mu = jnp.mean(x, axis=0)
            var = jnp.mean((x - mu) ** 2, axis=0)
            return (x - mu) * jax.lax.rsqrt(var + EPS) * g + b

        def _forward(x, batch, edge_index, norm1_g, norm1_b, norm2_g, norm2_b, W_conv, b_conv, Wq, Wk, Wv, Wo, proj):
            N = x.shape[0]
            E = edge_index.shape[1]
            h = x
            xn = _batchnorm(x, norm1_g, norm1_b)
            msg = xn[edge_index[0]]
            agg = jax.ops.segment_sum(msg, edge_index[1], num_segments=N)
            deg = jax.ops.segment_sum(jnp.ones((E,), x.dtype), edge_index[1], num_segments=N)
            agg = agg / jnp.maximum(deg, 1.0)[:, None]
            conv_out = jax.nn.relu(agg @ W_conv + b_conv)
            counts = jax.ops.segment_sum(jnp.ones((N,), jnp.int32), batch, num_segments=B)
            offsets = jnp.concatenate([jnp.zeros((1,), jnp.int32), jnp.cumsum(counts)[:-1]])
            pos = jnp.arange(N, dtype=jnp.int32) - offsets[batch]
            h_dense = jnp.zeros((B, MAXN, D), x.dtype).at[batch, pos].set(h)
            mask = jnp.zeros((B, MAXN), bool).at[batch, pos].set(True)

            def heads(t, W):
                return (t @ W).reshape(B, MAXN, HEADS, DH).transpose(0, 2, 1, 3)
            q, k, v = (heads(h_dense, Wq), heads(h_dense, Wk), heads(h_dense, Wv))
            scale = DH ** (-0.25)

            def phi(t, is_query):
                t = t * scale
                u = jnp.einsum('bhnd,md->bhnm', t, proj)
                diag = 0.5 * jnp.sum(t * t, axis=-1, keepdims=True)
                if is_query:
                    m_ = jnp.max(u, axis=-1, keepdims=True)
                else:
                    m_ = jnp.max(u, axis=(-2, -1), keepdims=True)
                return jnp.exp(u - diag - jax.lax.stop_gradient(m_)) / np.sqrt(M) + KEPS
            qf = phi(q, True)
            kf = phi(k, False) * mask[:, None, :, None]
            vm = v * mask[:, None, :, None]
            kv = jnp.einsum('bhnm,bhnd->bhmd', kf, vm)
            z = 1.0 / (jnp.einsum('bhnm,bhm->bhn', qf, kf.sum(axis=2)) + KEPS)
            attn = jnp.einsum('bhnm,bhmd->bhnd', qf, kv) * z[..., None]
            attn = attn.transpose(0, 2, 1, 3).reshape(B, MAXN, D) @ Wo
            h_attn = attn[batch, pos]
            return _batchnorm(conv_out + h_attn + h, norm2_g, norm2_b)
        key = jax.random.key(seed)
        ks = jax.random.split(key, 10)
        sizes = 1024 + np.arange(B) * 131 % 1025
        N = int(sizes.sum())
        E = N * 8
        batch = jnp.asarray(np.repeat(np.arange(B), sizes), dtype=jnp.int32)
        edge_index = jax.random.randint(ks[0], (2, E), 0, N, dtype=jnp.int32)
        s = 1.0 / np.sqrt(D)
        return {'x': jax.random.normal(ks[1], (N, D), jnp.float32), 'batch': batch, 'edge_index': edge_index, 'norm1_g': jnp.ones((D,), jnp.float32), 'norm1_b': jnp.zeros((D,), jnp.float32), 'norm2_g': jnp.ones((D,), jnp.float32), 'norm2_b': jnp.zeros((D,), jnp.float32), 'W_conv': jax.random.normal(ks[2], (D, D), jnp.float32) * s, 'b_conv': jnp.zeros((D,), jnp.float32), 'Wq': jax.random.normal(ks[3], (D, D), jnp.float32) * s, 'Wk': jax.random.normal(ks[4], (D, D), jnp.float32) * s, 'Wv': jax.random.normal(ks[5], (D, D), jnp.float32) * s, 'Wo': jax.random.normal(ks[6], (D, D), jnp.float32) * s, 'proj': jax.random.normal(ks[7], (M, DH), jnp.float32)}
    _L0_gnn_all = _L0_gnn_setup()
    _L0_gnn_in = {k: v for k, v in _L0_gnn_all.items() if k in ('norm1_g', 'norm1_b', 'norm2_g', 'norm2_b', 'W_conv', 'b_conv', 'Wq', 'Wk', 'Wv', 'Wo', 'proj')}
    del _L0_gnn_all

    def _L1_gnn_setup():
        import jax, jax.numpy as jnp
        import numpy as np
        N, E, H, D_IN, D_PRIME = (6250, 100000, 8, 512, 64)

        def _segment_softmax(scores, seg, num_segments):
            smax = jax.ops.segment_max(scores, seg, num_segments=num_segments)
            ex = jnp.exp(scores - smax[seg])
            denom = jax.ops.segment_sum(ex, seg, num_segments=num_segments)
            return ex / denom[seg]
        key = jax.random.key(seed)
        ks = jax.random.split(key, 6)
        x = jax.random.normal(ks[0], (N, D_IN), dtype=jnp.float32)
        edge_index = jax.random.randint(ks[1], (2, E), 0, N)
        Ws = jax.random.normal(ks[2], (H, D_IN, D_PRIME), dtype=jnp.float32) * 0.05
        Wb = jax.random.normal(ks[3], (H, D_PRIME), dtype=jnp.float32) * 0.05
        a_w = jax.random.normal(ks[4], (H, 2 * D_PRIME), dtype=jnp.float32) * 0.05
        a_b = jax.random.normal(ks[5], (H,), dtype=jnp.float32) * 0.05
        return dict(x=x, edge_index=edge_index, Ws=Ws, Wb=Wb, a_w=a_w, a_b=a_b)
    _L1_gnn_all = _L1_gnn_setup()
    _L1_gnn_in = {k: v for k, v in _L1_gnn_all.items() if k in ('Ws', 'Wb', 'a_w', 'a_b')}
    del _L1_gnn_all

    def _L2_gnn_setup():
        import jax, jax.numpy as jnp
        import numpy as np
        N = 6250
        E = 100000
        D = 512

        def _gcn_conv(x, edge_index, W, b):
            n = x.shape[0]
            xw = x @ W.T
            loop = jnp.arange(n, dtype=edge_index.dtype)
            row = jnp.concatenate([edge_index[0], loop])
            col = jnp.concatenate([edge_index[1], loop])
            deg = jax.ops.segment_sum(jnp.ones_like(row, dtype=xw.dtype), col, num_segments=n)
            dinv = jnp.where(deg > 0, jax.lax.rsqrt(deg), 0.0)
            norm = dinv[row] * dinv[col]
            msgs = norm[:, None] * xw[row]
            out = jax.ops.segment_sum(msgs, col, num_segments=n)
            return out + b

        def _batch_norm(h, gamma, beta, eps=1e-05):
            mean = jnp.mean(h, axis=0)
            var = jnp.var(h, axis=0)
            return (h - mean) * jax.lax.rsqrt(var + eps) * gamma + beta
        key = jax.random.key(seed)
        k1, k2, k3, k4, k5, k6 = jax.random.split(key, 6)
        x = jax.random.normal(k1, (N, D), dtype=jnp.float32)
        edge_index = jax.random.randint(k2, (2, E), 0, N, dtype=jnp.int64)
        W = jax.random.normal(k3, (D, D), dtype=jnp.float32) * (1.0 / np.sqrt(D))
        b = jnp.zeros((D,), dtype=jnp.float32)
        gamma = jnp.ones((D,), dtype=jnp.float32)
        beta = jnp.zeros((D,), dtype=jnp.float32)
        return {'x': x, 'edge_index': edge_index, 'W': W, 'b': b, 'gamma': gamma, 'beta': beta}
    _L2_gnn_all = _L2_gnn_setup()
    _L2_gnn_in = {k: v for k, v in _L2_gnn_all.items() if k in ('W', 'b', 'gamma', 'beta')}
    del _L2_gnn_all

    def _L3_gnn_setup():
        import jax, jax.numpy as jnp
        import numpy as np
        N_NODES = 40962
        LATENT_DIM = 512
        N_EDGES = 81924
        NUM_BLOCKS = 4
        NUM_HEADS = 4
        NUM_FREQ = 32
        BASE_PERIOD = 16
        NOISE_EMB_DIM = 16
        EPS = 1e-05

        def _cond_layer_norm(x, cond, sw, sb, bw, bb):
            mu = jnp.mean(x, axis=-1, keepdims=True)
            var = jnp.var(x, axis=-1, keepdims=True)
            xn = (x - mu) * jax.lax.rsqrt(var + EPS)
            scale = cond @ sw + sb
            bias = cond @ bw + bb
            return xn * (1.0 + scale) + bias

        def _sparse_attention(x, src, dst, wq, bq, wk, bk, wv, bv, wo, bo):
            N, D = x.shape
            H, Dh = (NUM_HEADS, D // NUM_HEADS)
            q = (x @ wq + bq).reshape(N, H, Dh) * Dh ** (-0.5)
            k = (x @ wk + bk).reshape(N, H, Dh)
            v = (x @ wv + bv).reshape(N, H, Dh)
            scores = jnp.einsum('ehd,ehd->eh', q[src], k[dst])
            smax = jax.ops.segment_max(scores, src, num_segments=N)
            ex = jnp.exp(scores - smax[src])
            denom = jax.ops.segment_sum(ex, src, num_segments=N)
            attn = ex / denom[src]
            out = jax.ops.segment_sum(attn[:, :, None] * v[dst], src, num_segments=N)
            return out.reshape(N, D) @ wo + bo

        def _forward(x, edge_index, noise_levels, f_w1, f_b1, f_w2, f_b2, s1_w, s1_b, b1_w, b1_b, wq, bq, wk, bk, wv, bv, wo, bo, s2_w, s2_b, b2_w, b2_b, m_w1, m_b1, m_w2, m_b2):
            src, dst = (edge_index[0], edge_index[1])
            freqs = jnp.arange(1, NUM_FREQ + 1, dtype=x.dtype) * (2.0 * np.pi / BASE_PERIOD)
            ph = noise_levels * freqs
            emb = jnp.concatenate([jnp.sin(ph), jnp.cos(ph)], axis=-1)
            cond = jax.nn.silu(emb @ f_w1 + f_b1) @ f_w2 + f_b2
            for i in range(NUM_BLOCKS):
                y = _cond_layer_norm(x, cond, s1_w[i], s1_b[i], b1_w[i], b1_b[i])
                y = _sparse_attention(y, src, dst, wq[i], bq[i], wk[i], bk[i], wv[i], bv[i], wo[i], bo[i])
                x = x + y
                y = _cond_layer_norm(x, cond, s2_w[i], s2_b[i], b2_w[i], b2_b[i])
                y = jax.nn.relu(y @ m_w1[i] + m_b1[i]) @ m_w2[i] + m_b2[i]
                x = x + y
            return x
        key = jax.random.key(seed)
        ks = jax.random.split(key, 20)

        def w(k, shape, s=0.02):
            return jax.random.normal(k, shape, dtype=jnp.float32) * s
        D, B, C = (LATENT_DIM, NUM_BLOCKS, NOISE_EMB_DIM)
        z = lambda *s: jnp.zeros(s, jnp.float32)
        return {'latent_mesh_nodes': jax.random.normal(ks[0], (N_NODES, D), dtype=jnp.float32), 'edge_index': jax.random.randint(ks[1], (2, N_EDGES), 0, N_NODES, dtype=jnp.int32), 'noise_levels': jax.random.uniform(ks[2], (N_NODES, 1), dtype=jnp.float32), 'f_w1': w(ks[3], (2 * NUM_FREQ, C)), 'f_b1': z(C), 'f_w2': w(ks[4], (C, C)), 'f_b2': z(C), 's1_w': w(ks[5], (B, C, D)), 's1_b': z(B, D), 'b1_w': w(ks[6], (B, C, D)), 'b1_b': z(B, D), 'wq': w(ks[7], (B, D, D)), 'bq': z(B, D), 'wk': w(ks[8], (B, D, D)), 'bk': z(B, D), 'wv': w(ks[9], (B, D, D)), 'bv': z(B, D), 'wo': w(ks[10], (B, D, D)), 'bo': z(B, D), 's2_w': w(ks[11], (B, C, D)), 's2_b': z(B, D), 'b2_w': w(ks[12], (B, C, D)), 'b2_b': z(B, D), 'm_w1': w(ks[13], (B, D, D)), 'm_b1': z(B, D), 'm_w2': w(ks[14], (B, D, D)), 'm_b2': z(B, D)}
    _L3_gnn_all = _L3_gnn_setup()
    _L3_gnn_in = {k: v for k, v in _L3_gnn_all.items() if k in ('f_w1', 'f_b1', 'f_w2', 'f_b2', 's1_w', 's1_b', 'b1_w', 'b1_b', 'wq', 'bq', 'wk', 'bk', 'wv', 'bv', 'wo', 'bo', 's2_w', 's2_b', 'b2_w', 'b2_b', 'm_w1', 'm_b1', 'm_w2', 'm_b2')}
    del _L3_gnn_all
    return {'x': x, 'src': src, 'dst': dst, 'node_vec1': node_vec1, 'L0_gnn_norm1_g': _L0_gnn_in['norm1_g'], 'L0_gnn_norm1_b': _L0_gnn_in['norm1_b'], 'L0_gnn_norm2_g': _L0_gnn_in['norm2_g'], 'L0_gnn_norm2_b': _L0_gnn_in['norm2_b'], 'L0_gnn_W_conv': _L0_gnn_in['W_conv'], 'L0_gnn_b_conv': _L0_gnn_in['b_conv'], 'L0_gnn_Wq': _L0_gnn_in['Wq'], 'L0_gnn_Wk': _L0_gnn_in['Wk'], 'L0_gnn_Wv': _L0_gnn_in['Wv'], 'L0_gnn_Wo': _L0_gnn_in['Wo'], 'L0_gnn_proj': _L0_gnn_in['proj'], 'L1_gnn_Ws': _L1_gnn_in['Ws'], 'L1_gnn_Wb': _L1_gnn_in['Wb'], 'L1_gnn_a_w': _L1_gnn_in['a_w'], 'L1_gnn_a_b': _L1_gnn_in['a_b'], 'L2_gnn_W': _L2_gnn_in['W'], 'L2_gnn_b': _L2_gnn_in['b'], 'L2_gnn_gamma': _L2_gnn_in['gamma'], 'L2_gnn_beta': _L2_gnn_in['beta'], 'L3_gnn_f_w1': _L3_gnn_in['f_w1'], 'L3_gnn_f_b1': _L3_gnn_in['f_b1'], 'L3_gnn_f_w2': _L3_gnn_in['f_w2'], 'L3_gnn_f_b2': _L3_gnn_in['f_b2'], 'L3_gnn_s1_w': _L3_gnn_in['s1_w'], 'L3_gnn_s1_b': _L3_gnn_in['s1_b'], 'L3_gnn_b1_w': _L3_gnn_in['b1_w'], 'L3_gnn_b1_b': _L3_gnn_in['b1_b'], 'L3_gnn_wq': _L3_gnn_in['wq'], 'L3_gnn_bq': _L3_gnn_in['bq'], 'L3_gnn_wk': _L3_gnn_in['wk'], 'L3_gnn_bk': _L3_gnn_in['bk'], 'L3_gnn_wv': _L3_gnn_in['wv'], 'L3_gnn_bv': _L3_gnn_in['bv'], 'L3_gnn_wo': _L3_gnn_in['wo'], 'L3_gnn_bo': _L3_gnn_in['bo'], 'L3_gnn_s2_w': _L3_gnn_in['s2_w'], 'L3_gnn_s2_b': _L3_gnn_in['s2_b'], 'L3_gnn_b2_w': _L3_gnn_in['b2_w'], 'L3_gnn_b2_b': _L3_gnn_in['b2_b'], 'L3_gnn_m_w1': _L3_gnn_in['m_w1'], 'L3_gnn_m_b1': _L3_gnn_in['m_b1'], 'L3_gnn_m_w2': _L3_gnn_in['m_w2'], 'L3_gnn_m_b2': _L3_gnn_in['m_b2']}

def reference(x, src, dst, node_vec1, L0_gnn_norm1_g, L0_gnn_norm1_b, L0_gnn_norm2_g, L0_gnn_norm2_b, L0_gnn_W_conv, L0_gnn_b_conv, L0_gnn_Wq, L0_gnn_Wk, L0_gnn_Wv, L0_gnn_Wo, L0_gnn_proj, L1_gnn_Ws, L1_gnn_Wb, L1_gnn_a_w, L1_gnn_a_b, L2_gnn_W, L2_gnn_b, L2_gnn_gamma, L2_gnn_beta, L3_gnn_f_w1, L3_gnn_f_b1, L3_gnn_f_w2, L3_gnn_f_b2, L3_gnn_s1_w, L3_gnn_s1_b, L3_gnn_b1_w, L3_gnn_b1_b, L3_gnn_wq, L3_gnn_bq, L3_gnn_wk, L3_gnn_bk, L3_gnn_wv, L3_gnn_bv, L3_gnn_wo, L3_gnn_bo, L3_gnn_s2_w, L3_gnn_s2_b, L3_gnn_b2_w, L3_gnn_b2_b, L3_gnn_m_w1, L3_gnn_m_b1, L3_gnn_m_w2, L3_gnn_m_b2):
    import jax
    import jax.numpy as jnp

    def _L0_gnn_ref(x, batch, edge_index, norm1_g, norm1_b, norm2_g, norm2_b, W_conv, b_conv, Wq, Wk, Wv, Wo, proj):
        import jax, jax.numpy as jnp
        import numpy as np
        B = 32
        MAXN = 256
        HEADS = 8
        DH = 64
        M = 256
        D = 512
        EPS = 1e-05
        KEPS = 1e-06

        def _batchnorm(x, g, b):
            mu = jnp.mean(x, axis=0)
            var = jnp.mean((x - mu) ** 2, axis=0)
            return (x - mu) * jax.lax.rsqrt(var + EPS) * g + b

        def _forward(x, batch, edge_index, norm1_g, norm1_b, norm2_g, norm2_b, W_conv, b_conv, Wq, Wk, Wv, Wo, proj):
            N = x.shape[0]
            E = edge_index.shape[1]
            h = x
            xn = _batchnorm(x, norm1_g, norm1_b)
            msg = xn[edge_index[0]]
            agg = jax.ops.segment_sum(msg, edge_index[1], num_segments=N)
            deg = jax.ops.segment_sum(jnp.ones((E,), x.dtype), edge_index[1], num_segments=N)
            agg = agg / jnp.maximum(deg, 1.0)[:, None]
            conv_out = jax.nn.relu(agg @ W_conv + b_conv)
            counts = jax.ops.segment_sum(jnp.ones((N,), jnp.int32), batch, num_segments=B)
            offsets = jnp.concatenate([jnp.zeros((1,), jnp.int32), jnp.cumsum(counts)[:-1]])
            pos = jnp.arange(N, dtype=jnp.int32) - offsets[batch]
            h_dense = jnp.zeros((B, MAXN, D), x.dtype).at[batch, pos].set(h)
            mask = jnp.zeros((B, MAXN), bool).at[batch, pos].set(True)

            def heads(t, W):
                return (t @ W).reshape(B, MAXN, HEADS, DH).transpose(0, 2, 1, 3)
            q, k, v = (heads(h_dense, Wq), heads(h_dense, Wk), heads(h_dense, Wv))
            scale = DH ** (-0.25)

            def phi(t, is_query):
                t = t * scale
                u = jnp.einsum('bhnd,md->bhnm', t, proj)
                diag = 0.5 * jnp.sum(t * t, axis=-1, keepdims=True)
                if is_query:
                    m_ = jnp.max(u, axis=-1, keepdims=True)
                else:
                    m_ = jnp.max(u, axis=(-2, -1), keepdims=True)
                return jnp.exp(u - diag - jax.lax.stop_gradient(m_)) / np.sqrt(M) + KEPS
            qf = phi(q, True)
            kf = phi(k, False) * mask[:, None, :, None]
            vm = v * mask[:, None, :, None]
            kv = jnp.einsum('bhnm,bhnd->bhmd', kf, vm)
            z = 1.0 / (jnp.einsum('bhnm,bhm->bhn', qf, kf.sum(axis=2)) + KEPS)
            attn = jnp.einsum('bhnm,bhmd->bhnd', qf, kv) * z[..., None]
            attn = attn.transpose(0, 2, 1, 3).reshape(B, MAXN, D) @ Wo
            h_attn = attn[batch, pos]
            return _batchnorm(conv_out + h_attn + h, norm2_g, norm2_b)
        return _forward(x, batch, edge_index, norm1_g, norm1_b, norm2_g, norm2_b, W_conv, b_conv, Wq, Wk, Wv, Wo, proj)

    def _L1_gnn_ref(x, edge_index, Ws, Wb, a_w, a_b):
        import jax, jax.numpy as jnp
        import numpy as np
        N, E, H, D_IN, D_PRIME = (6250, 100000, 8, 512, 64)

        def _segment_softmax(scores, seg, num_segments):
            smax = jax.ops.segment_max(scores, seg, num_segments=num_segments)
            ex = jnp.exp(scores - smax[seg])
            denom = jax.ops.segment_sum(ex, seg, num_segments=num_segments)
            return ex / denom[seg]
        v_src, v_tgt = (edge_index[0], edge_index[1])
        n = x.shape[0]
        outs = []
        for h in range(Ws.shape[0]):
            Wx = x @ Ws[h] + Wb[h]
            d = Wx.shape[-1]
            s = Wx[v_tgt] @ a_w[h, :d] + Wx[v_src] @ a_w[h, d:] + a_b[h]
            s = jax.nn.leaky_relu(s, negative_slope=0.2)
            alpha = _segment_softmax(s, v_tgt, n)
            outs.append(jax.ops.segment_sum(alpha[:, None] * Wx[v_src], v_tgt, num_segments=n))
        return jnp.stack(outs, axis=1).reshape(n, -1)

    def _L2_gnn_ref(x, edge_index, W, b, gamma, beta):
        import jax, jax.numpy as jnp
        import numpy as np
        N = 6250
        E = 100000
        D = 512

        def _gcn_conv(x, edge_index, W, b):
            n = x.shape[0]
            xw = x @ W.T
            loop = jnp.arange(n, dtype=edge_index.dtype)
            row = jnp.concatenate([edge_index[0], loop])
            col = jnp.concatenate([edge_index[1], loop])
            deg = jax.ops.segment_sum(jnp.ones_like(row, dtype=xw.dtype), col, num_segments=n)
            dinv = jnp.where(deg > 0, jax.lax.rsqrt(deg), 0.0)
            norm = dinv[row] * dinv[col]
            msgs = norm[:, None] * xw[row]
            out = jax.ops.segment_sum(msgs, col, num_segments=n)
            return out + b

        def _batch_norm(h, gamma, beta, eps=1e-05):
            mean = jnp.mean(h, axis=0)
            var = jnp.var(h, axis=0)
            return (h - mean) * jax.lax.rsqrt(var + eps) * gamma + beta
        identity = x
        h = _gcn_conv(x, edge_index, W, b)
        h = _batch_norm(h, gamma, beta)
        h = jax.nn.gelu(h, approximate=False)
        return h + identity

    def _L3_gnn_ref(latent_mesh_nodes, edge_index, noise_levels, f_w1, f_b1, f_w2, f_b2, s1_w, s1_b, b1_w, b1_b, wq, bq, wk, bk, wv, bv, wo, bo, s2_w, s2_b, b2_w, b2_b, m_w1, m_b1, m_w2, m_b2):
        import jax, jax.numpy as jnp
        import numpy as np
        N_NODES = 40962
        LATENT_DIM = 512
        N_EDGES = 81924
        NUM_BLOCKS = 4
        NUM_HEADS = 4
        NUM_FREQ = 32
        BASE_PERIOD = 16
        NOISE_EMB_DIM = 16
        EPS = 1e-05

        def _cond_layer_norm(x, cond, sw, sb, bw, bb):
            mu = jnp.mean(x, axis=-1, keepdims=True)
            var = jnp.var(x, axis=-1, keepdims=True)
            xn = (x - mu) * jax.lax.rsqrt(var + EPS)
            scale = cond @ sw + sb
            bias = cond @ bw + bb
            return xn * (1.0 + scale) + bias

        def _sparse_attention(x, src, dst, wq, bq, wk, bk, wv, bv, wo, bo):
            N, D = x.shape
            H, Dh = (NUM_HEADS, D // NUM_HEADS)
            q = (x @ wq + bq).reshape(N, H, Dh) * Dh ** (-0.5)
            k = (x @ wk + bk).reshape(N, H, Dh)
            v = (x @ wv + bv).reshape(N, H, Dh)
            scores = jnp.einsum('ehd,ehd->eh', q[src], k[dst])
            smax = jax.ops.segment_max(scores, src, num_segments=N)
            ex = jnp.exp(scores - smax[src])
            denom = jax.ops.segment_sum(ex, src, num_segments=N)
            attn = ex / denom[src]
            out = jax.ops.segment_sum(attn[:, :, None] * v[dst], src, num_segments=N)
            return out.reshape(N, D) @ wo + bo

        def _forward(x, edge_index, noise_levels, f_w1, f_b1, f_w2, f_b2, s1_w, s1_b, b1_w, b1_b, wq, bq, wk, bk, wv, bv, wo, bo, s2_w, s2_b, b2_w, b2_b, m_w1, m_b1, m_w2, m_b2):
            src, dst = (edge_index[0], edge_index[1])
            freqs = jnp.arange(1, NUM_FREQ + 1, dtype=x.dtype) * (2.0 * np.pi / BASE_PERIOD)
            ph = noise_levels * freqs
            emb = jnp.concatenate([jnp.sin(ph), jnp.cos(ph)], axis=-1)
            cond = jax.nn.silu(emb @ f_w1 + f_b1) @ f_w2 + f_b2
            for i in range(NUM_BLOCKS):
                y = _cond_layer_norm(x, cond, s1_w[i], s1_b[i], b1_w[i], b1_b[i])
                y = _sparse_attention(y, src, dst, wq[i], bq[i], wk[i], bk[i], wv[i], bv[i], wo[i], bo[i])
                x = x + y
                y = _cond_layer_norm(x, cond, s2_w[i], s2_b[i], b2_w[i], b2_b[i])
                y = jax.nn.relu(y @ m_w1[i] + m_b1[i]) @ m_w2[i] + m_b2[i]
                x = x + y
            return x
        return _forward(latent_mesh_nodes, edge_index, noise_levels, f_w1, f_b1, f_w2, f_b2, s1_w, s1_b, b1_w, b1_b, wq, bq, wk, bk, wv, bv, wo, bo, s2_w, s2_b, b2_w, b2_b, m_w1, m_b1, m_w2, m_b2)
    edge_index = jnp.stack([src, dst])
    batch0 = jnp.zeros((1250,), jnp.int32)
    x = _layernorm(x + _L0_gnn_ref(x, batch0, edge_index, L0_gnn_norm1_g, L0_gnn_norm1_b, L0_gnn_norm2_g, L0_gnn_norm2_b, L0_gnn_W_conv, L0_gnn_b_conv, L0_gnn_Wq, L0_gnn_Wk, L0_gnn_Wv, L0_gnn_Wo, L0_gnn_proj), axis=-1)
    x = _layernorm(x + _L1_gnn_ref(x, edge_index, L1_gnn_Ws, L1_gnn_Wb, L1_gnn_a_w, L1_gnn_a_b), axis=-1)
    x = _layernorm(x + _L2_gnn_ref(x, edge_index, L2_gnn_W, L2_gnn_b, L2_gnn_gamma, L2_gnn_beta), axis=-1)
    x = _layernorm(x + _L3_gnn_ref(x, edge_index, node_vec1, L3_gnn_f_w1, L3_gnn_f_b1, L3_gnn_f_w2, L3_gnn_f_b2, L3_gnn_s1_w, L3_gnn_s1_b, L3_gnn_b1_w, L3_gnn_b1_b, L3_gnn_wq, L3_gnn_bq, L3_gnn_wk, L3_gnn_bk, L3_gnn_wv, L3_gnn_bv, L3_gnn_wo, L3_gnn_bo, L3_gnn_s2_w, L3_gnn_s2_b, L3_gnn_b2_w, L3_gnn_b2_b, L3_gnn_m_w1, L3_gnn_m_b1, L3_gnn_m_w2, L3_gnn_m_b2), axis=-1)
    return x

_drawn_inputs = setup_inputs


def setup_inputs(seed=0):
    import zlib

    import numpy as np

    out = dict(_drawn_inputs(seed))
    spreads = {'L0_gnn_norm1_g': (1.0, 0.6),
     'L0_gnn_norm1_b': (0.0, 0.372),
     'L0_gnn_norm2_g': (1.0, 0.2),
     'L0_gnn_norm2_b': (0.0, 0.1),
     'L0_gnn_b_conv': (0.0, 0.39),
     'L2_gnn_b': (0.0, 0.8),
     'L2_gnn_gamma': (1.0, 0.2),
     'L2_gnn_beta': (0.0, 0.1),
     'L3_gnn_f_b1': (0.0, 0.8),
     'L3_gnn_f_b2': (0.0, 0.8),
     'L3_gnn_s1_b': (0.0, 0.8),
     'L3_gnn_b1_b': (0.0, 0.385),
     'L3_gnn_bq': (0.0, 0.8),
     'L3_gnn_bk': (0.0, 0.8),
     'L3_gnn_bv': (0.0, 0.1),
     'L3_gnn_bo': (0.0, 0.1),
     'L3_gnn_s2_b': (0.0, 0.578),
     'L3_gnn_b2_b': (0.0, 0.552),
     'L3_gnn_m_b1': (0.0, 0.1),
     'L3_gnn_m_b2': (0.0, 0.1)}
    factors = {'node_vec1': 8.0,
     'L0_gnn_Wq': 4.881,
     'L0_gnn_Wk': 5.21,
     'L0_gnn_Wv': 5.824,
     'L0_gnn_Wo': 5.777,
     'L0_gnn_proj': 5.021,
     'L1_gnn_a_b': 8.0,
     'L3_gnn_f_w1': 8.0,
     'L3_gnn_f_w2': 8.0,
     'L3_gnn_s1_w': 8.0,
     'L3_gnn_b1_w': 8.0,
     'L3_gnn_wq': 5.56,
     'L3_gnn_wk': 5.434,
     'L3_gnn_s2_w': 8.0,
     'L3_gnn_b2_w': 8.0}
    for name, (base, spread) in spreads.items():
        noise = np.random.default_rng([zlib.crc32(name.encode()), seed]).standard_normal(out[name].shape)
        drawn = base * np.exp(spread * noise) if base else spread * noise
        out[name] = jnp.asarray(drawn.astype(out[name].dtype))
    for name, factor in factors.items():
        out[name] = (out[name] * factor).astype(out[name].dtype)
    return out
```

```python
import math
from contextlib import ExitStack

import concourse.bass as bass
from concourse import mybir

ALU = mybir.AluOpType
ACT = mybir.ActivationFunctionType
AX = mybir.AxisListType
F32 = mybir.dt.float32
F32R = mybir.dt.float32r
BF16 = mybir.dt.bfloat16
F16 = mybir.dt.float16
I32 = mybir.dt.int32

BANK = 512
PE_ROWS = 128
EPS = 1e-5
KEPS = 1e-6
MASKED = -1e30


class Tick:
    def __init__(self, sem, value):
        self.sem, self.value = sem, value


class Queue:
    def __init__(self, sem):
        self.sem, self.count, self.steps, self.waited = sem, 0, [], {}

    def wait(self, after):
        for tick in after:
            if tick is not None and self.waited.get(id(tick.sem), 0) < tick.value:
                self.waited[id(tick.sem)] = tick.value
                self.steps.append(lambda e, t=tick: e.wait_ge(t.sem, t.value))

    def do(self, make, after=(), quiet=False):
        self.wait(after)
        if quiet:
            self.steps.append(make)
            return None
        self.count += 1
        self.steps.append(lambda e: make(e).then_inc(self.sem, 1))
        return Tick(self.sem, self.count)

    def last(self):
        return Tick(self.sem, self.count) if self.count else None

    def run(self, engine):
        for step in self.steps:
            step(engine)


class DmaSlot:
    def __init__(self, sem):
        self.sem, self.count = sem, 0

    def move(self, queue, out, in_, after=()):
        queue.wait(after)
        self.count += 16
        queue.steps.append(lambda e: e.dma_start(out, in_).then_inc(self.sem, 16))
        return Tick(self.sem, self.count)


def build_layers(nc, x, src, dst, noise, L0, L1, L2, L3, out, stop_after=None):
    N, D = x.shape
    E = src.shape[0]
    NP = 125
    NT = N // NP
    KD = D // PE_ROWS
    assert NP * NT == N and E % NP == 0 and KD * PE_ROWS == D
    NCHUNK = E // NP
    with ExitStack() as ctx:
        sem = lambda name: ctx.enter_context(nc.semaphore(name))
        pe, dve, act, pool, sp = (Queue(sem(n)) for n in ("pe_done", "dve_done", "act_done", "pool_done", "sp_done"))
        slots = {}

        def dma(name, queue, out_, in_, after=()):
            if name not in slots:
                slots[name] = DmaSlot(sem("dma_" + name))
            return slots[name].move(queue, out_, in_, after)

        ARENA = 212600
        ctx.enter_context(nc.sbuf_tensor("arena", [128, ARENA], mybir.dt.uint8))
        base = nc.sbuf_base - ARENA
        size = {F32: 4, F32R: 4, BF16: 2, F16: 2, I32: 4}

        class Region:
            def __init__(self, at, end):
                self.at, self.end = at, end

            def take(self, name, shape, dtype=F32):
                n = size[dtype]
                for s in shape[1:]:
                    n *= s
                t = nc.alloc_sbuf_tensor_at(name, shape, dtype, offset=base + self.at)
                self.at += (n + 31) // 32 * 32
                assert self.at <= self.end, (name, self.at, self.end)
                return t

        keep = Region(0, 76000)
        counts = keep.take("counts", [NP, NT, N])
        X = keep.take("X", [NP, NT, D])
        ident = keep.take("ident", [128, 128])
        ones = keep.take("ones", [128, 128])
        minus_half = keep.take("minus_half", [128, NT])
        deg = keep.take("deg", [NP, NT])
        stats = keep.take("stats", [NP, NT, 6])
        mean_var = keep.take("mean_var", [NP, NT, 2])
        rstd = keep.take("rstd", [NP, NT])
        WORK = keep.at
        psum = ctx.enter_context(nc.psum_tensor("psum", [128, 8 * BANK], F32))
        bank_free = [None] * 8

        def bank(b, n=BANK, rows=128):
            return psum[0:rows, b * BANK:b * BANK + n]

        def everything():
            return [q.last() for q in (pe, dve, act, pool)] + [Tick(s.sem, s.count) for s in slots.values()]

        def fence():
            done = everything()
            for q in (pe, dve, act, pool, sp):
                q.wait(done)

        def row_on_partitions(ap, n=NP):
            return ap.partition_broadcast(n)

        def transpose_nodes(source, store, ready, banks=(6, 7), width=NP):
            done = []
            for j in range(NT):
                b = banks[j % len(banks)]
                view = bank(b).rearrange("p (k c) -> p k c", k=KD)
                for k in range(KD):
                    t = pe.do(lambda e, j=j, k=k, v=view: e.transpose(
                        v[:, k, 0:width], source[0:width, j, k * 128:(k + 1) * 128], ident[0:width, 0:width]),
                        after=[ready[j], bank_free[b]], quiet=k < KD - 1)
                ticks = store(j, view[:, :, 0:width], t)
                bank_free[b] = ticks[-1]
                done.append(ticks[-1])
            return done

        def copy_out(i, out_, in_, after):
            if i % 2:
                return dve.do(lambda e: e.tensor_copy(out_, in_), after)
            return act.do(lambda e: e.copy(out_, in_), after)

        def layer_norm(ready):
            done = []
            for j in range(NT):
                t = dve.do(lambda e, j=j: e.bn_stats(stats[:, j, :], X[:, j, :]), [ready[j]])
            for j in range(NT):
                t = dve.do(lambda e, j=j: e.bn_aggr(mean_var[:, j, :], stats[:, j, :]), [dve.last()] if j == 0 else [])
            t = dve.do(lambda e: e.tensor_scalar(rstd[:], mean_var[:, :, 1], EPS, None, ALU.add), [t])
            t = pool.do(lambda e: e.tensor_tensor(rstd[:], rstd[:], minus_half[0:NP, :], ALU.pow), [t])
            for j in range(NT):
                done.append(dve.do(lambda e, j=j: e.tensor_scalar(
                    X[:, j, :], X[:, j, :], mean_var[:, j, 0:1], rstd[:, j:j + 1], ALU.subtract, ALU.mult), [t]))
            return done

        def batch_norm(source, target, gain_row, bias_row, region, tag, ready):
            gain = region.take(tag + "_gain", [NP, D])
            bias = region.take(tag + "_bias", [NP, D])
            mean = region.take(tag + "_mean", [NP, D])
            squares = [region.take(f"{tag}_square{i}", [NP, D]) for i in range(2)]
            root = region.take(tag + "_root", [NP, D])
            fix = region.take(tag + "_fix", [NP, D])
            t_gain = dma("gain", sp, gain[:], row_on_partitions(gain_row))
            t_bias = dma("bias", sp, bias[:], row_on_partitions(bias_row))
            for j in range(NT):
                t = pe.do(lambda e, j=j: e.matmul(bank(0, D, NP), ones[0:NP, 0:NP], source[:, j, :],
                                                  start=j == 0, stop=j == NT - 1), [ready[j], bank_free[0]])
            t_mean = act.do(lambda e: e.mul(mean[:], bank(0, D, NP), 1.0 / N), [t])
            squared = [None, None]
            for j in range(NT):
                centred = dve.do(lambda e, j=j: e.tensor_tensor(target[:, j, :], source[:, j, :], mean[:], ALU.subtract), [t_mean])
                sq = squares[j % 2]
                t = act.do(lambda e, j=j, sq=sq: e.square(sq[:], target[:, j, :]), [centred, squared[j % 2]])
                t = squared[j % 2] = pe.do(lambda e, j=j, sq=sq: e.matmul(
                    bank(1, D, NP), ones[0:NP, 0:NP], sq[:], start=j == 0, stop=j == NT - 1), [t, bank_free[1]])
            t = dve.do(lambda e: e.tensor_scalar(mean[:], bank(1, D, NP), 1.0 / N, EPS, ALU.mult, ALU.add), [t])
            bank_free[0] = t_mean
            bank_free[1] = t
            t = act.do(lambda e: e.sqrt(root[:], mean[:]), [t])
            t = dve.do(lambda e: e.reciprocal(root[:], root[:]), [t])
            t = dve.do(lambda e: e.tensor_tensor(fix[:], root[:], root[:], ALU.mult), [t])
            t = dve.do(lambda e: e.tensor_tensor(fix[:], fix[:], mean[:], ALU.mult), [t])
            t = dve.do(lambda e: e.tensor_scalar(fix[:], fix[:], -0.5, 1.5, ALU.mult, ALU.add), [t])
            t = dve.do(lambda e: e.tensor_tensor(root[:], root[:], fix[:], ALU.mult), [t])
            t = dve.do(lambda e: e.tensor_tensor(mean[:], root[:], gain[:], ALU.mult), [t, t_gain])
            t = [dve.do(lambda e, j=j: e.tensor_tensor(target[:, j, :], target[:, j, :], mean[:], ALU.mult), [t])
                 for j in range(NT)]
            return [dve.do(lambda e, j=j: e.tensor_tensor(target[:, j, :], target[:, j, :], bias[:], ALU.add), [t[j], t_bias])
                    for j in range(NT)]

        def gather_sum(source, ready, finish):
            done = []
            for j in range(NT):
                b = j % 4
                for s in range(NT):
                    t = pe.do(lambda e, j=j, s=s, b=b: e.matmul(
                        bank(b, D, NP), counts[:, s, j * NP:(j + 1) * NP], source[:, s, :], start=s == 0, stop=s == NT - 1),
                        [ready[s], bank_free[b]], quiet=s < NT - 1)
                bank_free[b] = finish(j, bank(b, D, NP), t)
                done.append(bank_free[b])
            return done

        def dense(xT, weight, bias_row, ready, finish, tiles=None, banks=(4, 5, 6, 7)):
            done = []
            for j in (range(NT) if tiles is None else tiles):
                b = banks[j % len(banks)]
                for k in range(KD):
                    t = pe.do(lambda e, j=j, k=k, b=b: e.matmul(
                        bank(b, D, NP), xT[:, k, j * NP:(j + 1) * NP], weight[:, k, :], start=k == 0,
                        stop=bias_row is None and k == KD - 1), [ready[j], bank_free[b]],
                        quiet=bias_row is not None or k < KD - 1)
                if bias_row is not None:
                    t = pe.do(lambda e, b=b: e.matmul(bank(b, D, NP), ones[0:1, 0:NP], bias_row, start=False, stop=True))
                bank_free[b] = finish(j, bank(b, D, NP), t)
                done.append(bank_free[b])
            return done

        t = dve.do(lambda e: e.memset(ones[:], 1.0))
        t_mh = dve.do(lambda e: e.memset(minus_half[:], -0.5))
        t = pool.do(lambda e: e.memset(ident[:], 0.0))
        t_ident = pool.do(lambda e: e.affine_select(out=ident[:], in_=ident[:], compare_op=ALU.not_equal, fill=1.0,
                                                    base=0, pattern=[[-1, 128]], channel_multiplier=1), [t])
        t_x = dma("x", sp, X[:], x.rearrange("(j p) d -> p j d", p=NP))

        wr = Region(WORK, ARENA)
        no_edge = wr.take("no_edge", [NP, NT, N], BF16)
        AT0 = wr.at
        HC = NCHUNK // 2
        edges_i = wr.take("edges_i", [HC, 2, 2, NP], I32)
        edges_f = wr.take("edges_f", [HC, 2, 2, NP])
        edge_col = wr.take("edge_col", [NP, 2, 2, HC])
        iota_i = wr.take("iota_i", [NP, N], I32)
        iota_h = wr.take("iota_h", [NP, N], F16)
        RING = 8
        src_hot = [wr.take(f"src_hot{i}", [NP, N], BF16) for i in range(RING)]
        dst_hot = [wr.take(f"dst_hot{i}", [NP, 2 * NP], BF16) for i in range(RING)]
        count_rows = [wr.take(f"count_rows{i}", [NP, N]) for i in range(2)]
        for half in range(2):
            for w, a in enumerate((src, dst)):
                t_e = dma("edges", sp, edges_i[:, half, w, :], a.rearrange("(h c p) -> h c p", h=2, p=NP)[half])
        t = pool.do(lambda e: e.iota(iota_i[:], pattern=[[1, N]], base=0, channel_multiplier=0))
        t_iota = pool.do(lambda e: e.tensor_copy(iota_h[:], iota_i[:]), [t])
        t = dve.do(lambda e: e.tensor_copy(edges_f[:], edges_i[:]), [t_e])
        for half in range(2):
            for w in range(2):
                tt = pe.do(lambda e, half=half, w=w: e.transpose(
                    psum[0:NP, (2 * w + half) * HC:(2 * w + half + 1) * HC], edges_f[:, half, w, :], ident[0:HC, 0:HC]), [t, t_ident])
        t_col = dve.do(lambda e: e.tensor_copy(edge_col[:].rearrange("p w h c -> p (w h c)"), psum[0:NP, 0:4 * HC]), [tt])
        bank_free[0] = t_col

        def build_counts():
            n = 0
            used = [None] * RING
            rows_free = [None, None]
            for r in range(NT // 2):
                for c in range(NCHUNK):
                    slot = n % RING
                    t1 = dve.do(lambda e, c=c, s=slot: e.tensor_scalar(
                        src_hot[s][:], iota_h[:], edge_col[:, 0, c // HC, c % HC:c % HC + 1], None, ALU.is_equal),
                        [t_col, t_iota, used[slot]])
                    t1 = dve.do(lambda e, c=c, s=slot, r=r: e.tensor_scalar(
                        dst_hot[s][:], iota_h[:, r * 2 * NP:(r + 1) * 2 * NP], edge_col[:, 1, c // HC, c % HC:c % HC + 1], None, ALU.is_equal))
                    for i in range(2):
                        for q in range(3):
                            w = min(BANK, N - q * BANK)
                            t2 = pe.do(lambda e, s=slot, i=i, q=q, w=w, c=c: e.matmul(
                                psum[0:NP, (3 * i + q) * BANK:(3 * i + q) * BANK + w], dst_hot[s][:, i * NP:(i + 1) * NP],
                                src_hot[s][:, q * BANK:q * BANK + w], start=c == 0, stop=c == NCHUNK - 1),
                                [t1] + [bank_free[b] for b in range(6)], quiet=not (i == 1 and q == 2))
                    used[slot] = t2
                    n += 1
                for i in range(2):
                    j = 2 * r + i
                    rows, ps = count_rows[i], psum[0:NP, 3 * i * BANK:3 * i * BANK + N]
                    t3 = act.do(lambda e, j=j, rows=rows, ps=ps: e.activation(rows[:], ps, ACT.Identity, accum_out=deg[:, j:j + 1]), [t2, rows_free[i]])
                    t4 = dve.do(lambda e, j=j, rows=rows: e.tensor_scalar(no_edge[:, j, :], rows[:], 0.0, MASKED, ALU.is_equal, ALU.mult), [t3])
                    for b in range(3 * i, 3 * i + 3):
                        bank_free[b] = t3
                    for s0 in range(0, NT, 4):
                        b = 6 + (s0 // 4) % 2
                        m = min(4, NT - s0)
                        view = bank(b, m * 128, NP).rearrange("p (k c) -> p k c", c=128)[:, :, 0:NP]
                        for k in range(m):
                            t5 = pe.do(lambda e, k=k, s0=s0, view=view, rows=rows: e.transpose(
                                view[:, k, :], rows[:, (s0 + k) * NP:(s0 + k + 1) * NP], ident[0:NP, 0:NP]), [t3, bank_free[b]])
                        bank_free[b] = act.do(lambda e, j=j, s0=s0, m=m, view=view: e.copy(
                            counts[:, s0:s0 + m, j * NP:(j + 1) * NP], view), [t5])
                    rows_free[i] = t5
                    act.wait([t4])

        build_counts()
        fence()
        if stop_after == "counts":
            t = dve.do(lambda e: e.tensor_copy(X[:], counts[:, :, 0:D]), [t_x])
            return finish_program(nc, ctx, out, X, dma, (pe, dve, act, pool, sp), [t], NP)

        wr = Region(AT0, ARENA)
        H = wr.take("H", [NP, NT, D])
        WA = wr.take("WA", [128, KD, D])
        WB = wr.take("WB", [128, KD, D])
        STAGE0 = wr.at

        def attention_layer0():
            g = Region(STAGE0, ARENA)
            M = L0["proj"].shape[0]
            DH = L0["proj"].shape[1]
            HEADS = D // DH
            RT = 2
            ROWS = RT * 128
            h_in = g.take("h_in", [128, RT, D])
            hT = g.take("hT", [128, KD, ROWS])
            nat = {c: g.take(c + "_nat", [128, RT, D]) for c in "qkv"}
            tT = {c: g.take(c + "_T", [128, KD, ROWS]) for c in "qk"}
            squares = g.take("squares", [128, RT, D])
            half_norm = {c: g.take(c + "_halfnorm", [128, RT, HEADS]) for c in "qk"}
            proj_in = g.take("proj_in", [128, M // 128, DH])
            projT = g.take("projT", [128, M])
            umax = {c: g.take(c + "_umax", [128, RT, HEADS]) for c in "qk"}
            shift = {c: g.take(c + "_shift", [128, RT, HEADS]) for c in "qk"}
            row_max = g.take("row_max", [HEADS, 1])
            both = g.take("both_max", [128, HEADS])
            diag = g.take("diag", [HEADS, HEADS])
            feat = {c: [g.take(f"{c}_feat{i}", [128, RT, M]) for i in range(2)] for c in "qk"}
            qfT = [g.take(f"qfT{i}", [128, M // 128, ROWS]) for i in range(2)]
            v1 = g.take("v_and_one", [128, RT, HEADS, DH + 1])
            kv = [g.take(f"kv{i}", [128, M // 128, DH + 1]) for i in range(2)]
            z = g.take("z", [128, RT])
            o_nat = g.take("o_nat", [128, RT, D])
            TILES = 4
            oT = g.take("oT", [128, KD, TILES * NP])
            t_h = dma("h_in", sp, h_in[:], x[0:ROWS].rearrange("(r p) d -> p r d", p=128))
            t_pj = dma("proj", sp, proj_in[:], L0["proj"].rearrange("(r p) d -> p r d", p=128))
            for r in range(RT):
                b = r
                for k in range(KD):
                    t = pe.do(lambda e, r=r, k=k, b=b: e.transpose(bank(b)[:, k * 128:(k + 1) * 128],
                                                               h_in[:, r, k * 128:(k + 1) * 128], ident[:]), [t_h, bank_free[b]])
                th = act.do(lambda e, r=r, b=b: e.copy(hT[:, :, r * 128:(r + 1) * 128], bank(b).rearrange("p (k c) -> p k c", k=KD)), [t])
                bank_free[b] = th
            for m in range(M // 128):
                t = pe.do(lambda e, m=m: e.transpose(psum[0:DH, 2 * BANK + m * 128:2 * BANK + (m + 1) * 128], proj_in[:, m, :], ident[:]), [t_pj, bank_free[2]])
            act.do(lambda e: e.copy(projT[0:DH, :], psum[0:DH, 2 * BANK:2 * BANK + M]), [t])
            t_proj = bank_free[2] = act.do(lambda e: e.copy(projT[DH:2 * DH, :], psum[0:DH, 2 * BANK:2 * BANK + M]), [t])
            scale = DH ** -0.25
            free_w = [None, None]
            ready = {}
            for i, (c, name) in enumerate((("q", "Wq"), ("k", "Wk"), ("v", "Wv"))):
                W = (WA, WB)[i % 2]
                tw = dma(("wa", "wb")[i % 2], sp, W[:], L0[name].rearrange("(k p) n -> p k n", p=128), [free_w[i % 2]])
                for r in range(RT):
                    b = 4 + r
                    for k in range(KD):
                        t = pe.do(lambda e, r=r, k=k, b=b, W=W: e.matmul(bank(b), hT[:, k, r * 128:(r + 1) * 128], W[:, k, :],
                                                                     start=k == 0, stop=k == KD - 1), [th, tw, bank_free[b]])
                    s = scale if c != "v" else 1.0
                    ready[c] = bank_free[b] = act.do(lambda e, r=r, b=b, c=c, s=s: e.mul(nat[c][:, r, :], bank(b), s), [t])
                free_w[i % 2] = t
            for c in "qk":
                t = dve.do(lambda e, c=c: e.tensor_tensor(squares[:], nat[c][:], nat[c][:], ALU.mult), [ready[c], dve.last()])
                t = dve.do(lambda e, c=c: e.tensor_reduce(half_norm[c][:], squares[:].rearrange("p r (h d) -> p r h d", h=HEADS), AX.X, ALU.add), [t])
                for r in range(RT):
                    b = r
                    for k in range(KD):
                        t = pe.do(lambda e, r=r, k=k, b=b, c=c: e.transpose(bank(b)[:, k * 128:(k + 1) * 128],
                                                                        nat[c][:, r, k * 128:(k + 1) * 128], ident[:]), [ready[c], bank_free[b]])
                    ready[c + "T"] = bank_free[b] = act.do(lambda e, r=r, b=b, c=c: e.copy(
                        tT[c][:, :, r * 128:(r + 1) * 128], bank(b).rearrange("p (k c) -> p k c", k=KD)), [t])
            dve.do(lambda e: e.memset(v1[:], 1.0))
            t_v1 = dve.do(lambda e: e.tensor_copy(v1[:, :, :, 0:DH], nat["v"][:].rearrange("p r (h d) -> p r h d", h=HEADS)), [ready["v"], dve.last()])

            def scores(c, h, b):
                k, p0 = h // 2, DH * (h % 2)
                for r in range(RT):
                    t = pe.do(lambda e, r=r: e.matmul(bank(b)[:, r * M:(r + 1) * M], tT[c][p0:p0 + DH, k, r * 128:(r + 1) * 128],
                                                      projT[p0:p0 + DH, :], start=r == 0, stop=r == RT - 1, skip_group_check=True),
                              [ready[c + "T"], t_proj, bank_free[b]])
                return t
            for h in range(HEADS):
                b = h % 2
                t = scores("k", h, b)
                t_um = bank_free[b] = dve.do(lambda e, h=h, b=b: e.tensor_reduce(
                    umax["k"][:, :, h], bank(b).rearrange("p (r m) -> p r m", r=RT), AX.X, ALU.max), [t])
            t = dve.do(lambda e: e.tensor_tensor(both[:], umax["k"][:, 0, :], umax["k"][:, 1, :], ALU.max), [t_um])
            t = pe.do(lambda e: e.transpose(psum[0:HEADS, 3 * BANK:3 * BANK + 128], both[:], ident[:]), [t, bank_free[3]])
            t = dve.do(lambda e: e.tensor_reduce(row_max[:], psum[0:HEADS, 3 * BANK:3 * BANK + 128], AX.X, ALU.max), [t])
            t = dve.do(lambda e: e.tensor_scalar(diag[:], ident[0:HEADS, 0:HEADS], row_max[:, 0:1], None, ALU.mult), [t])
            t = pe.do(lambda e: e.matmul(psum[:, 3 * BANK:3 * BANK + HEADS], ones[0:HEADS, :], diag[:], start=True, stop=True), [t])
            for r in range(RT):
                t_sk = dve.do(lambda e, r=r: e.scalar_tensor_tensor(shift["k"][:, r, :], half_norm["k"][:, r, :], -0.5,
                                                                psum[:, 3 * BANK:3 * BANK + HEADS], ALU.mult, ALU.subtract), [t])
            bank_free[3] = t_sk
            inv = 1.0 / math.sqrt(M)
            for h in range(HEADS):
                i = h % 2
                for c in "kq":
                    b = 0 if c == "k" else 1
                    t = scores(c, h, b)
                    ready_shift = t_sk
                    if c == "q":
                        t2 = dve.do(lambda e, h=h, b=b: e.tensor_reduce(
                            umax["q"][:, :, h], bank(b).rearrange("p (r m) -> p r m", r=RT), AX.X, ALU.max), [t])
                        ready_shift = dve.do(lambda e, h=h: e.scalar_tensor_tensor(
                            shift["q"][:, :, h], half_norm["q"][:, :, h], -0.5, umax["q"][:, :, h], ALU.mult, ALU.subtract), [t2])
                    for r in range(RT):
                        t3 = act.do(lambda e, h=h, r=r, b=b, c=c, i=i: e.activation(
                            feat[c][i][:, r, :], bank(b)[:, r * M:(r + 1) * M], ACT.Exp, bias=shift[c][:, r, h:h + 1]),
                            [t, ready_shift, pe.last() if r == 0 else None])
                    bank_free[b] = t3
                    t4 = dve.do(lambda e, c=c, i=i: e.tensor_scalar(feat[c][i][:], feat[c][i][:], inv, KEPS, ALU.mult, ALU.add), [t3])
                    if c == "k":
                        for m in range(M // 128):
                            for r in range(RT):
                                t5 = pe.do(lambda e, h=h, m=m, r=r, i=i: e.matmul(
                                    psum[:, (2 + m) * BANK:(2 + m) * BANK + DH + 1], feat["k"][i][:, r, m * 128:(m + 1) * 128], v1[:, r, h, :],
                                    start=r == 0, stop=r == RT - 1), [t4, t_v1, bank_free[2 + m]])
                            t_kv = bank_free[2 + m] = dve.do(lambda e, m=m, i=i: e.tensor_copy(
                                kv[i][:, m, :], psum[:, (2 + m) * BANK:(2 + m) * BANK + DH + 1]), [t5])
                    else:
                        for m in range(M // 128):
                            for r in range(RT):
                                t5 = pe.do(lambda e, m=m, r=r, i=i: e.transpose(
                                    psum[:, 4 * BANK + (m * RT + r) * 128:4 * BANK + (m * RT + r + 1) * 128], feat["q"][i][:, r, m * 128:(m + 1) * 128], ident[:]),
                                    [t4, bank_free[4]])
                        t_qf = bank_free[4] = act.do(lambda e, i=i: e.copy(qfT[i][:].rearrange("p m n -> p (m n)"), bank(4)), [t5])
                for r in range(RT):
                    b = 5 + r
                    for m in range(M // 128):
                        t6 = pe.do(lambda e, r=r, m=m, i=i, b=b: e.matmul(
                            psum[:, b * BANK:b * BANK + DH + 1], qfT[i][:, m, r * 128:(r + 1) * 128], kv[i][:, m, :], start=m == 0, stop=m == M // 128 - 1),
                            [t_qf, t_kv, bank_free[b]])
                    t7 = dve.do(lambda e, r=r, b=b: e.tensor_scalar(z[:, r:r + 1], psum[:, b * BANK + DH:b * BANK + DH + 1], KEPS, None, ALU.add), [t6])
                    t7 = dve.do(lambda e, r=r: e.reciprocal(z[:, r:r + 1], z[:, r:r + 1]), [t7])
                    t_o = bank_free[b] = dve.do(lambda e, r=r, b=b, h=h: e.tensor_scalar(
                        o_nat[:, r, h * DH:(h + 1) * DH], psum[:, b * BANK:b * BANK + DH], z[:, r:r + 1], None, ALU.mult), [t7])
            for r in range(RT):
                b = r
                for k in range(KD):
                    t = pe.do(lambda e, r=r, k=k, b=b: e.transpose(bank(b)[:, k * 128:(k + 1) * 128], o_nat[:, r, k * 128:(k + 1) * 128], ident[:]), [t_o, bank_free[b]])
                t_oT = bank_free[b] = act.do(lambda e, r=r, b=b: e.copy(oT[:, :, r * 128:(r + 1) * 128], bank(b).rearrange("p (k c) -> p k c", k=KD)), [t])
            t_oT = dve.do(lambda e: e.tensor_copy(oT[:, :, ROWS:], oT[:, :, ROWS - 1:ROWS].to_broadcast([128, KD, TILES * NP - ROWS])), [t_oT])
            tw = dma("wb", sp, WB[:], L0["Wo"].rearrange("(k p) n -> p k n", p=128), [free_w[1]])

            def finish(j, ps, t):
                for jj in ([j] if j < TILES - 1 else range(TILES - 1, NT)):
                    t2 = dve.do(lambda e, jj=jj: e.tensor_tensor(H[:, jj, :], ps, X[:, jj, :], ALU.add), [t, t_x])
                return t2
            pe.wait([tw])
            done = dense(oT, WB, None, [t_oT] * TILES, finish, tiles=range(TILES))
            return done[-1]

        t_attn = attention_layer0()
        fence()
        if stop_after == "attn0":
            t = dve.do(lambda e: e.tensor_copy(X[:], H[:]), [t_attn])
            return finish_program(nc, ctx, out, X, dma, (pe, dve, act, pool, sp), [t], NP)

        def layer0():
            g = Region(STAGE0, ARENA)
            A = g.take("A", [NP, NT, D])
            T = g.take("T", [128, KD, N])
            inv_deg = g.take("inv_deg", [NP, NT])
            b_conv = g.take("b_conv", [1, D])
            tw = dma("wa", sp, WA[:], L0["W_conv"].rearrange("(k p) n -> p k n", p=128))
            tb = dma("b_conv", sp, b_conv[:], L0["b_conv"].rearrange("(a n) -> a n", a=1))
            save = g.at
            xn_ready = batch_norm(X, A, L0["norm1_g"], L0["norm1_b"], g, "bn1", [None] * NT)
            t = dve.do(lambda e: e.tensor_scalar(inv_deg[:], deg[:], 1.0, None, ALU.max))
            t_inv = dve.do(lambda e: e.reciprocal(inv_deg[:], inv_deg[:]), [t])
            AGG = nc.alloc_sbuf_tensor_at("AGG", [NP, NT, D], F32, offset=base + save)
            act.wait([xn_ready[-1]])
            agg_ready = gather_sum(A, xn_ready, lambda j, ps, t: act.do(
                lambda e: e.activation(AGG[:, j, :], ps, ACT.Identity, scale=inv_deg[:, j:j + 1]), [t, t_inv]))
            t_T = transpose_nodes(AGG, lambda j, v, t: [copy_out(j, T[:, :, j * NP:(j + 1) * NP], v, [t])], agg_ready)
            pe.wait([tw, tb])

            def add_conv(j, ps, t):
                return dve.do(lambda e: e.scalar_tensor_tensor(H[:, j, :], ps, 0.0, H[:, j, :], ALU.max, ALU.add), [t])
            h_ready = dense(T, WA, b_conv[0:1, :], t_T, add_conv)
            fence()
            g = Region(STAGE0, ARENA)
            A = g.take("A2", [NP, NT, D])
            bn_ready = batch_norm(H, A, L0["norm2_g"], L0["norm2_b"], g, "bn2", h_ready)
            x_ready = [dve.do(lambda e, j=j: e.tensor_tensor(X[:, j, :], X[:, j, :], A[:, j, :], ALU.add), [bn_ready[j]]) for j in range(NT)]
            x_ready = layer_norm(x_ready)
            fence()
            return x_ready

        x_ready = layer0()
        if stop_after == "L0":
            return finish_program(nc, ctx, out, X, dma, (pe, dve, act, pool, sp), x_ready, NP)

        def layer1(x_ready):
            HEADS1, _, DH1 = L1["Ws"].shape
            g = Region(AT0, ARENA)
            H = nc.alloc_sbuf_tensor_at("H1", [NP, NT, D], F32, offset=base + g.at)
            g.at += 4 * NT * D
            WH = g.take("WH", [NP, NT, HEADS1, DH1 + 1])
            SHIFT0 = g.at
            T = g.take("T1", [128, KD, N])
            W1 = g.take("W1", [128, KD, D])
            Wb = g.take("Wb1", [1, D])
            aw = g.take("aw", [NP, HEADS1, 2 * DH1])
            ab = g.take("ab", [NP, HEADS1])
            prod = [g.take(f"prod{i}", [NP, HEADS1, DH1]) for i in range(2)]
            tgt = g.take("tgt_score", [NP, NT, HEADS1])
            srcs = g.take("src_score", [NP, NT, HEADS1])
            srcs02 = g.take("src_score02", [NP, NT, HEADS1])
            nb_max = g.take("nb_max", [NP, NT, HEADS1])
            leak = g.take("leak", [NP, NT, HEADS1])
            rowT = {n: g.take("rowT_" + n, [HEADS1, N]) for n in ("src", "pos", "neg")}
            pick = g.take("pick", [HEADS1, HEADS1, 128])
            trash = g.take("trash", [NP, N], BF16)
            t_w = []
            for k in range(KD):
                t_w = dma("wa", sp, W1[:, k, :].rearrange("p (h d) -> p h d", h=HEADS1), L1["Ws"][:, k * 128:(k + 1) * 128, :].rearrange("h p d -> p h d"))
            t_wb = dma("b_conv", sp, Wb[:], L1["Wb"].rearrange("(a h) d -> a (h d)", a=1))
            t_aw = dma("aw", sp, aw[:], row_on_partitions(L1["a_w"]))
            t_ab = dma("aw", sp, ab[:], row_on_partitions(L1["a_b"]))
            t_pick = pool.do(lambda e: e.tensor_copy(pick[:], ident[0:HEADS1, 0:HEADS1].unsqueeze(2).to_broadcast([HEADS1, HEADS1, 128])))
            t_T = transpose_nodes(X, lambda j, v, t: [copy_out(j, T[:, :, j * NP:(j + 1) * NP], v, [t])], x_ready)
            t_one = pool.do(lambda e: e.memset(WH[:, :, :, DH1:DH1 + 1], 1.0))
            pe.wait([t_w, t_wb])
            wh_ready = dense(T, W1, Wb[0:1, :], t_T, lambda j, ps, t: copy_out(
                j, WH[:, j, :, 0:DH1], ps.rearrange("p (h d) -> p h d", h=HEADS1), [t]))
            for j in range(NT):
                for i, target in ((0, tgt), (1, srcs)):
                    t = dve.do(lambda e, j=j, i=i: e.tensor_tensor(prod[i][:], WH[:, j, :, 0:DH1], aw[:, :, i * DH1:(i + 1) * DH1], ALU.mult),
                               [wh_ready[j], t_ab, t_one, dve.last()])
                    t = dve.do(lambda e, j=j, i=i, target=target: e.tensor_reduce(target[:, j, :], prod[i][:], AX.X, ALU.add), [t])
                t_tgt = dve.do(lambda e, j=j: e.tensor_tensor(tgt[:, j, :], tgt[:, j, :], ab[:], ALU.add), [dve.last()])
            t_src02 = pool.do(lambda e: e.tensor_scalar(srcs02[:], srcs[:], 0.2, None, ALU.mult), [t_tgt])

            def to_rows(source, row, ready):
                view = psum[0:HEADS1, 0:NT * 128].rearrange("p (j c) -> p j c", c=128)
                for j in range(NT):
                    t = pe.do(lambda e, j=j: e.transpose(view[:, j, 0:NP], source[:, j, :], ident[0:NP, 0:NP]),
                              [ready, bank_free[0], bank_free[1], bank_free[2]])
                t = act.do(lambda e: e.copy(row[:].rearrange("p (j c) -> p j c", c=NP), view[:, :, 0:NP]), [t])
                bank_free[0] = bank_free[1] = bank_free[2] = t
                return t

            def spread_row(row, h, b0, ready):
                for q in range(3):
                    w = min(BANK, N - q * BANK)
                    t = pe.do(lambda e, q=q, w=w: e.matmul(psum[0:NP, (b0 + q) * BANK:(b0 + q) * BANK + w], pick[:, h, 0:NP],
                                                          row[:, q * BANK:q * BANK + w], start=True, stop=True),
                              [ready, t_pick] + bank_free[b0:b0 + 3])
                return t

            def spread_view(b0):
                return psum[0:NP, b0 * BANK:b0 * BANK + N]
            t_rows = to_rows(srcs, rowT["src"], t_tgt)
            for h in range(HEADS1):
                b0 = 3 * (h % 2)
                t = spread_row(rowT["src"], h, b0, t_rows)
                for j in range(NT):
                    t2 = dve.do(lambda e, h=h, j=j, b0=b0: e.tensor_tensor_reduce(
                        trash[:], spread_view(b0), no_edge[:, j, :], 1.0, 3 * MASKED, ALU.add, ALU.max, nb_max[:, j, h:h + 1]), [t, dve.last()])
                bank_free[b0] = bank_free[b0 + 1] = bank_free[b0 + 2] = t2
            t = dve.do(lambda e: e.tensor_tensor(nb_max[:], nb_max[:], tgt[:], ALU.add), [t2])
            t = dve.do(lambda e: e.scalar_tensor_tensor(nb_max[:], nb_max[:], 0.2, nb_max[:], ALU.mult, ALU.max), [t])
            t_neg = dve.do(lambda e: e.scalar_tensor_tensor(leak[:], tgt[:], 0.2, nb_max[:], ALU.mult, ALU.subtract), [t])
            t_pos = dve.do(lambda e: e.tensor_tensor(nb_max[:], tgt[:], nb_max[:], ALU.subtract), [t_neg])
            t_pos = to_rows(nb_max, rowT["pos"], t_pos)
            t_neg = to_rows(leak, rowT["neg"], t_neg)
            fence()
            s = Region(WORK, AT0)
            pos_row = [s.take(f"pos_row{i}", [NP, N]) for i in range(2)]
            neg_row = [s.take(f"neg_row{i}", [NP, N]) for i in range(2)]
            s = Region(SHIFT0, SHIFT0 + 4 * KD * N + 4 * KD * D)
            low = [s.take(f"low{i}", [NP, N]) for i in range(2)]
            weight = [s.take(f"weight{i}", [NP, N]) for i in range(3)]
            recip = g.take("recip1", [NP, NT])
            PER_BANK = BANK // (DH1 + 1)
            low_free, weight_free = [None] * 2, [None] * 3
            row_free = [None, None]
            out_free = None
            n = 0
            for h in range(HEADS1):
                i = h % 2
                t = spread_row(rowT["pos"], h, 0, t_pos)
                t_a = act.do(lambda e, i=i: e.copy(pos_row[i][:], spread_view(0)), [t, row_free[i]])
                bank_free[0:3] = [t_a] * 3
                t = spread_row(rowT["neg"], h, 3, t_neg)
                t_b = act.do(lambda e, i=i: e.copy(neg_row[i][:], spread_view(3)), [t])
                bank_free[3:6] = [t_b] * 3
                for s_ in range(NT):
                    lo, wt = low[n % 2], weight[n % 3]
                    t = pool.do(lambda e, lo=lo, i=i, s_=s_, h=h: e.tensor_scalar(lo[:], neg_row[i][:], srcs02[:, s_, h:h + 1], None, ALU.add), [t_b, low_free[n % 2]])
                    t = dve.do(lambda e, lo=lo, wt=wt, i=i, s_=s_, h=h: e.scalar_tensor_tensor(
                        wt[:], pos_row[i][:], srcs[:, s_, h:h + 1], lo[:], ALU.add, ALU.max), [t, t_a, weight_free[n % 3]])
                    low_free[n % 2] = t
                    row_free[i] = t
                    t = act.do(lambda e, wt=wt: e.activation(wt[:], wt[:], ACT.Exp), [t])
                    t = dve.do(lambda e, wt=wt, s_=s_: e.scalar_tensor_tensor(wt[:], wt[:], 1.0, counts[:, s_, :], ALU.min, ALU.mult), [t])
                    for j in range(NT):
                        b, c = 6 + j // PER_BANK, (j % PER_BANK) * (DH1 + 1)
                        t2 = pe.do(lambda e, wt=wt, j=j, b=b, c=c, s_=s_, h=h: e.matmul(
                            psum[0:NP, b * BANK + c:b * BANK + c + DH1 + 1], wt[:, j * NP:(j + 1) * NP], WH[:, s_, h, :],
                            start=s_ == 0 and j % PER_BANK == 0, stop=s_ == NT - 1 and j in (PER_BANK - 1, NT - 1), skip_group_check=True),
                            [t, out_free if s_ == 0 else None])
                    weight_free[n % 3] = t2
                    n += 1
                for j0, j1 in ((0, PER_BANK), (PER_BANK, NT)):
                    b = 6 + j0 // PER_BANK
                    v = psum[0:NP, b * BANK:b * BANK + (j1 - j0) * (DH1 + 1)].rearrange("p (j c) -> p j c", c=DH1 + 1)
                    t = dve.do(lambda e, v=v, j0=j0, j1=j1: e.tensor_scalar(recip[:, j0:j1], v[:, :, DH1], 1e-30, None, ALU.max), [t2])
                    t = dve.do(lambda e, j0=j0, j1=j1: e.reciprocal(recip[:, j0:j1], recip[:, j0:j1]), [t])
                    out_free = dve.do(lambda e, v=v, j0=j0, j1=j1, h=h: e.tensor_tensor(
                        H[:, j0:j1, h * DH1:(h + 1) * DH1], v[:, :, 0:DH1], recip[:, j0:j1].unsqueeze(2).to_broadcast([NP, j1 - j0, DH1]), ALU.mult), [t])
            x_ready = [dve.do(lambda e, j=j: e.tensor_tensor(X[:, j, :], X[:, j, :], H[:, j, :], ALU.add), [out_free]) for j in range(NT)]
            x_ready = layer_norm(x_ready)
            fence()
            return x_ready

        x_ready = layer1(x_ready)
        if stop_after == "L1":
            return finish_program(nc, ctx, out, X, dma, (pe, dve, act, pool, sp), x_ready, NP)

        def layer2(x_ready):
            g = Region(WORK, ARENA)
            Y = g.take("Y2", [NP, NT, D])
            H = g.take("H2", [NP, NT, D])
            T = g.take("T2", [128, KD, N])
            W_in = g.take("W2_in", [128, KD, D])
            WT = g.take("W2_T", [128, KD, D])
            b2 = g.take("b2", [NP, D])
            dinv = g.take("dinv", [NP, NT])
            t_w = dma("wa", sp, W_in[:], L2["W"].rearrange("(m p) n -> p m n", p=128))
            t_b2 = dma("b_conv", sp, b2[:], row_on_partitions(L2["b"]))
            t = dve.do(lambda e: e.tensor_scalar(dinv[:], deg[:], 1.0, None, ALU.add))
            t_dinv = pool.do(lambda e: e.tensor_tensor(dinv[:], dinv[:], minus_half[0:NP, :], ALU.pow), [t])
            for k in range(KD):
                b = k
                for m in range(KD):
                    t = pe.do(lambda e, k=k, m=m, b=b: e.transpose(bank(b)[:, m * 128:(m + 1) * 128], W_in[:, m, k * 128:(k + 1) * 128], ident[:]), [t_w, bank_free[b]])
                t_WT = bank_free[b] = act.do(lambda e, k=k, b=b: e.copy(WT[:, k, :], bank(b)), [t])
            t_T = transpose_nodes(X, lambda j, v, t: [copy_out(j, T[:, :, j * NP:(j + 1) * NP], v, [t])], x_ready)
            pe.wait([t_WT])
            y_ready = dense(T, WT, None, t_T, lambda j, ps, t: act.do(
                lambda e: e.activation(Y[:, j, :], ps, ACT.Identity, scale=dinv[:, j:j + 1]), [t, t_dinv]))
            h_ready = [dve.do(lambda e, j=j: e.scalar_tensor_tensor(H[:, j, :], Y[:, j, :], dinv[:, j:j + 1], b2[:], ALU.mult, ALU.add),
                              [y_ready[j], t_b2]) for j in range(NT)]
            h_ready = gather_sum(Y, y_ready, lambda j, ps, t: dve.do(
                lambda e: e.scalar_tensor_tensor(H[:, j, :], ps, dinv[:, j:j + 1], H[:, j, :], ALU.mult, ALU.add), [t, h_ready[j]]))
            dve.wait([pe.last()])
            bn_ready = batch_norm(H, Y, L2["gamma"], L2["beta"], g, "bn3", h_ready)
            x_ready = []
            for j in range(NT):
                t = act.do(lambda e, j=j: e.activation(Y[:, j, :], Y[:, j, :], ACT.Gelu), [bn_ready[j]])
                t = dve.do(lambda e, j=j: e.scalar_tensor_tensor(X[:, j, :], X[:, j, :], 2.0, Y[:, j, :], ALU.mult, ALU.add), [t])
                x_ready.append(t)
            x_ready = layer_norm(x_ready)
            fence()
            return x_ready

        x_ready = layer2(x_ready)
        if stop_after == "L2":
            return finish_program(nc, ctx, out, X, dma, (pe, dve, act, pool, sp), x_ready, NP)

        def layer3(x_ready):
            BLOCKS, COND = L3["s1_w"].shape[0], L3["s1_w"].shape[1]
            HEADS = 4
            DH = D // HEADS
            SCALE = DH ** -0.5
            FREQS = L3["f_w1"].shape[0] // 2
            TWO_PI = 2 * math.pi
            x_in = nc.dram_tensor("x_in", [N, D], F32, kind="Internal").ap()
            tiles_of = lambda ap: ap.rearrange("(j p) d -> p j d", p=NP)
            t_save = dma("x_in", sp, tiles_of(x_in), X[:], x_ready)
            g = Region(WORK, ARENA)
            cond3 = g.take("cond3", [96, N], F32R)
            yT = [g.take(f"yT_{p}", [128, KD, N], F32R) for p in ("hi", "lo")]
            bias_out = g.take("bias_out", [NP, D])
            has_edge = g.take("has_edge", [NP, NT])
            shift = g.take("ln_shift", [NP, NT])
            bias_cols = g.take("bias_cols", [128, 3, BLOCKS, KD])
            PHASE = g.at

            def load_bias_columns():
                rows = Region(PHASE, ARENA).take("bias_rows", [3 * BLOCKS * KD, 128])
                for n, name in enumerate(("bq", "bk", "m_b1")):
                    t = dma("bias_rows", sp, rows[n * BLOCKS * KD:(n + 1) * BLOCKS * KD, :], L3[name].rearrange("i (k p) -> (i k) p", p=128))
                R = 3 * BLOCKS * KD
                t = pe.do(lambda e: e.transpose(psum[:, 7 * BANK:7 * BANK + R], rows[:], ident[0:R, 0:R]), [t, bank_free[7]])
                bank_free[7] = act.do(lambda e: e.copy(bias_cols[:].rearrange("p n i k -> p (n i k)"), psum[:, 7 * BANK:7 * BANK + R]), [t])
            load_bias_columns()
            fence()

            def split_lo(q, lo, exact, hi, after):
                return q.do(lambda e: e.tensor_tensor(lo, exact, hi.bitcast(F32), ALU.subtract), after)

            def condition():
                g = Region(PHASE, ARENA)
                R = 2 * FREQS
                angle = g.take("angle", [R, N])
                turns = g.take("turns", [R, N])
                freq_i = g.take("freq_i", [R, 1], I32)
                freq = g.take("freq", [R, 1])
                quarter = g.take("quarter", [R, 1])
                hidden = g.take("hidden", [COND, N])
                sig = g.take("sig", [COND, N])
                f_w1 = g.take("f_w1", [R, COND])
                f_b1 = g.take("f_b1", [COND, 1])
                f_w2x3 = g.take("f_w2x3", [COND, 96])
                f_b2x3 = g.take("f_b2x3", [96, 1])
                exact = g.take("cond_exact", [96, N])
                t_n = dma("noise", sp, angle[:], noise.rearrange("n o -> (n o)").partition_broadcast(R))
                dma("cond_w", sp, f_w1[:], L3["f_w1"])
                dma("cond_w", sp, f_b1[:], L3["f_b1"].rearrange("(p o) -> p o", o=1))
                t0 = dve.do(lambda e: e.memset(f_w2x3[:], 0.0))
                t0 = dve.do(lambda e: e.tensor_tensor(f_b2x3[:], ident[0:96, COND:COND + 1], ident[0:96, 32 + COND:33 + COND], ALU.add))
                t0 = dve.do(lambda e: e.tensor_tensor(f_b2x3[:], f_b2x3[:], ident[0:96, 64 + COND:65 + COND], ALU.add), [t0])
                for i in range(3):
                    dma("cond_w", sp, f_w2x3[:, 32 * i:32 * i + COND], L3["f_w2"], [t0])
                    t_w = dma("cond_w", sp, f_b2x3[32 * i:32 * i + COND, :], L3["f_b2"].rearrange("(p o) -> p o", o=1))
                pool.do(lambda e: e.iota(freq_i[0:FREQS, :], pattern=[[0, 1]], base=1, channel_multiplier=1))
                t = pool.do(lambda e: e.iota(freq_i[FREQS:R, :], pattern=[[0, 1]], base=1, channel_multiplier=1))
                dve.do(lambda e: e.memset(quarter[0:FREQS, :], 0.0))
                t_q = dve.do(lambda e: e.memset(quarter[FREQS:R, :], 0.25))
                t = dve.do(lambda e: e.tensor_copy(freq[:], freq_i[:]), [t])
                t = dve.do(lambda e: e.tensor_scalar(freq[:], freq[:], TWO_PI / 16, None, ALU.mult), [t])
                t = dve.do(lambda e: e.tensor_scalar(angle[:], angle[:], freq[:, 0:1], None, ALU.mult), [t, t_n])
                t = dve.do(lambda e: e.tensor_scalar(turns[:], angle[:], 1 / TWO_PI, quarter[:, 0:1], ALU.mult, ALU.add), [t, t_q])
                ROUND = 1.5 * 2 ** 23
                t = dve.do(lambda e: e.tensor_scalar(turns[:], turns[:], ROUND, None, ALU.add), [t])
                t = dve.do(lambda e: e.tensor_scalar(turns[:], turns[:], ROUND, None, ALU.subtract), [t])
                part1 = 6.28125
                part2 = math.ldexp(round(math.ldexp(TWO_PI - part1, 21)), -21)
                part3 = TWO_PI - part1 - part2
                for part in (part1, part2, part3):
                    t = dve.do(lambda e, part=part: e.scalar_tensor_tensor(angle[:], turns[:], -part, angle[:], ALU.mult, ALU.add), [t])
                t = dve.do(lambda e: e.tensor_scalar(quarter[:], quarter[:], TWO_PI, None, ALU.mult), [t])
                t = dve.do(lambda e: e.tensor_scalar(angle[:], angle[:], quarter[:, 0:1], None, ALU.add), [t])
                PI = 3.1415925
                t = dve.do(lambda e: e.tensor_scalar(angle[:], angle[:], PI, -PI, ALU.min, ALU.max), [t])
                t = act.do(lambda e: e.activation(angle[:], angle[:], ACT.Sin), [t])

                def product(rows, lhsT, rhs, b0, after):
                    for q in range(3):
                        w = min(BANK, N - q * BANK)
                        t = pe.do(lambda e, q=q, w=w: e.matmul(psum[0:rows, (b0 + q) * BANK:(b0 + q) * BANK + w], lhsT,
                                                          rhs[:, q * BANK:q * BANK + w], start=True, stop=True), after)
                    return psum[0:rows, b0 * BANK:b0 * BANK + N], t
                ps, t = product(COND, f_w1[:], angle, 0, [t, t_w])
                t1 = act.do(lambda e: e.activation(hidden[:], ps, ACT.Identity, bias=f_b1[:, 0:1]), [t])
                t = act.do(lambda e: e.activation(sig[:], hidden[:], ACT.Exp, scale=-1.0), [t1])
                t = dve.do(lambda e: e.tensor_scalar(sig[:], sig[:], 1.0, None, ALU.add), [t])
                t = dve.do(lambda e: e.reciprocal(sig[:], sig[:]), [t])
                t = dve.do(lambda e: e.tensor_tensor(hidden[:], hidden[:], sig[:], ALU.mult), [t])
                ps2, t = product(96, f_w2x3[:], hidden, 3, [t])
                t = act.do(lambda e: e.activation(exact[:], ps2, ACT.Identity, bias=f_b2x3[:, 0:1]), [t])
                t = act.do(lambda e: e.copy(cond3[:], exact[:]), [t])
                return split_lo(dve, cond3[32:64, :], exact[32:64, :], cond3[32:64, :], [t])
            condition()
            fence()
            g = Region(PHASE, ARENA)
            absent = [g.take(f"absent{i}", [NP, N]) for i in range(2)]
            free = [None, None]
            for s in range(NT):
                a = absent[s % 2]
                t1 = dve.do(lambda e, s=s, a=a: e.tensor_scalar(a[:], counts[:, s, :], 0.0, MASKED, ALU.is_equal, ALU.mult), [free[s % 2]])
                t = dve.do(lambda e, s=s: e.tensor_reduce(has_edge[:, s:s + 1], counts[:, s, :], AX.X, ALU.max))
                t = dve.do(lambda e, s=s: e.tensor_scalar(counts[:, s, :], counts[:, s, :], 1.0, None, ALU.max), [t, t1])
                t = act.do(lambda e, s=s: e.activation(counts[:, s, :], counts[:, s, :], ACT.Ln), [t])
                free[s % 2] = dve.do(lambda e, s=s, a=a: e.scalar_tensor_tensor(counts[:, s, :], counts[:, s, :], 1 / SCALE, a[:], ALU.mult, ALU.add), [t])
            dve.do(lambda e: e.tensor_scalar(has_edge[:], has_edge[:], 1.0, None, ALU.min), [dve.last()])
            edge_term = counts

            def split_weight(name, stage, hi, lo, source, free):
                t = dma(name, sp, stage[:], source, [pool_done.get(name)])
                t = pool.do(lambda e: e.tensor_copy(hi[:], stage[:]), [t] + free)
                t = pool_done[name] = split_lo(pool, lo[:], stage[:], hi[:], [t])
                return t
            pool_done = {}

            def cond_norm(i, a, g, t_bias):
                stage = g.take(f"cw_in{i}{a}", [96, 2, D])
                w3 = g.take(f"cw3_{i}{a}", [96, 2, D], F32R)
                xn = [g.take(f"xn{i}{a}{n}", [NP, D]) for n in range(3)]
                t0 = pool.do(lambda e: e.memset(stage[:], 0.0))
                for n, c in enumerate("sb"):
                    for r in range(3):
                        dma("cw", sp, stage[32 * r:32 * r + COND, n, :], L3[f"{c}{a}_w"][i], [t0])
                        t = dma("cw", sp, stage[32 * r + COND:32 * r + COND + 1, n, :], L3[f"{c}{a}_b"][i:i + 1, :])
                t = act.do(lambda e: e.copy(w3[:], stage[:]), [t])
                t_w = split_lo(dve, w3[64:96, :, :], stage[64:96, :, :], w3[64:96, :, :], [t])
                for j in range(NT):
                    dve.do(lambda e, j=j: e.bn_stats(stats[:, j, :], X[:, j, :]))
                t = dve.last()
                for j in range(NT):
                    dve.do(lambda e, j=j: e.bn_aggr(mean_var[:, j, :], stats[:, j, :]), [t])
                t = dve.do(lambda e: e.tensor_scalar(rstd[:], mean_var[:, :, 1], EPS, None, ALU.add), [dve.last()])
                t = pool.do(lambda e: e.tensor_tensor(rstd[:], rstd[:], minus_half[0:NP, :], ALU.pow), [t])
                t = dve.do(lambda e: e.scalar_tensor_tensor(shift[:], mean_var[:, :, 0], -1.0, rstd[:], ALU.mult, ALU.mult), [t])
                xn_free = [None] * 3
                for j in range(NT):
                    x_, b0 = xn[j % 3], 2 * (j % 2)
                    t1 = act.do(lambda e, j=j, x_=x_: e.activation(x_[:], X[:, j, :], ACT.Identity, bias=shift[:, j:j + 1], scale=rstd[:, j:j + 1]), [t, xn_free[j % 3]])
                    for n in range(2):
                        t2 = pe.do(lambda e, j=j, n=n, b0=b0: e.matmul(bank(b0 + n, D, NP), cond3[:, j * NP:(j + 1) * NP], w3[:, n, :], start=True, stop=True), [t_w, bank_free[b0 + n]])
                    t3 = bank_free[b0] = dve.do(lambda e, x_=x_, b0=b0: e.scalar_tensor_tensor(x_[:], bank(b0, D, NP), 1.0, x_[:], ALU.add, ALU.mult), [t1, t2])
                    t4 = bank_free[b0 + 1] = dve.do(lambda e, x_=x_, b0=b0: e.tensor_tensor(x_[:], bank(b0 + 1, D, NP), x_[:], ALU.add), [t3])
                    b = 4 + j % 2
                    v = bank(b).rearrange("p (k c) -> p k c", k=KD)
                    for k in range(KD):
                        t5 = pe.do(lambda e, x_=x_, k=k, v=v: e.transpose(v[:, k, 0:NP], x_[:, k * 128:(k + 1) * 128], ident[0:NP, 0:NP]), [t4, bank_free[b]])
                    xn_free[j % 3] = t5
                    c = slice(j * NP, (j + 1) * NP)
                    t6 = act.do(lambda e, v=v, c=c: e.copy(yT[0][:, :, c], v[:, :, 0:NP]), [t5])
                    bank_free[b] = split_lo(dve, yT[1][:, :, c], v[:, :, 0:NP], yT[0][:, :, c], [t6])
                for j in range(NT):
                    t_b = pool.do(lambda e, j=j: e.tensor_tensor(X[:, j, :], X[:, j, :], bias_out[:], ALU.add), [t_bias, act.last()])
                return bank_free[4 + (NT - 1) % 2], t_b

            def three_products(out_, lhs, rhs, first, last, after, quiet=False):
                for n, (a, b) in enumerate(((0, 0), (0, 1), (1, 0))):
                    t = pe.do(lambda e, a=a, b=b, n=n: e.matmul(out_, lhs[a], rhs[b], start=first and n == 0, stop=last and n == 2),
                              after, quiet=quiet or n < 2)
                return t

            def attention_block(i):
                fence()
                g = Region(PHASE, ARENA)
                qk = {c: [g.take(f"{c}{i}_{p}", [128, N], F32R) for p in ("hi", "lo")] for c in "qk"}
                v2 = g.take(f"v2_{i}", [NP, NT, 2, DH], F32R)
                oT = [g.take(f"oT{i}_{p}", [128, N], F32R) for p in ("hi", "lo")]
                pT = [g.take(f"pT{i}_{p}", [NP, NT, NP], F32R) for p in ("hi", "lo")]
                prob = [g.take(f"prob{i}_{n}", [NP, N]) for n in range(3)]
                w_in = g.take(f"w_in{i}", [128, KD, DH])
                w2 = {c: [g.take(f"w{c}{i}_{p}", [128, KD, DH], F32R) for p in ("hi", "lo")] for c in "qkv"}
                wo_in = g.take(f"wo_in{i}", [128, D])
                wo2 = [g.take(f"wo{i}_{p}", [128, D], F32R) for p in ("hi", "lo")]
                b_v = g.take(f"b_v{i}", [NP, D])
                o_sb = [g.take(f"o_sb{i}_{n}", [NP, DH]) for n in range(2)]
                o_lo = g.take(f"o_lo{i}", [NP, DH])
                row_max = g.take(f"row_max{i}", [NP, 4])
                row_sum = g.take(f"row_sum{i}", [NP, 4])
                t_bv = dma("b_v", sp, b_v[:], row_on_partitions(L3["bv"][i]))
                t_bo = dma("bias_out", sp, bias_out[:], row_on_partitions(L3["bo"][i]))

                def load_head(h, after):
                    cols = slice(h * DH, (h + 1) * DH)
                    t = {}
                    for c in "qkv":
                        t[c] = split_weight("w_in", w_in, w2[c][0], w2[c][1],
                                            L3["w" + c][i].rearrange("(k p) n -> p k n", p=128)[:, :, cols], [after.get(c)])
                    t["o"] = split_weight("w_o", wo_in, wo2[0], wo2[1], L3["wo"][i][cols, :], [after.get("o")])
                    return t

                def project_qk(c, h, w_ready, y_ready):
                    b0, n = (0, 0) if c == "q" else (3, 1)
                    for q in range(3):
                        w = min(BANK, N - q * BANK)
                        for k in range(KD):
                            t = three_products(psum[:, (b0 + q) * BANK:(b0 + q) * BANK + w], [p[:, k, :] for p in w2[c]],
                                               [p[:, k, q * BANK:q * BANK + w] for p in yT], k == 0, k == KD - 1,
                                               [w_ready, y_ready] + bank_free[b0:b0 + 3])
                    ps = psum[:, b0 * BANK:b0 * BANK + N]
                    bias = bias_cols[:, n, i, h:h + 1]
                    t1 = act.do(lambda e: e.activation(qk[c][0][:], ps, ACT.Identity, bias=bias), [t])
                    t2 = dve.do(lambda e: e.scalar_tensor_tensor(qk[c][1][:], ps, bias, qk[c][0][:].bitcast(F32), ALU.add, ALU.subtract), [t1])
                    bank_free[b0:b0 + 3] = [t2] * 3
                    return t2, t

                def project_v(h, w_ready, buf, buf_free):
                    v32 = buf[:, 0:N].rearrange("p (j c) -> p j c", j=NT) if False else None
                    for j0 in range(0, NT, 4):
                        m = min(4, NT - j0)
                        b = 6 + (j0 // 4) % 2
                        for j in range(j0, j0 + m):
                            o = psum[0:NP, b * BANK + (j - j0) * DH:b * BANK + (j - j0 + 1) * DH]
                            for k in range(KD):
                                t = three_products(o, [p[:, k, j * NP:(j + 1) * NP] for p in yT], [p[:, k, :] for p in w2["v"]],
                                                   k == 0, k == KD - 1, [w_ready, bank_free[b]])
                        v = bank(b, m * DH, NP).rearrange("p (j c) -> p j c", c=DH)
                        tmp = buf[:, 0:m * DH].rearrange("p (j c) -> p j c", c=DH)
                        bv = b_v[:, h * DH:(h + 1) * DH].unsqueeze(1).to_broadcast([NP, m, DH])
                        t1 = bank_free[b] = dve.do(lambda e, v=v, tmp=tmp, bv=bv: e.tensor_tensor(tmp, v, bv, ALU.add), [t, t_bv, buf_free])
                        t2 = act.do(lambda e, tmp=tmp, j0=j0, m=m: e.copy(v2[:, j0:j0 + m, 0, :], tmp), [t1])
                        buf_free = split_lo(dve, v2[:, j0:j0 + m, 1, :], tmp, v2[:, j0:j0 + m, 0, :], [t2])
                    return buf_free, t

                prob_free = [None] * 3
                w_ready = load_head(0, {})
                t_y, t_b = cond_norm(i, 1, Region(PHASE, PHASE + 20000), t_bo)
                t_oT = None
                n_prob = 0
                wo_used = None

                def output_product(h, t_oT, t_w, t_b):
                    for j in range(NT):
                        b = 6 + j % 2
                        t = three_products(bank(b, D, NP), [p[:, j * NP:(j + 1) * NP] for p in oT], [p[:] for p in wo2], True, True,
                                           [t_oT, t_w, bank_free[b]])
                        bank_free[b] = dve.do(lambda e, j=j, b=b: e.tensor_tensor(X[:, j, :], bank(b, D, NP), X[:, j, :], ALU.add), [t, t_b])
                    return t
                for h in range(HEADS):
                    t_q, uq = project_qk("q", h, w_ready["q"], t_y)
                    t_k, uk = project_qk("k", h, w_ready["k"], t_y)
                    if h:
                        wo_used = output_product(h - 1, t_oT, wo_ready, t_b)
                    p = n_prob % 3
                    n_prob += 1
                    t_v, uv = project_v(h, w_ready["v"], prob[p], prob_free[p])
                    prob_free[p] = t_v
                    wo_ready = w_ready["o"]
                    if h + 1 < HEADS:
                        w_next = {}
                        cols = slice((h + 1) * DH, (h + 2) * DH)
                        for c, used in (("q", uq), ("k", uk), ("v", uv)):
                            w_next[c] = split_weight("w_in", w_in, w2[c][0], w2[c][1],
                                                     L3["w" + c][i].rearrange("(k p) n -> p k n", p=128)[:, :, cols], [used])
                    if h:
                        wo_ready = split_weight("w_o", wo_in, wo2[0], wo2[1], L3["wo"][i][h * DH:(h + 1) * DH, :], [wo_used])
                    soft, turned = {}, {}

                    def scores(n):
                        nonlocal n_prob
                        for q in range(3):
                            w = min(BANK, N - q * BANK)
                            t = three_products(psum[0:NP, q * BANK:q * BANK + w], [p[:, n * NP:(n + 1) * NP] for p in qk["q"]],
                                               [p[:, q * BANK:q * BANK + w] for p in qk["k"]], True, True, [t_q, t_k] + bank_free[0:3])
                        p = n_prob % 3
                        n_prob += 1
                        P, m = prob[p], n % 4
                        t = dve.do(lambda e, P=P, m=m: e.tensor_tensor_reduce(
                            P[:], psum[0:NP, 0:N], edge_term[:, n, :], 1.0, 3 * MASKED, ALU.add, ALU.max, row_max[:, m:m + 1]), [t, prob_free[p]])
                        bank_free[0:3] = [t] * 3
                        t = dve.do(lambda e, m=m: e.tensor_scalar(row_max[:, m:m + 1], row_max[:, m:m + 1], -SCALE, None, ALU.mult), [t])
                        t = act.do(lambda e, P=P, m=m: e.activation(P[:], P[:], ACT.Exp, bias=row_max[:, m:m + 1], scale=SCALE,
                                                                accum_out=row_sum[:, m:m + 1]), [t])
                        t1 = dve.do(lambda e, m=m: e.reciprocal(row_sum[:, m:m + 1], row_sum[:, m:m + 1]), [t])
                        t1 = dve.do(lambda e, m=m: e.tensor_tensor(row_sum[:, m:m + 1], row_sum[:, m:m + 1], has_edge[:, n:n + 1], ALU.mult), [t1])
                        soft[n] = (p, t, t1)

                    def turn(n):
                        p, t0, _ = soft[n]
                        turned[n] = []
                        for q in range(3):
                            m = min(4, NT - 4 * q)
                            b = 3 + q
                            v = bank(b, m * 128, NP).rearrange("p (k c) -> p k c", c=128)
                            for k in range(m):
                                d = 4 * q + k
                                t = pe.do(lambda e, k=k, d=d, v=v, p=p: e.transpose(v[:, k, 0:NP], prob[p][:, d * NP:(d + 1) * NP], ident[0:NP, 0:NP]),
                                          [t0, bank_free[b]], quiet=k < m - 1)
                            hi, lo = (x_[:, 4 * q:4 * q + m, :] for x_ in pT)
                            t1 = act.do(lambda e, v=v, hi=hi: e.copy(hi, v[:, :, 0:NP]), [t])
                            bank_free[b] = split_lo(dve, lo, v[:, :, 0:NP], hi, [t1])
                            turned[n].append(bank_free[b])
                        prob_free[p] = t

                    def mix(n):
                        for d in range(NT):
                            pe.wait([turned[n][d // 4], t_v, bank_free[6]])
                            whole = lambda e, d=d: e.matmul(bank(6, 2 * DH, NP), pT[0][:, d, :], v2[:, d, :, :].rearrange("p a c -> p (a c)"),
                                                            start=d == 0, stop=d == NT - 1)
                            rest = lambda e, d=d: e.matmul(bank(6, DH, NP), pT[1][:, d, :], v2[:, d, 0, :], start=False, stop=False,
                                                           skip_group_check=True)
                            for make in ((whole, rest) if d < NT - 1 else (rest, whole)):
                                t = pe.do(make, quiet=not (d == NT - 1 and make is whole))
                        m, m2 = n % 4, n % 2
                        ps = psum[0:NP, 6 * BANK:6 * BANK + 2 * DH]
                        r = row_sum[:, m:m + 1]
                        t = act.do(lambda e: e.activation(o_lo[:], ps[:, DH:2 * DH], ACT.Identity, scale=r), [t, soft[n][2], dve.last()])
                        t = bank_free[6] = dve.do(lambda e: e.scalar_tensor_tensor(o_sb[m2][:], ps[:, 0:DH], r, o_lo[:], ALU.mult, ALU.add), [t])
                        return t

                    def turn_output(n, t):
                        t = pe.do(lambda e: e.transpose(psum[:, 7 * BANK:7 * BANK + NP], o_sb[n % 2][:], ident[0:NP, 0:NP]), [t, bank_free[7]])
                        c = slice(n * NP, (n + 1) * NP)
                        t = act.do(lambda e: e.copy(oT[0][:, c], psum[:, 7 * BANK:7 * BANK + NP]), [t])
                        bank_free[7] = split_lo(dve, oT[1][:, c], psum[:, 7 * BANK:7 * BANK + NP], oT[0][:, c], [t])
                    mixed = {}
                    for n in range(NT + 3):
                        if n < NT:
                            scores(n)
                        if 0 <= n - 2 < NT:
                            mixed[n - 2] = mix(n - 2)
                        if 0 <= n - 1 < NT:
                            turn(n - 1)
                        if n - 3 >= 0:
                            turn_output(n - 3, mixed[n - 3])
                    t_oT = bank_free[7]
                    if h + 1 < HEADS:
                        w_ready = w_next
                        w_ready["o"] = None
                output_product(HEADS - 1, t_oT, wo_ready, t_b)

            def mlp_block(i):
                fence()
                g = Region(PHASE, ARENA)
                hT = [g.take(f"hT{i}_{p}", [128, KD, N], F32R) for p in ("hi", "lo")]
                m_in = g.take(f"m_in{i}", [128, KD, D])
                m1 = [g.take(f"m1_{i}_{p}", [128, KD, D], F32R) for p in ("hi", "lo")]
                m2 = [g.take(f"m2_{i}_{p}", [128, KD, D], F32R) for p in ("hi", "lo")]
                relu = g.take(f"relu{i}", [128, N])
                t_b2 = dma("bias_out", sp, bias_out[:], row_on_partitions(L3["m_b2"][i]))
                t_m1 = split_weight("m_in", m_in, m1[0], m1[1], L3["m_w1"][i].rearrange("(k p) n -> p k n", p=128), [])
                t_y, t_b = cond_norm(i, 2, Region(PHASE, PHASE + 20000), t_b2)
                t_m2 = split_weight("m_in", m_in, m2[0], m2[1], L3["m_w2"][i].rearrange("(k p) n -> p k n", p=128), [])
                relu_free = None
                for m in range(KD):
                    b0 = 3 * (m % 2)
                    for q in range(3):
                        w = min(BANK, N - q * BANK)
                        for k in range(KD):
                            t = three_products(psum[:, (b0 + q) * BANK:(b0 + q) * BANK + w], [p[:, k, m * 128:(m + 1) * 128] for p in m1],
                                               [p[:, k, q * BANK:q * BANK + w] for p in yT], k == 0, k == KD - 1,
                                               [t_m1, t_y] + bank_free[b0:b0 + 3])
                    ps = psum[:, b0 * BANK:b0 * BANK + N]
                    t1 = act.do(lambda e, m=m, ps=ps: e.activation(relu[:], ps, ACT.Relu, bias=bias_cols[:, 2, i, m:m + 1]), [t, relu_free])
                    bank_free[b0:b0 + 3] = [t1] * 3
                    t2 = act.do(lambda e, m=m: e.copy(hT[0][:, m, :], relu[:]), [t1])
                    relu_free = split_lo(dve, hT[1][:, m, :], relu[:], hT[0][:, m, :], [t2])
                for j in range(NT):
                    b = 6 + j % 2
                    for k in range(KD):
                        t = three_products(bank(b, D, NP), [p[:, k, j * NP:(j + 1) * NP] for p in hT], [p[:, k, :] for p in m2],
                                           k == 0, k == KD - 1, [relu_free, t_m2, bank_free[b]])
                    bank_free[b] = dve.do(lambda e, j=j, b=b: e.tensor_tensor(X[:, j, :], bank(b, D, NP), X[:, j, :], ALU.add), [t, t_b])

            for i in range(BLOCKS):
                attention_block(i)
                if stop_after == f"xa{i}":
                    return [dve.last()]
                mlp_block(i)
                if stop_after == f"xb{i}":
                    return [dve.last()]
            fence()
            before = Region(PHASE, ARENA).take("x_before", [NP, NT, D])
            t = dma("x_in", sp, before[:], tiles_of(x_in), [t_save])
            ready = [dve.do(lambda e, j=j: e.tensor_tensor(X[:, j, :], X[:, j, :], before[:, j, :], ALU.add), [t]) for j in range(NT)]
            return layer_norm(ready)

        x_ready = layer3(x_ready)
        finish_program(nc, ctx, out, X, dma, (pe, dve, act, pool, sp), x_ready, NP)


def finish_program(nc, ctx, out, X, dma, queues, ready, NP):
    pe, dve, act, pool, sp = queues
    t = dma("out", sp, out.rearrange("(j p) d -> p j d", p=NP), X[:], ready)
    sp.wait([t])
    block = ctx.enter_context(nc.Block())
    block.tensor(lambda e: pe.run(e))
    block.vector(lambda e: dve.run(e))
    block.scalar(lambda e: act.run(e))
    block.gpsimd(lambda e: pool.run(e))
    block.sync(lambda e: sp.run(e))


_INS = ['x', 'src', 'dst', 'node_vec1', 'L0_gnn_norm1_g', 'L0_gnn_norm1_b', 'L0_gnn_norm2_g', 'L0_gnn_norm2_b', 'L0_gnn_W_conv',
        'L0_gnn_b_conv', 'L0_gnn_Wq', 'L0_gnn_Wk', 'L0_gnn_Wv', 'L0_gnn_Wo', 'L0_gnn_proj', 'L1_gnn_Ws', 'L1_gnn_Wb', 'L1_gnn_a_w',
        'L1_gnn_a_b', 'L2_gnn_W', 'L2_gnn_b', 'L2_gnn_gamma', 'L2_gnn_beta', 'L3_gnn_f_w1', 'L3_gnn_f_b1', 'L3_gnn_f_w2',
        'L3_gnn_f_b2', 'L3_gnn_s1_w', 'L3_gnn_s1_b', 'L3_gnn_b1_w', 'L3_gnn_b1_b', 'L3_gnn_wq', 'L3_gnn_bq', 'L3_gnn_wk',
        'L3_gnn_bk', 'L3_gnn_wv', 'L3_gnn_bv', 'L3_gnn_wo', 'L3_gnn_bo', 'L3_gnn_s2_w', 'L3_gnn_s2_b', 'L3_gnn_b2_w',
        'L3_gnn_b2_b', 'L3_gnn_m_w1', 'L3_gnn_m_b1', 'L3_gnn_m_w2', 'L3_gnn_m_b2']


def build(nc, args, out, stop_after=None):
    layer = lambda p: {k[len(p):]: v for k, v in args.items() if k.startswith(p)}
    build_layers(nc, args["x"], args["src"], args["dst"], args["node_vec1"], layer("L0_gnn_"), layer("L1_gnn_"),
                 layer("L2_gnn_"), layer("L3_gnn_"), out, stop_after)


def kernel(**inputs):
    import numpy as _np
    import concourse.bacc as _bacc
    from concourse import mybir as _mybir
    from concourse.bass_utils import run_bass_kernel_spmd as _run

    nc = _bacc.Bacc("TRN2", target_bir_lowering=False, num_devices=1)
    arrays, args = {}, {}
    for name in _INS:
        a = _np.ascontiguousarray(inputs[name])
        arrays[f"in_{name}"] = a
        args[name] = nc.dram_tensor(f"in_{name}", a.shape, _mybir.dt.from_np(a.dtype), kind="ExternalInput").ap()
    out = nc.dram_tensor("out", inputs["x"].shape, _mybir.dt.float32, kind="ExternalOutput").ap()
    build(nc, args, out)
    return _run(nc, [arrays], core_ids=[0]).results[0]["out"]
```

```python
import math
from contextlib import ExitStack

import concourse.bass as bass
from concourse import mybir

ALU = mybir.AluOpType
ACT = mybir.ActivationFunctionType
AX = mybir.AxisListType
F32 = mybir.dt.float32
F32R = mybir.dt.float32r
BF16 = mybir.dt.bfloat16
F16 = mybir.dt.float16
I32 = mybir.dt.int32

BANK = 512
PE_ROWS = 128
EPS = 1e-5
KEPS = 1e-6
MASKED = -1e30


class Tick:
    def __init__(self, sem, value):
        self.sem, self.value = sem, value


class Queue:
    def __init__(self, sem):
        self.sem, self.count, self.steps, self.waited = sem, 0, [], {}

    def wait(self, after):
        for tick in after:
            if tick is not None and self.waited.get(id(tick.sem), 0) < tick.value:
                self.waited[id(tick.sem)] = tick.value
                self.steps.append(lambda e, t=tick: e.wait_ge(t.sem, t.value))

    def do(self, make, after=(), quiet=False):
        self.wait(after)
        if quiet:
            self.steps.append(make)
            return None
        self.count += 1
        self.steps.append(lambda e: make(e).then_inc(self.sem, 1))
        return Tick(self.sem, self.count)

    def last(self):
        return Tick(self.sem, self.count) if self.count else None

    def run(self, engine):
        for step in self.steps:
            step(engine)


class DmaSlot:
    def __init__(self, sem):
        self.sem, self.count = sem, 0

    def move(self, queue, out, in_, after=()):
        queue.wait(after)
        self.count += 16
        queue.steps.append(lambda e: e.dma_start(out, in_).then_inc(self.sem, 16))
        return Tick(self.sem, self.count)


def build_layers(nc, x, src, dst, noise, L0, L1, L2, L3, out, stop_after=None):
    N, D = x.shape
    E = src.shape[0]
    NP = 125
    NT = N // NP
    KD = D // PE_ROWS
    assert NP * NT == N and E % NP == 0 and KD * PE_ROWS == D
    NCHUNK = E // NP
    with ExitStack() as ctx:
        sem = lambda name: ctx.enter_context(nc.semaphore(name))
        pe, dve, act, pool, sp = (Queue(sem(n)) for n in ("pe_done", "dve_done", "act_done", "pool_done", "sp_done"))
        slots = {}

        def dma(name, queue, out_, in_, after=()):
            if name not in slots:
                slots[name] = DmaSlot(sem("dma_" + name))
            return slots[name].move(queue, out_, in_, after)

        ARENA = 212600
        ctx.enter_context(nc.sbuf_tensor("arena", [128, ARENA], mybir.dt.uint8))
        base = nc.sbuf_base - ARENA
        size = {F32: 4, F32R: 4, BF16: 2, F16: 2, I32: 4}

        class Region:
            def __init__(self, at, end):
                self.at, self.end = at, end

            def take(self, name, shape, dtype=F32):
                n = size[dtype]
                for s in shape[1:]:
                    n *= s
                t = nc.alloc_sbuf_tensor_at(name, shape, dtype, offset=base + self.at)
                self.at += (n + 31) // 32 * 32
                assert self.at <= self.end, (name, self.at, self.end)
                return t

        keep = Region(0, 76000)
        counts = keep.take("counts", [NP, NT, N])
        X = keep.take("X", [NP, NT, D])
        ident = keep.take("ident", [128, 128])
        ones = keep.take("ones", [128, 128])
        minus_half = keep.take("minus_half", [128, NT])
        deg = keep.take("deg", [NP, NT])
        stats = keep.take("stats", [NP, NT, 6])
        mean_var = keep.take("mean_var", [NP, NT, 2])
        rstd = keep.take("rstd", [NP, NT])
        WORK = keep.at
        psum = ctx.enter_context(nc.psum_tensor("psum", [128, 8 * BANK], F32))
        bank_free = [None] * 8

        def bank(b, n=BANK, rows=128):
            return psum[0:rows, b * BANK:b * BANK + n]

        def everything():
            return [q.last() for q in (pe, dve, act, pool)] + [Tick(s.sem, s.count) for s in slots.values()]

        def fence():
            done = everything()
            for q in (pe, dve, act, pool, sp):
                q.wait(done)

        def row_on_partitions(ap, n=NP):
            return ap.partition_broadcast(n)

        def transpose_nodes(source, store, ready, banks=(6, 7), width=NP):
            done = []
            for j in range(NT):
                b = banks[j % len(banks)]
                view = bank(b).rearrange("p (k c) -> p k c", k=KD)
                for k in range(KD):
                    t = pe.do(lambda e, j=j, k=k, v=view: e.transpose(
                        v[:, k, 0:width], source[0:width, j, k * 128:(k + 1) * 128], ident[0:width, 0:width]),
                        after=[ready[j], bank_free[b]], quiet=k < KD - 1)
                ticks = store(j, view[:, :, 0:width], t)
                bank_free[b] = ticks[-1]
                done.append(ticks[-1])
            return done

        def copy_out(i, out_, in_, after):
            if i % 2:
                return dve.do(lambda e: e.tensor_copy(out_, in_), after)
            return act.do(lambda e: e.copy(out_, in_), after)

        def layer_norm(ready):
            done = []
            for j in range(NT):
                t = dve.do(lambda e, j=j: e.bn_stats(stats[:, j, :], X[:, j, :]), [ready[j]])
            for j in range(NT):
                t = dve.do(lambda e, j=j: e.bn_aggr(mean_var[:, j, :], stats[:, j, :]), [dve.last()] if j == 0 else [])
            t = dve.do(lambda e: e.tensor_scalar(rstd[:], mean_var[:, :, 1], EPS, None, ALU.add), [t])
            t = pool.do(lambda e: e.tensor_tensor(rstd[:], rstd[:], minus_half[0:NP, :], ALU.pow), [t])
            for j in range(NT):
                done.append(dve.do(lambda e, j=j: e.tensor_scalar(
                    X[:, j, :], X[:, j, :], mean_var[:, j, 0:1], rstd[:, j:j + 1], ALU.subtract, ALU.mult), [t]))
            return done

        def batch_norm(source, target, gain_row, bias_row, region, tag, ready):
            gain = region.take(tag + "_gain", [NP, D])
            bias = region.take(tag + "_bias", [NP, D])
            mean = region.take(tag + "_mean", [NP, D])
            squares = [region.take(f"{tag}_square{i}", [NP, D]) for i in range(2)]
            root = region.take(tag + "_root", [NP, D])
            fix = region.take(tag + "_fix", [NP, D])
            t_gain = dma("gain", sp, gain[:], row_on_partitions(gain_row))
            t_bias = dma("bias", sp, bias[:], row_on_partitions(bias_row))
            for j in range(NT):
                t = pe.do(lambda e, j=j: e.matmul(bank(0, D, NP), ones[0:NP, 0:NP], source[:, j, :],
                                                  start=j == 0, stop=j == NT - 1), [ready[j], bank_free[0]])
            t_mean = act.do(lambda e: e.mul(mean[:], bank(0, D, NP), 1.0 / N), [t])
            squared = [None, None]
            for j in range(NT):
                centred = dve.do(lambda e, j=j: e.tensor_tensor(target[:, j, :], source[:, j, :], mean[:], ALU.subtract), [t_mean])
                sq = squares[j % 2]
                t = act.do(lambda e, j=j, sq=sq: e.square(sq[:], target[:, j, :]), [centred, squared[j % 2]])
                t = squared[j % 2] = pe.do(lambda e, j=j, sq=sq: e.matmul(
                    bank(1, D, NP), ones[0:NP, 0:NP], sq[:], start=j == 0, stop=j == NT - 1), [t, bank_free[1]])
            t = dve.do(lambda e: e.tensor_scalar(mean[:], bank(1, D, NP), 1.0 / N, EPS, ALU.mult, ALU.add), [t])
            bank_free[0] = t_mean
            bank_free[1] = t
            t = act.do(lambda e: e.sqrt(root[:], mean[:]), [t])
            t = dve.do(lambda e: e.reciprocal(root[:], root[:]), [t])
            t = dve.do(lambda e: e.tensor_tensor(fix[:], root[:], root[:], ALU.mult), [t])
            t = dve.do(lambda e: e.tensor_tensor(fix[:], fix[:], mean[:], ALU.mult), [t])
            t = dve.do(lambda e: e.tensor_scalar(fix[:], fix[:], -0.5, 1.5, ALU.mult, ALU.add), [t])
            t = dve.do(lambda e: e.tensor_tensor(root[:], root[:], fix[:], ALU.mult), [t])
            t = dve.do(lambda e: e.tensor_tensor(mean[:], root[:], gain[:], ALU.mult), [t, t_gain])
            t = [dve.do(lambda e, j=j: e.tensor_tensor(target[:, j, :], target[:, j, :], mean[:], ALU.mult), [t])
                 for j in range(NT)]
            return [dve.do(lambda e, j=j: e.tensor_tensor(target[:, j, :], target[:, j, :], bias[:], ALU.add), [t[j], t_bias])
                    for j in range(NT)]

        def gather_sum(source, ready, finish):
            done = []
            for j in range(NT):
                b = j % 4
                for s in range(NT):
                    t = pe.do(lambda e, j=j, s=s, b=b: e.matmul(
                        bank(b, D, NP), counts[:, s, j * NP:(j + 1) * NP], source[:, s, :], start=s == 0, stop=s == NT - 1),
                        [ready[s], bank_free[b]], quiet=s < NT - 1)
                bank_free[b] = finish(j, bank(b, D, NP), t)
                done.append(bank_free[b])
            return done

        def dense(xT, weight, bias_row, ready, finish, tiles=None, banks=(4, 5, 6, 7)):
            done = []
            for j in (range(NT) if tiles is None else tiles):
                b = banks[j % len(banks)]
                for k in range(KD):
                    t = pe.do(lambda e, j=j, k=k, b=b: e.matmul(
                        bank(b, D, NP), xT[:, k, j * NP:(j + 1) * NP], weight[:, k, :], start=k == 0,
                        stop=bias_row is None and k == KD - 1), [ready[j], bank_free[b]],
                        quiet=bias_row is not None or k < KD - 1)
                if bias_row is not None:
                    t = pe.do(lambda e, b=b: e.matmul(bank(b, D, NP), ones[0:1, 0:NP], bias_row, start=False, stop=True))
                bank_free[b] = finish(j, bank(b, D, NP), t)
                done.append(bank_free[b])
            return done

        t = dve.do(lambda e: e.memset(ones[:], 1.0))
        t_mh = dve.do(lambda e: e.memset(minus_half[:], -0.5))
        t = pool.do(lambda e: e.memset(ident[:], 0.0))
        t_ident = pool.do(lambda e: e.affine_select(out=ident[:], in_=ident[:], compare_op=ALU.not_equal, fill=1.0,
                                                    base=0, pattern=[[-1, 128]], channel_multiplier=1), [t])
        t_x = dma("x", sp, X[:], x.rearrange("(j p) d -> p j d", p=NP))

        wr = Region(WORK, ARENA)
        no_edge = wr.take("no_edge", [NP, NT, N], BF16)
        AT0 = wr.at
        HC = NCHUNK // 2
        edges_i = wr.take("edges_i", [HC, 2, 2, NP], I32)
        edges_f = wr.take("edges_f", [HC, 2, 2, NP])
        edge_col = wr.take("edge_col", [NP, 2, 2, HC])
        iota_i = wr.take("iota_i", [NP, N], I32)
        iota_h = wr.take("iota_h", [NP, N], F16)
        RING = 8
        src_hot = [wr.take(f"src_hot{i}", [NP, N], BF16) for i in range(RING)]
        dst_hot = [wr.take(f"dst_hot{i}", [NP, 2 * NP], BF16) for i in range(RING)]
        count_rows = [wr.take(f"count_rows{i}", [NP, N]) for i in range(2)]
        for half in range(2):
            for w, a in enumerate((src, dst)):
                t_e = dma("edges", sp, edges_i[:, half, w, :], a.rearrange("(h c p) -> h c p", h=2, p=NP)[half])
        t = pool.do(lambda e: e.iota(iota_i[:], pattern=[[1, N]], base=0, channel_multiplier=0))
        t_iota = pool.do(lambda e: e.tensor_copy(iota_h[:], iota_i[:]), [t])
        t = dve.do(lambda e: e.tensor_copy(edges_f[:], edges_i[:]), [t_e])
        for half in range(2):
            for w in range(2):
                tt = pe.do(lambda e, half=half, w=w: e.transpose(
                    psum[0:NP, (2 * w + half) * HC:(2 * w + half + 1) * HC], edges_f[:, half, w, :], ident[0:HC, 0:HC]), [t, t_ident])
        t_col = dve.do(lambda e: e.tensor_copy(edge_col[:].rearrange("p w h c -> p (w h c)"), psum[0:NP, 0:4 * HC]), [tt])
        bank_free[0] = t_col

        def build_counts():
            n = 0
            used = [None] * RING
            rows_free = [None, None]
            for r in range(NT // 2):
                for c in range(NCHUNK):
                    slot = n % RING
                    t1 = dve.do(lambda e, c=c, s=slot: e.tensor_scalar(
                        src_hot[s][:], iota_h[:], edge_col[:, 0, c // HC, c % HC:c % HC + 1], None, ALU.is_equal),
                        [t_col, t_iota, used[slot]])
                    t1 = dve.do(lambda e, c=c, s=slot, r=r: e.tensor_scalar(
                        dst_hot[s][:], iota_h[:, r * 2 * NP:(r + 1) * 2 * NP], edge_col[:, 1, c // HC, c % HC:c % HC + 1], None, ALU.is_equal))
                    for i in range(2):
                        for q in range(3):
                            w = min(BANK, N - q * BANK)
                            t2 = pe.do(lambda e, s=slot, i=i, q=q, w=w, c=c: e.matmul(
                                psum[0:NP, (3 * i + q) * BANK:(3 * i + q) * BANK + w], dst_hot[s][:, i * NP:(i + 1) * NP],
                                src_hot[s][:, q * BANK:q * BANK + w], start=c == 0, stop=c == NCHUNK - 1),
                                [t1] + [bank_free[b] for b in range(6)], quiet=not (i == 1 and q == 2))
                    used[slot] = t2
                    n += 1
                for i in range(2):
                    j = 2 * r + i
                    rows, ps = count_rows[i], psum[0:NP, 3 * i * BANK:3 * i * BANK + N]
                    t3 = act.do(lambda e, j=j, rows=rows, ps=ps: e.activation(rows[:], ps, ACT.Identity, accum_out=deg[:, j:j + 1]), [t2, rows_free[i]])
                    t4 = dve.do(lambda e, j=j, rows=rows: e.tensor_scalar(no_edge[:, j, :], rows[:], 0.0, MASKED, ALU.is_equal, ALU.mult), [t3])
                    for b in range(3 * i, 3 * i + 3):
                        bank_free[b] = t3
                    for s0 in range(0, NT, 4):
                        b = 6 + (s0 // 4) % 2
                        m = min(4, NT - s0)
                        view = bank(b, m * 128, NP).rearrange("p (k c) -> p k c", c=128)[:, :, 0:NP]
                        for k in range(m):
                            t5 = pe.do(lambda e, k=k, s0=s0, view=view, rows=rows: e.transpose(
                                view[:, k, :], rows[:, (s0 + k) * NP:(s0 + k + 1) * NP], ident[0:NP, 0:NP]), [t3, bank_free[b]])
                        bank_free[b] = act.do(lambda e, j=j, s0=s0, m=m, view=view: e.copy(
                            counts[:, s0:s0 + m, j * NP:(j + 1) * NP], view), [t5])
                    rows_free[i] = t5
                    act.wait([t4])

        build_counts()
        fence()
        if stop_after == "counts":
            t = dve.do(lambda e: e.tensor_copy(X[:], counts[:, :, 0:D]), [t_x])
            return finish_program(nc, ctx, out, X, dma, (pe, dve, act, pool, sp), [t], NP)

        wr = Region(AT0, ARENA)
        H = wr.take("H", [NP, NT, D])
        WA = wr.take("WA", [128, KD, D])
        WB = wr.take("WB", [128, KD, D])
        STAGE0 = wr.at

        def attention_layer0():
            g = Region(STAGE0, ARENA)
            M = L0["proj"].shape[0]
            DH = L0["proj"].shape[1]
            HEADS = D // DH
            RT = 2
            ROWS = RT * 128
            h_in = g.take("h_in", [128, RT, D])
            hT = g.take("hT", [128, KD, ROWS])
            nat = {c: g.take(c + "_nat", [128, RT, D]) for c in "qkv"}
            tT = {c: g.take(c + "_T", [128, KD, ROWS]) for c in "qk"}
            squares = g.take("squares", [128, RT, D])
            half_norm = {c: g.take(c + "_halfnorm", [128, RT, HEADS]) for c in "qk"}
            proj_in = g.take("proj_in", [128, M // 128, DH])
            projT = g.take("projT", [128, M])
            umax = {c: g.take(c + "_umax", [128, RT, HEADS]) for c in "qk"}
            shift = {c: g.take(c + "_shift", [128, RT, HEADS]) for c in "qk"}
            row_max = g.take("row_max", [HEADS, 1])
            both = g.take("both_max", [128, HEADS])
            diag = g.take("diag", [HEADS, HEADS])
            feat = {c: [g.take(f"{c}_feat{i}", [128, RT, M]) for i in range(2)] for c in "qk"}
            qfT = [g.take(f"qfT{i}", [128, M // 128, ROWS]) for i in range(2)]
            v1 = g.take("v_and_one", [128, RT, HEADS, DH + 1])
            kv = [g.take(f"kv{i}", [128, M // 128, DH + 1]) for i in range(2)]
            z = g.take("z", [128, RT])
            o_nat = g.take("o_nat", [128, RT, D])
            TILES = 4
            oT = g.take("oT", [128, KD, TILES * NP])
            t_h = dma("h_in", sp, h_in[:], x[0:ROWS].rearrange("(r p) d -> p r d", p=128))
            t_pj = dma("proj", sp, proj_in[:], L0["proj"].rearrange("(r p) d -> p r d", p=128))
            for r in range(RT):
                b = r
                for k in range(KD):
                    t = pe.do(lambda e, r=r, k=k, b=b: e.transpose(bank(b)[:, k * 128:(k + 1) * 128],
                                                               h_in[:, r, k * 128:(k + 1) * 128], ident[:]), [t_h, bank_free[b]])
                th = act.do(lambda e, r=r, b=b: e.copy(hT[:, :, r * 128:(r + 1) * 128], bank(b).rearrange("p (k c) -> p k c", k=KD)), [t])
                bank_free[b] = th
            for m in range(M // 128):
                t = pe.do(lambda e, m=m: e.transpose(psum[0:DH, 2 * BANK + m * 128:2 * BANK + (m + 1) * 128], proj_in[:, m, :], ident[:]), [t_pj, bank_free[2]])
            act.do(lambda e: e.copy(projT[0:DH, :], psum[0:DH, 2 * BANK:2 * BANK + M]), [t])
            t_proj = bank_free[2] = act.do(lambda e: e.copy(projT[DH:2 * DH, :], psum[0:DH, 2 * BANK:2 * BANK + M]), [t])
            scale = DH ** -0.25
            free_w = [None, None]
            ready = {}
            for i, (c, name) in enumerate((("q", "Wq"), ("k", "Wk"), ("v", "Wv"))):
                W = (WA, WB)[i % 2]
                tw = dma(("wa", "wb")[i % 2], sp, W[:], L0[name].rearrange("(k p) n -> p k n", p=128), [free_w[i % 2]])
                for r in range(RT):
                    b = 4 + r
                    for k in range(KD):
                        t = pe.do(lambda e, r=r, k=k, b=b, W=W: e.matmul(bank(b), hT[:, k, r * 128:(r + 1) * 128], W[:, k, :],
                                                                     start=k == 0, stop=k == KD - 1), [th, tw, bank_free[b]])
                    s = scale if c != "v" else 1.0
                    ready[c] = bank_free[b] = act.do(lambda e, r=r, b=b, c=c, s=s: e.mul(nat[c][:, r, :], bank(b), s), [t])
                free_w[i % 2] = t
            for c in "qk":
                t = dve.do(lambda e, c=c: e.tensor_tensor(squares[:], nat[c][:], nat[c][:], ALU.mult), [ready[c], dve.last()])
                t = dve.do(lambda e, c=c: e.tensor_reduce(half_norm[c][:], squares[:].rearrange("p r (h d) -> p r h d", h=HEADS), AX.X, ALU.add), [t])
                for r in range(RT):
                    b = r
                    for k in range(KD):
                        t = pe.do(lambda e, r=r, k=k, b=b, c=c: e.transpose(bank(b)[:, k * 128:(k + 1) * 128],
                                                                        nat[c][:, r, k * 128:(k + 1) * 128], ident[:]), [ready[c], bank_free[b]])
                    ready[c + "T"] = bank_free[b] = act.do(lambda e, r=r, b=b, c=c: e.copy(
                        tT[c][:, :, r * 128:(r + 1) * 128], bank(b).rearrange("p (k c) -> p k c", k=KD)), [t])
            dve.do(lambda e: e.memset(v1[:], 1.0))
            t_v1 = dve.do(lambda e: e.tensor_copy(v1[:, :, :, 0:DH], nat["v"][:].rearrange("p r (h d) -> p r h d", h=HEADS)), [ready["v"], dve.last()])

            def scores(c, h, b):
                k, p0 = h // 2, DH * (h % 2)
                for r in range(RT):
                    t = pe.do(lambda e, r=r: e.matmul(bank(b)[:, r * M:(r + 1) * M], tT[c][p0:p0 + DH, k, r * 128:(r + 1) * 128],
                                                      projT[p0:p0 + DH, :], start=r == 0, stop=r == RT - 1, skip_group_check=True),
                              [ready[c + "T"], t_proj, bank_free[b]])
                return t
            for h in range(HEADS):
                b = h % 2
                t = scores("k", h, b)
                t_um = bank_free[b] = dve.do(lambda e, h=h, b=b: e.tensor_reduce(
                    umax["k"][:, :, h], bank(b).rearrange("p (r m) -> p r m", r=RT), AX.X, ALU.max), [t])
            t = dve.do(lambda e: e.tensor_tensor(both[:], umax["k"][:, 0, :], umax["k"][:, 1, :], ALU.max), [t_um])
            t = pe.do(lambda e: e.transpose(psum[0:HEADS, 3 * BANK:3 * BANK + 128], both[:], ident[:]), [t, bank_free[3]])
            t = dve.do(lambda e: e.tensor_reduce(row_max[:], psum[0:HEADS, 3 * BANK:3 * BANK + 128], AX.X, ALU.max), [t])
            t = dve.do(lambda e: e.tensor_scalar(diag[:], ident[0:HEADS, 0:HEADS], row_max[:, 0:1], None, ALU.mult), [t])
            t = pe.do(lambda e: e.matmul(psum[:, 3 * BANK:3 * BANK + HEADS], ones[0:HEADS, :], diag[:], start=True, stop=True), [t])
            for r in range(RT):
                t_sk = dve.do(lambda e, r=r: e.scalar_tensor_tensor(shift["k"][:, r, :], half_norm["k"][:, r, :], -0.5,
                                                                psum[:, 3 * BANK:3 * BANK + HEADS], ALU.mult, ALU.subtract), [t])
            bank_free[3] = t_sk
            inv = 1.0 / math.sqrt(M)
            for h in range(HEADS):
                i = h % 2
                for c in "kq":
                    b = 0 if c == "k" else 1
                    t = scores(c, h, b)
                    ready_shift = t_sk
                    if c == "q":
                        t2 = dve.do(lambda e, h=h, b=b: e.tensor_reduce(
                            umax["q"][:, :, h], bank(b).rearrange("p (r m) -> p r m", r=RT), AX.X, ALU.max), [t])
                        ready_shift = dve.do(lambda e, h=h: e.scalar_tensor_tensor(
                            shift["q"][:, :, h], half_norm["q"][:, :, h], -0.5, umax["q"][:, :, h], ALU.mult, ALU.subtract), [t2])
                    for r in range(RT):
                        t3 = act.do(lambda e, h=h, r=r, b=b, c=c, i=i: e.activation(
                            feat[c][i][:, r, :], bank(b)[:, r * M:(r + 1) * M], ACT.Exp, bias=shift[c][:, r, h:h + 1]),
                            [t, ready_shift, pe.last() if r == 0 else None])
                    bank_free[b] = t3
                    t4 = dve.do(lambda e, c=c, i=i: e.tensor_scalar(feat[c][i][:], feat[c][i][:], inv, KEPS, ALU.mult, ALU.add), [t3])
                    if c == "k":
                        for m in range(M // 128):
                            for r in range(RT):
                                t5 = pe.do(lambda e, h=h, m=m, r=r, i=i: e.matmul(
                                    psum[:, (2 + m) * BANK:(2 + m) * BANK + DH + 1], feat["k"][i][:, r, m * 128:(m + 1) * 128], v1[:, r, h, :],
                                    start=r == 0, stop=r == RT - 1), [t4, t_v1, bank_free[2 + m]])
                            t_kv = bank_free[2 + m] = dve.do(lambda e, m=m, i=i: e.tensor_copy(
                                kv[i][:, m, :], psum[:, (2 + m) * BANK:(2 + m) * BANK + DH + 1]), [t5])
                    else:
                        for m in range(M // 128):
                            for r in range(RT):
                                t5 = pe.do(lambda e, m=m, r=r, i=i: e.transpose(
                                    psum[:, 4 * BANK + (m * RT + r) * 128:4 * BANK + (m * RT + r + 1) * 128], feat["q"][i][:, r, m * 128:(m + 1) * 128], ident[:]),
                                    [t4, bank_free[4]])
                        t_qf = bank_free[4] = act.do(lambda e, i=i: e.copy(qfT[i][:].rearrange("p m n -> p (m n)"), bank(4)), [t5])
                for r in range(RT):
                    b = 5 + r
                    for m in range(M // 128):
                        t6 = pe.do(lambda e, r=r, m=m, i=i, b=b: e.matmul(
                            psum[:, b * BANK:b * BANK + DH + 1], qfT[i][:, m, r * 128:(r + 1) * 128], kv[i][:, m, :], start=m == 0, stop=m == M // 128 - 1),
                            [t_qf, t_kv, bank_free[b]])
                    t7 = dve.do(lambda e, r=r, b=b: e.tensor_scalar(z[:, r:r + 1], psum[:, b * BANK + DH:b * BANK + DH + 1], KEPS, None, ALU.add), [t6])
                    t7 = dve.do(lambda e, r=r: e.reciprocal(z[:, r:r + 1], z[:, r:r + 1]), [t7])
                    t_o = bank_free[b] = dve.do(lambda e, r=r, b=b, h=h: e.tensor_scalar(
                        o_nat[:, r, h * DH:(h + 1) * DH], psum[:, b * BANK:b * BANK + DH], z[:, r:r + 1], None, ALU.mult), [t7])
            for r in range(RT):
                b = r
                for k in range(KD):
                    t = pe.do(lambda e, r=r, k=k, b=b: e.transpose(bank(b)[:, k * 128:(k + 1) * 128], o_nat[:, r, k * 128:(k + 1) * 128], ident[:]), [t_o, bank_free[b]])
                t_oT = bank_free[b] = act.do(lambda e, r=r, b=b: e.copy(oT[:, :, r * 128:(r + 1) * 128], bank(b).rearrange("p (k c) -> p k c", k=KD)), [t])
            t_oT = dve.do(lambda e: e.tensor_copy(oT[:, :, ROWS:], oT[:, :, ROWS - 1:ROWS].to_broadcast([128, KD, TILES * NP - ROWS])), [t_oT])
            tw = dma("wb", sp, WB[:], L0["Wo"].rearrange("(k p) n -> p k n", p=128), [free_w[1]])

            def finish(j, ps, t):
                for jj in ([j] if j < TILES - 1 else range(TILES - 1, NT)):
                    t2 = dve.do(lambda e, jj=jj: e.tensor_tensor(H[:, jj, :], ps, X[:, jj, :], ALU.add), [t, t_x])
                return t2
            pe.wait([tw])
            done = dense(oT, WB, None, [t_oT] * TILES, finish, tiles=range(TILES))
            return done[-1]

        t_attn = attention_layer0()
        fence()
        if stop_after == "attn0":
            t = dve.do(lambda e: e.tensor_copy(X[:], H[:]), [t_attn])
            return finish_program(nc, ctx, out, X, dma, (pe, dve, act, pool, sp), [t], NP)

        def layer0():
            g = Region(STAGE0, ARENA)
            A = g.take("A", [NP, NT, D])
            T = g.take("T", [128, KD, N])
            inv_deg = g.take("inv_deg", [NP, NT])
            b_conv = g.take("b_conv", [1, D])
            tw = dma("wa", sp, WA[:], L0["W_conv"].rearrange("(k p) n -> p k n", p=128))
            tb = dma("b_conv", sp, b_conv[:], L0["b_conv"].rearrange("(a n) -> a n", a=1))
            save = g.at
            xn_ready = batch_norm(X, A, L0["norm1_g"], L0["norm1_b"], g, "bn1", [None] * NT)
            t = dve.do(lambda e: e.tensor_scalar(inv_deg[:], deg[:], 1.0, None, ALU.max))
            t_inv = dve.do(lambda e: e.reciprocal(inv_deg[:], inv_deg[:]), [t])
            AGG = nc.alloc_sbuf_tensor_at("AGG", [NP, NT, D], F32, offset=base + save)
            act.wait([xn_ready[-1]])
            agg_ready = gather_sum(A, xn_ready, lambda j, ps, t: act.do(
                lambda e: e.activation(AGG[:, j, :], ps, ACT.Identity, scale=inv_deg[:, j:j + 1]), [t, t_inv]))
            t_T = transpose_nodes(AGG, lambda j, v, t: [copy_out(j, T[:, :, j * NP:(j + 1) * NP], v, [t])], agg_ready)
            pe.wait([tw, tb])

            def add_conv(j, ps, t):
                return dve.do(lambda e: e.scalar_tensor_tensor(H[:, j, :], ps, 0.0, H[:, j, :], ALU.max, ALU.add), [t])
            h_ready = dense(T, WA, b_conv[0:1, :], t_T, add_conv)
            fence()
            g = Region(STAGE0, ARENA)
            A = g.take("A2", [NP, NT, D])
            bn_ready = batch_norm(H, A, L0["norm2_g"], L0["norm2_b"], g, "bn2", h_ready)
            x_ready = [dve.do(lambda e, j=j: e.tensor_tensor(X[:, j, :], X[:, j, :], A[:, j, :], ALU.add), [bn_ready[j]]) for j in range(NT)]
            x_ready = layer_norm(x_ready)
            fence()
            return x_ready

        x_ready = layer0()
        if stop_after == "L0":
            return finish_program(nc, ctx, out, X, dma, (pe, dve, act, pool, sp), x_ready, NP)

        def layer1(x_ready):
            HEADS1, _, DH1 = L1["Ws"].shape
            g = Region(AT0, ARENA)
            H = nc.alloc_sbuf_tensor_at("H1", [NP, NT, D], F32, offset=base + g.at)
            g.at += 4 * NT * D
            WH = g.take("WH", [NP, NT, HEADS1, DH1 + 1])
            SHIFT0 = g.at
            T = g.take("T1", [128, KD, N])
            W1 = g.take("W1", [128, KD, D])
            Wb = g.take("Wb1", [1, D])
            aw = g.take("aw", [NP, HEADS1, 2 * DH1])
            ab = g.take("ab", [NP, HEADS1])
            prod = [g.take(f"prod{i}", [NP, HEADS1, DH1]) for i in range(2)]
            tgt = g.take("tgt_score", [NP, NT, HEADS1])
            srcs = g.take("src_score", [NP, NT, HEADS1])
            srcs02 = g.take("src_score02", [NP, NT, HEADS1])
            nb_max = g.take("nb_max", [NP, NT, HEADS1])
            leak = g.take("leak", [NP, NT, HEADS1])
            rowT = {n: g.take("rowT_" + n, [HEADS1, N]) for n in ("src", "pos", "neg")}
            pick = g.take("pick", [HEADS1, HEADS1, 128])
            trash = g.take("trash", [NP, N], BF16)
            t_w = []
            for k in range(KD):
                t_w = dma("wa", sp, W1[:, k, :].rearrange("p (h d) -> p h d", h=HEADS1), L1["Ws"][:, k * 128:(k + 1) * 128, :].rearrange("h p d -> p h d"))
            t_wb = dma("b_conv", sp, Wb[:], L1["Wb"].rearrange("(a h) d -> a (h d)", a=1))
            t_aw = dma("aw", sp, aw[:], row_on_partitions(L1["a_w"]))
            t_ab = dma("aw", sp, ab[:], row_on_partitions(L1["a_b"]))
            t_pick = pool.do(lambda e: e.tensor_copy(pick[:], ident[0:HEADS1, 0:HEADS1].unsqueeze(2).to_broadcast([HEADS1, HEADS1, 128])))
            t_T = transpose_nodes(X, lambda j, v, t: [copy_out(j, T[:, :, j * NP:(j + 1) * NP], v, [t])], x_ready)
            t_one = pool.do(lambda e: e.memset(WH[:, :, :, DH1:DH1 + 1], 1.0))
            pe.wait([t_w, t_wb])
            wh_ready = dense(T, W1, Wb[0:1, :], t_T, lambda j, ps, t: copy_out(
                j, WH[:, j, :, 0:DH1], ps.rearrange("p (h d) -> p h d", h=HEADS1), [t]))
            for j in range(NT):
                for i, target in ((0, tgt), (1, srcs)):
                    t = dve.do(lambda e, j=j, i=i: e.tensor_tensor(prod[i][:], WH[:, j, :, 0:DH1], aw[:, :, i * DH1:(i + 1) * DH1], ALU.mult),
                               [wh_ready[j], t_ab, t_one, dve.last()])
                    t = dve.do(lambda e, j=j, i=i, target=target: e.tensor_reduce(target[:, j, :], prod[i][:], AX.X, ALU.add), [t])
                t_tgt = dve.do(lambda e, j=j: e.tensor_tensor(tgt[:, j, :], tgt[:, j, :], ab[:], ALU.add), [dve.last()])
            t_src02 = pool.do(lambda e: e.tensor_scalar(srcs02[:], srcs[:], 0.2, None, ALU.mult), [t_tgt])

            def to_rows(source, row, ready):
                view = psum[0:HEADS1, 0:NT * 128].rearrange("p (j c) -> p j c", c=128)
                for j in range(NT):
                    t = pe.do(lambda e, j=j: e.transpose(view[:, j, 0:NP], source[:, j, :], ident[0:NP, 0:NP]),
                              [ready, bank_free[0], bank_free[1], bank_free[2]])
                t = act.do(lambda e: e.copy(row[:].rearrange("p (j c) -> p j c", c=NP), view[:, :, 0:NP]), [t])
                bank_free[0] = bank_free[1] = bank_free[2] = t
                return t

            def spread_row(row, h, b0, ready):
                for q in range(3):
                    w = min(BANK, N - q * BANK)
                    t = pe.do(lambda e, q=q, w=w: e.matmul(psum[0:NP, (b0 + q) * BANK:(b0 + q) * BANK + w], pick[:, h, 0:NP],
                                                          row[:, q * BANK:q * BANK + w], start=True, stop=True),
                              [ready, t_pick] + bank_free[b0:b0 + 3])
                return t

            def spread_view(b0):
                return psum[0:NP, b0 * BANK:b0 * BANK + N]
            t_rows = to_rows(srcs, rowT["src"], t_tgt)
            for h in range(HEADS1):
                b0 = 3 * (h % 2)
                t = spread_row(rowT["src"], h, b0, t_rows)
                for j in range(NT):
                    t2 = dve.do(lambda e, h=h, j=j, b0=b0: e.tensor_tensor_reduce(
                        trash[:], spread_view(b0), no_edge[:, j, :], 1.0, 3 * MASKED, ALU.add, ALU.max, nb_max[:, j, h:h + 1]), [t, dve.last()])
                bank_free[b0] = bank_free[b0 + 1] = bank_free[b0 + 2] = t2
            t = dve.do(lambda e: e.tensor_tensor(nb_max[:], nb_max[:], tgt[:], ALU.add), [t2])
            t = dve.do(lambda e: e.scalar_tensor_tensor(nb_max[:], nb_max[:], 0.2, nb_max[:], ALU.mult, ALU.max), [t])
            t_neg = dve.do(lambda e: e.scalar_tensor_tensor(leak[:], tgt[:], 0.2, nb_max[:], ALU.mult, ALU.subtract), [t])
            t_pos = dve.do(lambda e: e.tensor_tensor(nb_max[:], tgt[:], nb_max[:], ALU.subtract), [t_neg])
            t_pos = to_rows(nb_max, rowT["pos"], t_pos)
            t_neg = to_rows(leak, rowT["neg"], t_neg)
            fence()
            s = Region(WORK, AT0)
            pos_row = [s.take(f"pos_row{i}", [NP, N]) for i in range(2)]
            neg_row = [s.take(f"neg_row{i}", [NP, N]) for i in range(2)]
            s = Region(SHIFT0, SHIFT0 + 4 * KD * N + 4 * KD * D)
            low = [s.take(f"low{i}", [NP, N]) for i in range(2)]
            weight = [s.take(f"weight{i}", [NP, N]) for i in range(3)]
            recip = g.take("recip1", [NP, NT])
            PER_BANK = BANK // (DH1 + 1)
            low_free, weight_free = [None] * 2, [None] * 3
            row_free = [None, None]
            out_free = None
            n = 0
            for h in range(HEADS1):
                i = h % 2
                t = spread_row(rowT["pos"], h, 0, t_pos)
                t_a = act.do(lambda e, i=i: e.copy(pos_row[i][:], spread_view(0)), [t, row_free[i]])
                bank_free[0:3] = [t_a] * 3
                t = spread_row(rowT["neg"], h, 3, t_neg)
                t_b = act.do(lambda e, i=i: e.copy(neg_row[i][:], spread_view(3)), [t])
                bank_free[3:6] = [t_b] * 3
                for s_ in range(NT):
                    lo, wt = low[n % 2], weight[n % 3]
                    t = pool.do(lambda e, lo=lo, i=i, s_=s_, h=h: e.tensor_scalar(lo[:], neg_row[i][:], srcs02[:, s_, h:h + 1], None, ALU.add), [t_b, low_free[n % 2]])
                    t = dve.do(lambda e, lo=lo, wt=wt, i=i, s_=s_, h=h: e.scalar_tensor_tensor(
                        wt[:], pos_row[i][:], srcs[:, s_, h:h + 1], lo[:], ALU.add, ALU.max), [t, t_a, weight_free[n % 3]])
                    low_free[n % 2] = t
                    row_free[i] = t
                    t = act.do(lambda e, wt=wt: e.activation(wt[:], wt[:], ACT.Exp), [t])
                    t = dve.do(lambda e, wt=wt, s_=s_: e.scalar_tensor_tensor(wt[:], wt[:], 1.0, counts[:, s_, :], ALU.min, ALU.mult), [t])
                    for j in range(NT):
                        b, c = 6 + j // PER_BANK, (j % PER_BANK) * (DH1 + 1)
                        t2 = pe.do(lambda e, wt=wt, j=j, b=b, c=c, s_=s_, h=h: e.matmul(
                            psum[0:NP, b * BANK + c:b * BANK + c + DH1 + 1], wt[:, j * NP:(j + 1) * NP], WH[:, s_, h, :],
                            start=s_ == 0 and j % PER_BANK == 0, stop=s_ == NT - 1 and j in (PER_BANK - 1, NT - 1), skip_group_check=True),
                            [t, out_free if s_ == 0 else None])
                    weight_free[n % 3] = t2
                    n += 1
                for j0, j1 in ((0, PER_BANK), (PER_BANK, NT)):
                    b = 6 + j0 // PER_BANK
                    v = psum[0:NP, b * BANK:b * BANK + (j1 - j0) * (DH1 + 1)].rearrange("p (j c) -> p j c", c=DH1 + 1)
                    t = dve.do(lambda e, v=v, j0=j0, j1=j1: e.tensor_scalar(recip[:, j0:j1], v[:, :, DH1], 1e-30, None, ALU.max), [t2])
                    t = dve.do(lambda e, j0=j0, j1=j1: e.reciprocal(recip[:, j0:j1], recip[:, j0:j1]), [t])
                    out_free = dve.do(lambda e, v=v, j0=j0, j1=j1, h=h: e.tensor_tensor(
                        H[:, j0:j1, h * DH1:(h + 1) * DH1], v[:, :, 0:DH1], recip[:, j0:j1].unsqueeze(2).to_broadcast([NP, j1 - j0, DH1]), ALU.mult), [t])
            x_ready = [dve.do(lambda e, j=j: e.tensor_tensor(X[:, j, :], X[:, j, :], H[:, j, :], ALU.add), [out_free]) for j in range(NT)]
            x_ready = layer_norm(x_ready)
            fence()
            return x_ready

        x_ready = layer1(x_ready)
        if stop_after == "L1":
            return finish_program(nc, ctx, out, X, dma, (pe, dve, act, pool, sp), x_ready, NP)

        def layer2(x_ready):
            g = Region(WORK, ARENA)
            Y = g.take("Y2", [NP, NT, D])
            H = g.take("H2", [NP, NT, D])
            T = g.take("T2", [128, KD, N])
            W_in = g.take("W2_in", [128, KD, D])
            WT = g.take("W2_T", [128, KD, D])
            b2 = g.take("b2", [NP, D])
            dinv = g.take("dinv", [NP, NT])
            t_w = dma("wa", sp, W_in[:], L2["W"].rearrange("(m p) n -> p m n", p=128))
            t_b2 = dma("b_conv", sp, b2[:], row_on_partitions(L2["b"]))
            t = dve.do(lambda e: e.tensor_scalar(dinv[:], deg[:], 1.0, None, ALU.add))
            t_dinv = pool.do(lambda e: e.tensor_tensor(dinv[:], dinv[:], minus_half[0:NP, :], ALU.pow), [t])
            for k in range(KD):
                b = k
                for m in range(KD):
                    t = pe.do(lambda e, k=k, m=m, b=b: e.transpose(bank(b)[:, m * 128:(m + 1) * 128], W_in[:, m, k * 128:(k + 1) * 128], ident[:]), [t_w, bank_free[b]])
                t_WT = bank_free[b] = act.do(lambda e, k=k, b=b: e.copy(WT[:, k, :], bank(b)), [t])
            t_T = transpose_nodes(X, lambda j, v, t: [copy_out(j, T[:, :, j * NP:(j + 1) * NP], v, [t])], x_ready)
            pe.wait([t_WT])
            y_ready = dense(T, WT, None, t_T, lambda j, ps, t: act.do(
                lambda e: e.activation(Y[:, j, :], ps, ACT.Identity, scale=dinv[:, j:j + 1]), [t, t_dinv]))
            h_ready = [dve.do(lambda e, j=j: e.scalar_tensor_tensor(H[:, j, :], Y[:, j, :], dinv[:, j:j + 1], b2[:], ALU.mult, ALU.add),
                              [y_ready[j], t_b2]) for j in range(NT)]
            h_ready = gather_sum(Y, y_ready, lambda j, ps, t: dve.do(
                lambda e: e.scalar_tensor_tensor(H[:, j, :], ps, dinv[:, j:j + 1], H[:, j, :], ALU.mult, ALU.add), [t, h_ready[j]]))
            dve.wait([pe.last()])
            bn_ready = batch_norm(H, Y, L2["gamma"], L2["beta"], g, "bn3", h_ready)
            x_ready = []
            for j in range(NT):
                t = act.do(lambda e, j=j: e.activation(Y[:, j, :], Y[:, j, :], ACT.Gelu), [bn_ready[j]])
                t = dve.do(lambda e, j=j: e.scalar_tensor_tensor(X[:, j, :], X[:, j, :], 2.0, Y[:, j, :], ALU.mult, ALU.add), [t])
                x_ready.append(t)
            x_ready = layer_norm(x_ready)
            fence()
            return x_ready

        x_ready = layer2(x_ready)
        if stop_after == "L2":
            return finish_program(nc, ctx, out, X, dma, (pe, dve, act, pool, sp), x_ready, NP)

        def layer3(x_ready):
            BLOCKS, COND = L3["s1_w"].shape[0], L3["s1_w"].shape[1]
            HEADS = 4
            DH = D // HEADS
            SCALE = DH ** -0.5
            FREQS = L3["f_w1"].shape[0] // 2
            TWO_PI = 2 * math.pi
            x_in = nc.dram_tensor("x_in", [N, D], F32, kind="Internal").ap()
            tiles_of = lambda ap: ap.rearrange("(j p) d -> p j d", p=NP)
            t_save = dma("x_in", sp, tiles_of(x_in), X[:], x_ready)
            g = Region(WORK, ARENA)
            cond3 = g.take("cond3", [96, N], F32R)
            yT = [g.take(f"yT_{p}", [128, KD, N], F32R) for p in ("hi", "lo")]
            bias_out = g.take("bias_out", [NP, D])
            has_edge = g.take("has_edge", [NP, NT])
            shift = g.take("ln_shift", [NP, NT])
            bias_cols = g.take("bias_cols", [128, 4, BLOCKS, KD])
            PHASE = g.at

            def load_bias_columns():
                rows = Region(PHASE, ARENA).take("bias_rows", [4 * BLOCKS * KD, 128])
                for n, name in enumerate(("bq", "bk", "bv", "m_b1")):
                    t = dma("bias_rows", sp, rows[n * BLOCKS * KD:(n + 1) * BLOCKS * KD, :], L3[name].rearrange("i (k p) -> (i k) p", p=128))
                R = 4 * BLOCKS * KD
                t = pe.do(lambda e: e.transpose(psum[:, 7 * BANK:7 * BANK + R], rows[:], ident[0:R, 0:R]), [t, bank_free[7]])
                bank_free[7] = act.do(lambda e: e.copy(bias_cols[:].rearrange("p n i k -> p (n i k)"), psum[:, 7 * BANK:7 * BANK + R]), [t])
            load_bias_columns()
            fence()

            def split_lo(q, lo, exact, hi, after):
                return q.do(lambda e: e.tensor_tensor(lo, exact, hi.bitcast(F32), ALU.subtract), after)

            def condition():
                g = Region(PHASE, ARENA)
                R = 2 * FREQS
                angle = g.take("angle", [R, N])
                turns = g.take("turns", [R, N])
                freq_i = g.take("freq_i", [R, 1], I32)
                freq = g.take("freq", [R, 1])
                quarter = g.take("quarter", [R, 1])
                hidden = g.take("hidden", [COND, N])
                sig = g.take("sig", [COND, N])
                f_w1 = g.take("f_w1", [R, COND])
                f_b1 = g.take("f_b1", [COND, 1])
                f_w2x3 = g.take("f_w2x3", [COND, 96])
                f_b2x3 = g.take("f_b2x3", [96, 1])
                exact = g.take("cond_exact", [96, N])
                t_n = dma("noise", sp, angle[:], noise.rearrange("n o -> (n o)").partition_broadcast(R))
                dma("cond_w", sp, f_w1[:], L3["f_w1"])
                dma("cond_w", sp, f_b1[:], L3["f_b1"].rearrange("(p o) -> p o", o=1))
                t0 = dve.do(lambda e: e.memset(f_w2x3[:], 0.0))
                t0 = dve.do(lambda e: e.tensor_tensor(f_b2x3[:], ident[0:96, COND:COND + 1], ident[0:96, 32 + COND:33 + COND], ALU.add))
                t0 = dve.do(lambda e: e.tensor_tensor(f_b2x3[:], f_b2x3[:], ident[0:96, 64 + COND:65 + COND], ALU.add), [t0])
                for i in range(3):
                    dma("cond_w", sp, f_w2x3[:, 32 * i:32 * i + COND], L3["f_w2"], [t0])
                    t_w = dma("cond_w", sp, f_b2x3[32 * i:32 * i + COND, :], L3["f_b2"].rearrange("(p o) -> p o", o=1))
                pool.do(lambda e: e.iota(freq_i[0:FREQS, :], pattern=[[0, 1]], base=1, channel_multiplier=1))
                t = pool.do(lambda e: e.iota(freq_i[FREQS:R, :], pattern=[[0, 1]], base=1, channel_multiplier=1))
                dve.do(lambda e: e.memset(quarter[0:FREQS, :], 0.0))
                t_q = dve.do(lambda e: e.memset(quarter[FREQS:R, :], 0.25))
                t = dve.do(lambda e: e.tensor_copy(freq[:], freq_i[:]), [t])
                t = dve.do(lambda e: e.tensor_scalar(freq[:], freq[:], TWO_PI / 16, None, ALU.mult), [t])
                t = dve.do(lambda e: e.tensor_scalar(angle[:], angle[:], freq[:, 0:1], None, ALU.mult), [t, t_n])
                t = dve.do(lambda e: e.tensor_scalar(turns[:], angle[:], 1 / TWO_PI, quarter[:, 0:1], ALU.mult, ALU.add), [t, t_q])
                ROUND = 1.5 * 2 ** 23
                t = dve.do(lambda e: e.tensor_scalar(turns[:], turns[:], ROUND, None, ALU.add), [t])
                t = dve.do(lambda e: e.tensor_scalar(turns[:], turns[:], ROUND, None, ALU.subtract), [t])
                part1 = 6.28125
                part2 = math.ldexp(round(math.ldexp(TWO_PI - part1, 21)), -21)
                part3 = TWO_PI - part1 - part2
                for part in (part1, part2, part3):
                    t = dve.do(lambda e, part=part: e.scalar_tensor_tensor(angle[:], turns[:], -part, angle[:], ALU.mult, ALU.add), [t])
                t = dve.do(lambda e: e.tensor_scalar(quarter[:], quarter[:], TWO_PI, None, ALU.mult), [t])
                t = dve.do(lambda e: e.tensor_scalar(angle[:], angle[:], quarter[:, 0:1], None, ALU.add), [t])
                PI = 3.1415925
                t = dve.do(lambda e: e.tensor_scalar(angle[:], angle[:], PI, -PI, ALU.min, ALU.max), [t])
                t = act.do(lambda e: e.activation(angle[:], angle[:], ACT.Sin), [t])

                def product(rows, lhsT, rhs, b0, after):
                    for q in range(3):
                        w = min(BANK, N - q * BANK)
                        t = pe.do(lambda e, q=q, w=w: e.matmul(psum[0:rows, (b0 + q) * BANK:(b0 + q) * BANK + w], lhsT,
                                                          rhs[:, q * BANK:q * BANK + w], start=True, stop=True), after)
                    return psum[0:rows, b0 * BANK:b0 * BANK + N], t
                ps, t = product(COND, f_w1[:], angle, 0, [t, t_w])
                t1 = act.do(lambda e: e.activation(hidden[:], ps, ACT.Identity, bias=f_b1[:, 0:1]), [t])
                t = act.do(lambda e: e.activation(sig[:], hidden[:], ACT.Exp, scale=-1.0), [t1])
                t = dve.do(lambda e: e.tensor_scalar(sig[:], sig[:], 1.0, None, ALU.add), [t])
                t = dve.do(lambda e: e.reciprocal(sig[:], sig[:]), [t])
                t = dve.do(lambda e: e.tensor_tensor(hidden[:], hidden[:], sig[:], ALU.mult), [t])
                ps2, t = product(96, f_w2x3[:], hidden, 3, [t])
                t = act.do(lambda e: e.activation(exact[:], ps2, ACT.Identity, bias=f_b2x3[:, 0:1]), [t])
                t = act.do(lambda e: e.copy(cond3[:], exact[:]), [t])
                return split_lo(dve, cond3[32:64, :], exact[32:64, :], cond3[32:64, :], [t])
            condition()
            fence()
            g = Region(PHASE, ARENA)
            absent = [g.take(f"absent{i}", [NP, N]) for i in range(2)]
            free = [None, None]
            for s in range(NT):
                a = absent[s % 2]
                t1 = dve.do(lambda e, s=s, a=a: e.tensor_scalar(a[:], counts[:, s, :], 0.0, MASKED, ALU.is_equal, ALU.mult), [free[s % 2]])
                t = dve.do(lambda e, s=s: e.tensor_reduce(has_edge[:, s:s + 1], counts[:, s, :], AX.X, ALU.max))
                t = dve.do(lambda e, s=s: e.tensor_scalar(counts[:, s, :], counts[:, s, :], 1.0, None, ALU.max), [t, t1])
                t = act.do(lambda e, s=s: e.activation(counts[:, s, :], counts[:, s, :], ACT.Ln), [t])
                free[s % 2] = dve.do(lambda e, s=s, a=a: e.scalar_tensor_tensor(counts[:, s, :], counts[:, s, :], 1 / SCALE, a[:], ALU.mult, ALU.add), [t])
            dve.do(lambda e: e.tensor_scalar(has_edge[:], has_edge[:], 1.0, None, ALU.min), [dve.last()])
            edge_term = counts

            def split_weight(name, stage, hi, lo, source, free):
                t = dma(name, sp, stage[:], source, [pool_done.get(name)])
                t = pool.do(lambda e: e.tensor_copy(hi[:], stage[:]), [t] + free)
                t = pool_done[name] = split_lo(pool, lo[:], stage[:], hi[:], [t])
                return t
            pool_done = {}

            def norm_stats(j, t):
                t = dve.do(lambda e: e.bn_stats(stats[:, j, :], X[:, j, :]), [t])
                return dve.do(lambda e: e.bn_aggr(mean_var[:, j, :], stats[:, j, :]), [t])

            def cond_norm(i, a, g, t_bias):
                stage = g.take(f"cw_in{i}{a}", [96, 2, D])
                w3 = g.take(f"cw3_{i}{a}", [96, 2, D], F32R)
                xn = [g.take(f"xn{i}{a}{n}", [NP, D]) for n in range(3)]
                t0 = pool.do(lambda e: e.memset(stage[:], 0.0))
                for n, c in enumerate("sb"):
                    for r in range(3):
                        dma("cw", sp, stage[32 * r:32 * r + COND, n, :], L3[f"{c}{a}_w"][i], [t0])
                        t = dma("cw", sp, stage[32 * r + COND:32 * r + COND + 1, n, :], L3[f"{c}{a}_b"][i:i + 1, :])
                t = act.do(lambda e: e.copy(w3[:], stage[:]), [t])
                t_w = split_lo(dve, w3[64:96, :, :], stage[64:96, :, :], w3[64:96, :, :], [t])
                t = dve.do(lambda e: e.tensor_scalar(rstd[:], mean_var[:, :, 1], EPS, None, ALU.add), [dve.last()])
                t = pool.do(lambda e: e.tensor_tensor(rstd[:], rstd[:], minus_half[0:NP, :], ALU.pow), [t])
                t = dve.do(lambda e: e.scalar_tensor_tensor(shift[:], mean_var[:, :, 0], -1.0, rstd[:], ALU.mult, ALU.mult), [t])
                xn_free = [None] * 3
                turned = {}

                def norm_tile(j):
                    x_, b0 = xn[j % 3], 2 * (j % 2)
                    t1 = act.do(lambda e: e.activation(x_[:], X[:, j, :], ACT.Identity, bias=shift[:, j:j + 1], scale=rstd[:, j:j + 1]), [t, xn_free[j % 3]])
                    for n in range(2):
                        t2 = pe.do(lambda e, n=n: e.matmul(bank(b0 + n, D, NP), cond3[:, j * NP:(j + 1) * NP], w3[:, n, :], start=True, stop=True), [t_w, bank_free[b0 + n]])
                    t3 = bank_free[b0] = dve.do(lambda e: e.scalar_tensor_tensor(x_[:], bank(b0, D, NP), 1.0, x_[:], ALU.add, ALU.mult), [t1, t2])
                    t4 = bank_free[b0 + 1] = dve.do(lambda e: e.tensor_tensor(x_[:], bank(b0 + 1, D, NP), x_[:], ALU.add), [t3])
                    b = 4 + j % 2
                    v = bank(b).rearrange("p (k c) -> p k c", k=KD)
                    for k in range(KD):
                        t5 = pe.do(lambda e, k=k: e.transpose(v[:, k, 0:NP], x_[:, k * 128:(k + 1) * 128], ident[0:NP, 0:NP]), [t4, bank_free[b]], quiet=k < KD - 1)
                    xn_free[j % 3] = turned[j] = t5

                def store_tile(j):
                    b, c = 4 + j % 2, slice(j * NP, (j + 1) * NP)
                    v = bank(b).rearrange("p (k c) -> p k c", k=KD)[:, :, 0:NP]
                    t6 = act.do(lambda e: e.copy(yT[0][:, :, c], v), [turned[j]])
                    bank_free[b] = split_lo(dve, yT[1][:, :, c], v, yT[0][:, :, c], [t6])
                for j in range(NT + 1):
                    if j < NT:
                        norm_tile(j)
                    if j:
                        store_tile(j - 1)
                for j in range(NT):
                    t_b = pool.do(lambda e, j=j: e.tensor_tensor(X[:, j, :], X[:, j, :], bias_out[:], ALU.add), [t_bias, act.last()])
                return bank_free[4 + (NT - 1) % 2], t_b

            def three_products(out_, lhs, rhs, first, last, after, quiet=False):
                for n, (a, b) in enumerate(((0, 0), (0, 1), (1, 0))):
                    t = pe.do(lambda e, a=a, b=b, n=n: e.matmul(out_, lhs[a], rhs[b], start=first and n == 0, stop=last and n == 2),
                              after, quiet=quiet or n < 2)
                return t

            def attention_block(i):
                fence()
                g = Region(PHASE, ARENA)
                PAIR = 2 * NP
                qk = {c: [g.take(f"{c}{i}_{p}", [128, N], F32R) for p in ("hi", "lo")] for c in "qk"}
                v2 = [g.take(f"v{i}_{p}", [NP, NT, DH], F32R) for p in ("hi", "lo")]
                oT = [g.take(f"oT{i}_{p}", [128, PAIR], F32R) for p in ("hi", "lo")]
                pT = [g.take(f"pT{i}_{p}", [NP, NT, PAIR], F32R) for p in ("hi", "lo")]
                prob = [g.take(f"prob{i}_{n}", [128, N]) for n in range(4)]
                w_in = g.take(f"w_in{i}", [128, KD, DH])
                w2 = [[g.take(f"w{i}_{n}_{p}", [128, KD, DH], F32R) for p in ("hi", "lo")] for n in range(2)]
                wo_in = g.take(f"wo_in{i}", [128, D])
                wo2 = [g.take(f"wo{i}_{p}", [128, D], F32R) for p in ("hi", "lo")]
                row_max = g.take(f"row_max{i}", [NP, NT])
                row_sum = g.take(f"row_sum{i}", [NP, NT])
                t_bo = dma("bias_out", sp, bias_out[:], row_on_partitions(L3["bo"][i]))
                w_ready, w_used, n_load = {}, [None, None], [0]

                def load_head(c, h):
                    n = n_load[0] % 2
                    n_load[0] += 1
                    t = split_weight("w_in", w_in, w2[n][0], w2[n][1],
                                     L3["w" + c][i].rearrange("(k p) n -> p k n", p=128)[:, :, h * DH:(h + 1) * DH], [w_used[n]])
                    w_ready[c, h] = (n, t)

                def load_wo(h, used):
                    w_ready["o", h] = split_weight("w_o", wo_in, wo2[0], wo2[1], L3["wo"][i][h * DH:(h + 1) * DH, :], [used])

                def project(c, h, b0, t_y, store):
                    buf, t_w = w_ready[c, h]
                    for q in range(3):
                        cols = slice(q * BANK, min((q + 1) * BANK, N))
                        ps = psum[:, (b0 + q) * BANK:(b0 + q) * BANK + cols.stop - cols.start]
                        for k in range(KD):
                            t = three_products(ps, [p[:, k, :] for p in w2[buf]], [p[:, k, cols] for p in yT], k == 0, k == KD - 1,
                                               [t_w, t_y, bank_free[b0 + q]])
                        bank_free[b0 + q] = store(cols, ps, t)
                    w_used[buf] = t

                def project_qk(c, h, b0, t_y):
                    bias = bias_cols[:, "qk".index(c), i, h:h + 1]

                    def store(cols, ps, t):
                        hi, lo = (p[:, cols] for p in qk[c])
                        t = act.do(lambda e: e.activation(hi, ps, ACT.Identity, bias=bias), [t])
                        return dve.do(lambda e: e.scalar_tensor_tensor(lo, ps, bias, hi.bitcast(F32), ALU.add, ALU.subtract), [t])
                    project(c, h, b0, t_y, store)
                    t_qk[c] = bank_free[b0 + 2]

                prob_free, n_prob = [None] * 4, [0]

                def next_prob():
                    n_prob[0] += 1
                    return (n_prob[0] - 1) % 4
                t_qk = {}
                load_head("q", 0)
                load_head("k", 0)
                load_wo(0, None)
                t_y, t_b = cond_norm(i, 1, Region(PHASE, PHASE + 20000), t_bo)
                project_qk("q", 0, 0, t_y)
                load_head("v", 0)
                project_qk("k", 0, 3, t_y)
                if HEADS > 1:
                    load_head("q", 1)

                def head(h):
                    t_q, t_k = t_qk["q"], t_qk["k"]
                    soft, turned = {}, {}
                    v_ready = []

                    def scores(n):
                        for q in range(3):
                            w = min(BANK, N - q * BANK)
                            t = three_products(psum[0:NP, q * BANK:q * BANK + w], [p[:, n * NP:(n + 1) * NP] for p in qk["q"]],
                                               [p[:, q * BANK:q * BANK + w] for p in qk["k"]], True, True, [t_q, t_k, bank_free[q]])
                        p = next_prob()
                        P, mx = prob[p][0:NP, :], row_max[:, n:n + 1]
                        t = dve.do(lambda e: e.tensor_tensor_reduce(P, psum[0:NP, 0:N], edge_term[:, n, :], 1.0, 3 * MASKED,
                                                                    ALU.add, ALU.max, mx), [t, prob_free[p]])
                        bank_free[0:3] = [t] * 3
                        t = dve.do(lambda e: e.tensor_scalar(mx, mx, -SCALE, None, ALU.mult), [t])
                        soft[n] = (p, t)

                    def exponentials(n):
                        p, t = soft[n]
                        P, mx, sm = prob[p][0:NP, :], row_max[:, n:n + 1], row_sum[:, n:n + 1]
                        t = act.do(lambda e: e.activation(P, P, ACT.Exp, bias=mx, scale=SCALE, accum_out=sm), [t])
                        soft[n] = (p, t)

                    def normalise(n):
                        p, t = soft[n]
                        P, sm = prob[p][0:NP, :], row_sum[:, n:n + 1]
                        t = dve.do(lambda e: e.reciprocal(sm, sm), [t])
                        t = dve.do(lambda e: e.tensor_tensor(sm, sm, has_edge[:, n:n + 1], ALU.mult), [t])
                        t = act.do(lambda e: e.activation(P, P, ACT.Identity, scale=sm), [t])
                        soft[n] = (p, t)

                    def turn(n):
                        p, t0 = soft[n]
                        turned[n] = []
                        for q in range(3):
                            m = min(4, NT - 4 * q)
                            b = 3 + q
                            v = bank(b, m * 128, NP).rearrange("p (k c) -> p k c", c=128)
                            for k in range(m):
                                d = 4 * q + k
                                t = pe.do(lambda e, k=k, d=d, v=v: e.transpose(v[:, k, 0:NP], prob[p][0:NP, d * NP:(d + 1) * NP], ident[0:NP, 0:NP]),
                                          [t0, bank_free[b]], quiet=k < m - 1)
                            half = slice((n % 2) * NP, (n % 2 + 1) * NP)
                            hi, lo = (x_[:, 4 * q:4 * q + m, half] for x_ in pT)
                            t1 = act.do(lambda e, v=v, hi=hi: e.copy(hi, v[:, :, 0:NP]), [t])
                            bank_free[b] = split_lo(dve, lo, v[:, :, 0:NP], hi, [t1])
                            turned[n].append(bank_free[b])
                        prob_free[p] = t

                    def mix(g):
                        for d in range(NT):
                            t = three_products(bank(6, PAIR), [v[:, d, :] for v in v2], [x_[:, d, :] for x_ in pT], d == 0, d == NT - 1,
                                               [turned[2 * g][d // 4], turned[2 * g + 1][d // 4], v_ready[d // 4], bank_free[6]])
                        t = act.do(lambda e: e.copy(oT[0][:], bank(6, PAIR)), [t])
                        bank_free[6] = split_lo(dve, oT[1][:], bank(6, PAIR), oT[0][:], [t])
                        return bank_free[6]

                    def output_product(g, t_o):
                        for n, b in ((2 * g, 7), (2 * g + 1, 6)):
                            half = slice((n % 2) * NP, (n % 2 + 1) * NP)
                            t = three_products(bank(b, D, NP), [p[:, half] for p in oT], [p[:] for p in wo2], True, True,
                                               [w_ready["o", h], t_o, bank_free[b]])
                            bank_free[b] = dve.do(lambda e, n=n, b=b: e.tensor_tensor(X[:, n, :], bank(b, D, NP), X[:, n, :], ALU.add), [t, t_b])
                            if h == HEADS - 1:
                                norm_stats(n, bank_free[b])
                        return t

                    def make_v():
                        p = next_prob()
                        vT = prob[p]
                        bias = bias_cols[:, 2, i, h:h + 1]
                        free = prob_free[p]
                        ready = {}

                        def store(cols, ps, t):
                            ready["t"] = act.do(lambda e: e.activation(vT[:, cols], ps, ACT.Identity, bias=bias), [t, free])
                            return ready["t"]
                        project("v", h, 0, t_y, store)
                        return p, ready["t"]

                    def turn_v(p, t0):
                        for q in range(3):
                            m, b = min(4, NT - 4 * q), 3 + q
                            v = bank(b, m * 128, NP).rearrange("p (k c) -> p k c", c=128)
                            for k in range(m):
                                d = 4 * q + k
                                t = pe.do(lambda e, k=k, d=d, v=v: e.transpose(v[:, k, :], prob[p][:, d * NP:(d + 1) * NP], ident[:]),
                                          [t0, bank_free[b]], quiet=k < m - 1)
                            hi, lo = (x_[:, 4 * q:4 * q + m, :] for x_ in v2)
                            t1 = act.do(lambda e, v=v, hi=hi: e.copy(hi, v), [t])
                            bank_free[b] = split_lo(dve, lo, v, hi, [t1])
                            v_ready.append(bank_free[b])
                        prob_free[p] = t
                    last = h + 1 == HEADS
                    v_at = make_v()
                    if not last:
                        load_head("k", h + 1)
                    scores(0)
                    exponentials(0)
                    turn_v(*v_at)
                    normalise(0)
                    scores(1)
                    exponentials(1)
                    PAIRS = NT // 2
                    for g in range(PAIRS):
                        more = 2 * g + 2 < NT
                        turn(2 * g)
                        normalise(2 * g + 1)
                        if g:
                            output_product(g - 1, t_o)
                        if more:
                            scores(2 * g + 2)
                        elif not last:
                            project_qk("q", h + 1, 0, t_y)
                            load_head("v", h + 1)
                        turn(2 * g + 1)
                        if more:
                            exponentials(2 * g + 2)
                            normalise(2 * g + 2)
                            scores(2 * g + 3)
                            exponentials(2 * g + 3)
                        elif not last:
                            project_qk("k", h + 1, 3, t_y)
                            if h + 2 < HEADS:
                                load_head("q", h + 2)
                        t_o = mix(g)
                    t = output_product(PAIRS - 1, t_o)
                    if not last:
                        load_wo(h + 1, t)
                for h in range(HEADS):
                    head(h)

            def mlp_block(i):
                fence()
                g = Region(PHASE, ARENA)
                hT = [g.take(f"hT{i}_{p}", [128, KD, N], F32R) for p in ("hi", "lo")]
                m_in = g.take(f"m_in{i}", [128, KD, D])
                m1 = [g.take(f"m1_{i}_{p}", [128, KD, D], F32R) for p in ("hi", "lo")]
                m2 = [g.take(f"m2_{i}_{p}", [128, KD, D], F32R) for p in ("hi", "lo")]
                relu = g.take(f"relu{i}", [128, N])
                t_b2 = dma("bias_out", sp, bias_out[:], row_on_partitions(L3["m_b2"][i]))
                t_m1 = split_weight("m_in", m_in, m1[0], m1[1], L3["m_w1"][i].rearrange("(k p) n -> p k n", p=128), [])
                t_y, t_b = cond_norm(i, 2, Region(PHASE, PHASE + 20000), t_b2)
                t_m2 = split_weight("m_in", m_in, m2[0], m2[1], L3["m_w2"][i].rearrange("(k p) n -> p k n", p=128), [])
                relu_free = None
                for m in range(KD):
                    b0 = 3 * (m % 2)
                    for q in range(3):
                        w = min(BANK, N - q * BANK)
                        for k in range(KD):
                            t = three_products(psum[:, (b0 + q) * BANK:(b0 + q) * BANK + w], [p[:, k, m * 128:(m + 1) * 128] for p in m1],
                                               [p[:, k, q * BANK:q * BANK + w] for p in yT], k == 0, k == KD - 1,
                                               [t_m1, t_y] + bank_free[b0:b0 + 3])
                    ps = psum[:, b0 * BANK:b0 * BANK + N]
                    t1 = act.do(lambda e, m=m, ps=ps: e.activation(relu[:], ps, ACT.Relu, bias=bias_cols[:, 3, i, m:m + 1]), [t, relu_free])
                    bank_free[b0:b0 + 3] = [t1] * 3
                    t2 = act.do(lambda e, m=m: e.copy(hT[0][:, m, :], relu[:]), [t1])
                    relu_free = split_lo(dve, hT[1][:, m, :], relu[:], hT[0][:, m, :], [t2])
                for j in range(NT):
                    b = 6 + j % 2
                    for k in range(KD):
                        t = three_products(bank(b, D, NP), [p[:, k, j * NP:(j + 1) * NP] for p in hT], [p[:, k, :] for p in m2],
                                           k == 0, k == KD - 1, [relu_free, t_m2, bank_free[b]])
                    bank_free[b] = dve.do(lambda e, j=j, b=b: e.tensor_tensor(X[:, j, :], bank(b, D, NP), X[:, j, :], ALU.add), [t, t_b])
                    norm_stats(j, bank_free[b])

            for j in range(NT):
                norm_stats(j, x_ready[j])
            for i in range(BLOCKS):
                attention_block(i)
                if stop_after == f"xa{i}":
                    return [dve.last()]
                mlp_block(i)
                if stop_after == f"xb{i}":
                    return [dve.last()]
            fence()
            before = Region(PHASE, ARENA).take("x_before", [NP, NT, D])
            t = dma("x_in", sp, before[:], tiles_of(x_in), [t_save])
            ready = [dve.do(lambda e, j=j: e.tensor_tensor(X[:, j, :], X[:, j, :], before[:, j, :], ALU.add), [t]) for j in range(NT)]
            return layer_norm(ready)

        x_ready = layer3(x_ready)
        finish_program(nc, ctx, out, X, dma, (pe, dve, act, pool, sp), x_ready, NP)


def finish_program(nc, ctx, out, X, dma, queues, ready, NP):
    pe, dve, act, pool, sp = queues
    t = dma("out", sp, out.rearrange("(j p) d -> p j d", p=NP), X[:], ready)
    sp.wait([t])
    block = ctx.enter_context(nc.Block())
    block.tensor(lambda e: pe.run(e))
    block.vector(lambda e: dve.run(e))
    block.scalar(lambda e: act.run(e))
    block.gpsimd(lambda e: pool.run(e))
    block.sync(lambda e: sp.run(e))


_INS = ['x', 'src', 'dst', 'node_vec1', 'L0_gnn_norm1_g', 'L0_gnn_norm1_b', 'L0_gnn_norm2_g', 'L0_gnn_norm2_b', 'L0_gnn_W_conv',
        'L0_gnn_b_conv', 'L0_gnn_Wq', 'L0_gnn_Wk', 'L0_gnn_Wv', 'L0_gnn_Wo', 'L0_gnn_proj', 'L1_gnn_Ws', 'L1_gnn_Wb', 'L1_gnn_a_w',
        'L1_gnn_a_b', 'L2_gnn_W', 'L2_gnn_b', 'L2_gnn_gamma', 'L2_gnn_beta', 'L3_gnn_f_w1', 'L3_gnn_f_b1', 'L3_gnn_f_w2',
        'L3_gnn_f_b2', 'L3_gnn_s1_w', 'L3_gnn_s1_b', 'L3_gnn_b1_w', 'L3_gnn_b1_b', 'L3_gnn_wq', 'L3_gnn_bq', 'L3_gnn_wk',
        'L3_gnn_bk', 'L3_gnn_wv', 'L3_gnn_bv', 'L3_gnn_wo', 'L3_gnn_bo', 'L3_gnn_s2_w', 'L3_gnn_s2_b', 'L3_gnn_b2_w',
        'L3_gnn_b2_b', 'L3_gnn_m_w1', 'L3_gnn_m_b1', 'L3_gnn_m_w2', 'L3_gnn_m_b2']


def build(nc, args, out, stop_after=None):
    layer = lambda p: {k[len(p):]: v for k, v in args.items() if k.startswith(p)}
    build_layers(nc, args["x"], args["src"], args["dst"], args["node_vec1"], layer("L0_gnn_"), layer("L1_gnn_"),
                 layer("L2_gnn_"), layer("L3_gnn_"), out, stop_after)


def kernel(**inputs):
    import numpy as _np
    import concourse.bacc as _bacc
    from concourse import mybir as _mybir
    from concourse.bass_utils import run_bass_kernel_spmd as _run

    nc = _bacc.Bacc("TRN2", target_bir_lowering=False, num_devices=1)
    arrays, args = {}, {}
    for name in _INS:
        a = _np.ascontiguousarray(inputs[name])
        arrays[f"in_{name}"] = a
        args[name] = nc.dram_tensor(f"in_{name}", a.shape, _mybir.dt.from_np(a.dtype), kind="ExternalInput").ap()
    out = nc.dram_tensor("out", inputs["x"].shape, _mybir.dt.float32, kind="ExternalOutput").ap()
    build(nc, args, out)
    return _run(nc, [arrays], core_ids=[0]).results[0]["out"]
```

```python
import math
from contextlib import ExitStack

import concourse.bass as bass
from concourse import mybir

ALU = mybir.AluOpType
ACT = mybir.ActivationFunctionType
AX = mybir.AxisListType
F32 = mybir.dt.float32
F32R = mybir.dt.float32r
BF16 = mybir.dt.bfloat16
F16 = mybir.dt.float16
I32 = mybir.dt.int32

BANK = 512
PE_ROWS = 128
EPS = 1e-5
KEPS = 1e-6
MASKED = -1e30


class Tick:
    def __init__(self, sem, value):
        self.sem, self.value = sem, value


class Queue:
    def __init__(self, sem):
        self.sem, self.count, self.steps, self.waited = sem, 0, [], {}

    def wait(self, after):
        for tick in after:
            if tick is not None and self.waited.get(id(tick.sem), 0) < tick.value:
                self.waited[id(tick.sem)] = tick.value
                self.steps.append(lambda e, t=tick: e.wait_ge(t.sem, t.value))

    def do(self, make, after=(), quiet=False):
        self.wait(after)
        if quiet:
            self.steps.append(make)
            return None
        self.count += 1
        self.steps.append(lambda e: make(e).then_inc(self.sem, 1))
        return Tick(self.sem, self.count)

    def last(self):
        return Tick(self.sem, self.count) if self.count else None

    def run(self, engine):
        for step in self.steps:
            step(engine)


class DmaSlot:
    def __init__(self, sem):
        self.sem, self.count = sem, 0

    def move(self, queue, out, in_, after=()):
        queue.wait(after)
        self.count += 16
        queue.steps.append(lambda e: e.dma_start(out, in_).then_inc(self.sem, 16))
        return Tick(self.sem, self.count)


def build_layers(nc, x, src, dst, noise, L0, L1, L2, L3, out, stop_after=None):
    N, D = x.shape
    E = src.shape[0]
    NP = 125
    NT = N // NP
    KD = D // PE_ROWS
    assert NP * NT == N and E % NP == 0 and KD * PE_ROWS == D
    NCHUNK = E // NP
    with ExitStack() as ctx:
        sem = lambda name: ctx.enter_context(nc.semaphore(name))
        pe, dve, act, pool, sp = (Queue(sem(n)) for n in ("pe_done", "dve_done", "act_done", "pool_done", "sp_done"))
        slots = {}

        def dma(name, queue, out_, in_, after=()):
            if name not in slots:
                slots[name] = DmaSlot(sem("dma_" + name))
            return slots[name].move(queue, out_, in_, after)

        ARENA = 212672
        ctx.enter_context(nc.sbuf_tensor("arena", [128, ARENA], mybir.dt.uint8))
        base = nc.sbuf_base - ARENA
        size = {F32: 4, F32R: 4, BF16: 2, F16: 2, I32: 4}

        class Region:
            def __init__(self, at, end):
                self.at, self.end = at, end

            def take(self, name, shape, dtype=F32):
                n = size[dtype]
                for s in shape[1:]:
                    n *= s
                t = nc.alloc_sbuf_tensor_at(name, shape, dtype, offset=base + self.at)
                self.at += (n + 31) // 32 * 32
                assert self.at <= self.end, (name, self.at, self.end)
                return t

        keep = Region(0, 76000)
        counts = keep.take("counts", [NP, NT, N])
        X = keep.take("X", [NP, NT, D])
        ident = keep.take("ident", [128, 128])
        ones = keep.take("ones", [128, 128])
        minus_half = keep.take("minus_half", [128, NT])
        deg = keep.take("deg", [NP, NT])
        stats = keep.take("stats", [NP, NT, 6])
        mean_var = keep.take("mean_var", [NP, NT, 2])
        rstd = keep.take("rstd", [NP, NT])
        WORK = keep.at
        psum = ctx.enter_context(nc.psum_tensor("psum", [128, 8 * BANK], F32))
        bank_free = [None] * 8

        def bank(b, n=BANK, rows=128):
            return psum[0:rows, b * BANK:b * BANK + n]

        def everything():
            return [q.last() for q in (pe, dve, act, pool)] + [Tick(s.sem, s.count) for s in slots.values()]

        def fence():
            done = everything()
            for q in (pe, dve, act, pool, sp):
                q.wait(done)

        def row_on_partitions(ap, n=NP):
            return ap.partition_broadcast(n)

        def transpose_nodes(source, store, ready, banks=(6, 7), width=NP):
            done = []
            for j in range(NT):
                b = banks[j % len(banks)]
                view = bank(b).rearrange("p (k c) -> p k c", k=KD)
                for k in range(KD):
                    t = pe.do(lambda e, j=j, k=k, v=view: e.transpose(
                        v[:, k, 0:width], source[0:width, j, k * 128:(k + 1) * 128], ident[0:width, 0:width]),
                        after=[ready[j], bank_free[b]], quiet=k < KD - 1)
                ticks = store(j, view[:, :, 0:width], t)
                bank_free[b] = ticks[-1]
                done.append(ticks[-1])
            return done

        def copy_out(i, out_, in_, after):
            if i % 2:
                return dve.do(lambda e: e.tensor_copy(out_, in_), after)
            return act.do(lambda e: e.copy(out_, in_), after)

        def layer_norm(ready):
            done = []
            for j in range(NT):
                t = dve.do(lambda e, j=j: e.bn_stats(stats[:, j, :], X[:, j, :]), [ready[j]])
            for j in range(NT):
                t = dve.do(lambda e, j=j: e.bn_aggr(mean_var[:, j, :], stats[:, j, :]), [dve.last()] if j == 0 else [])
            t = dve.do(lambda e: e.tensor_scalar(rstd[:], mean_var[:, :, 1], EPS, None, ALU.add), [t])
            t = pool.do(lambda e: e.tensor_tensor(rstd[:], rstd[:], minus_half[0:NP, :], ALU.pow), [t])
            for j in range(NT):
                done.append(dve.do(lambda e, j=j: e.tensor_scalar(
                    X[:, j, :], X[:, j, :], mean_var[:, j, 0:1], rstd[:, j:j + 1], ALU.subtract, ALU.mult), [t]))
            return done

        def batch_norm(source, target, gain_row, bias_row, region, tag, ready):
            gain = region.take(tag + "_gain", [NP, D])
            bias = region.take(tag + "_bias", [NP, D])
            mean = region.take(tag + "_mean", [NP, D])
            squares = [region.take(f"{tag}_square{i}", [NP, D]) for i in range(2)]
            root = region.take(tag + "_root", [NP, D])
            fix = region.take(tag + "_fix", [NP, D])
            t_gain = dma("gain", sp, gain[:], row_on_partitions(gain_row))
            t_bias = dma("bias", sp, bias[:], row_on_partitions(bias_row))
            for j in range(NT):
                t = pe.do(lambda e, j=j: e.matmul(bank(0, D, NP), ones[0:NP, 0:NP], source[:, j, :],
                                                  start=j == 0, stop=j == NT - 1), [ready[j], bank_free[0]])
            t_mean = act.do(lambda e: e.mul(mean[:], bank(0, D, NP), 1.0 / N), [t])
            squared = [None, None]
            for j in range(NT):
                centred = dve.do(lambda e, j=j: e.tensor_tensor(target[:, j, :], source[:, j, :], mean[:], ALU.subtract), [t_mean])
                sq = squares[j % 2]
                t = act.do(lambda e, j=j, sq=sq: e.square(sq[:], target[:, j, :]), [centred, squared[j % 2]])
                t = squared[j % 2] = pe.do(lambda e, j=j, sq=sq: e.matmul(
                    bank(1, D, NP), ones[0:NP, 0:NP], sq[:], start=j == 0, stop=j == NT - 1), [t, bank_free[1]])
            t = dve.do(lambda e: e.tensor_scalar(mean[:], bank(1, D, NP), 1.0 / N, EPS, ALU.mult, ALU.add), [t])
            bank_free[0] = t_mean
            bank_free[1] = t
            t = act.do(lambda e: e.sqrt(root[:], mean[:]), [t])
            t = dve.do(lambda e: e.reciprocal(root[:], root[:]), [t])
            t = dve.do(lambda e: e.tensor_tensor(fix[:], root[:], root[:], ALU.mult), [t])
            t = dve.do(lambda e: e.tensor_tensor(fix[:], fix[:], mean[:], ALU.mult), [t])
            t = dve.do(lambda e: e.tensor_scalar(fix[:], fix[:], -0.5, 1.5, ALU.mult, ALU.add), [t])
            t = dve.do(lambda e: e.tensor_tensor(root[:], root[:], fix[:], ALU.mult), [t])
            t = dve.do(lambda e: e.tensor_tensor(mean[:], root[:], gain[:], ALU.mult), [t, t_gain])
            t = [dve.do(lambda e, j=j: e.tensor_tensor(target[:, j, :], target[:, j, :], mean[:], ALU.mult), [t])
                 for j in range(NT)]
            return [dve.do(lambda e, j=j: e.tensor_tensor(target[:, j, :], target[:, j, :], bias[:], ALU.add), [t[j], t_bias])
                    for j in range(NT)]

        def gather_sum(source, ready, finish):
            done = []
            for j in range(NT):
                b = j % 4
                for s in range(NT):
                    t = pe.do(lambda e, j=j, s=s, b=b: e.matmul(
                        bank(b, D, NP), counts[:, s, j * NP:(j + 1) * NP], source[:, s, :], start=s == 0, stop=s == NT - 1),
                        [ready[s], bank_free[b]], quiet=s < NT - 1)
                bank_free[b] = finish(j, bank(b, D, NP), t)
                done.append(bank_free[b])
            return done

        def dense(xT, weight, bias_row, ready, finish, tiles=None, banks=(4, 5, 6, 7)):
            done = []
            for j in (range(NT) if tiles is None else tiles):
                b = banks[j % len(banks)]
                for k in range(KD):
                    t = pe.do(lambda e, j=j, k=k, b=b: e.matmul(
                        bank(b, D, NP), xT[:, k, j * NP:(j + 1) * NP], weight[:, k, :], start=k == 0,
                        stop=bias_row is None and k == KD - 1), [ready[j], bank_free[b]],
                        quiet=bias_row is not None or k < KD - 1)
                if bias_row is not None:
                    t = pe.do(lambda e, b=b: e.matmul(bank(b, D, NP), ones[0:1, 0:NP], bias_row, start=False, stop=True))
                bank_free[b] = finish(j, bank(b, D, NP), t)
                done.append(bank_free[b])
            return done

        t = dve.do(lambda e: e.memset(ones[:], 1.0))
        t_mh = dve.do(lambda e: e.memset(minus_half[:], -0.5))
        t = pool.do(lambda e: e.memset(ident[:], 0.0))
        t_ident = pool.do(lambda e: e.affine_select(out=ident[:], in_=ident[:], compare_op=ALU.not_equal, fill=1.0,
                                                    base=0, pattern=[[-1, 128]], channel_multiplier=1), [t])
        t_x = dma("x", sp, X[:], x.rearrange("(j p) d -> p j d", p=NP))

        wr = Region(WORK, ARENA)
        no_edge = wr.take("no_edge", [NP, NT, N], BF16)
        AT0 = wr.at
        HC = NCHUNK // 2
        GROUP = 5
        GROUPS = NCHUNK // GROUP
        BLOCK = 8
        BLOCKS_E = GROUPS // BLOCK
        assert GROUPS * GROUP == NCHUNK and BLOCKS_E * BLOCK == GROUPS and GROUPS <= 32
        edges_i = wr.take("edges_i", [HC, 2, 2, NP], I32)
        edges_f = wr.take("edges_f", [HC, 2, 2, NP])
        edge_col = wr.take("edge_col", [NP, 2, 2, HC])
        group_dst = wr.take("group_dst", [GROUPS, GROUP * NP], I32)
        group_f = wr.take("group_f", [GROUPS, GROUP * NP])
        group_low = wr.take("group_low", [GROUPS, 1])
        group_high = wr.take("group_high", [GROUPS, 1])
        touches = wr.take("touches", [GROUPS, NT])
        below = wr.take("below", [GROUPS, NT])
        flags = wr.take("flags", [NT, GROUPS], I32)
        block_flags = wr.take("block_flags", [NT, BLOCKS_E], I32)
        zeros = wr.take("zeros", [1, BANK], BF16)
        tally = wr.take("tally", [1, 4])
        iota_i = wr.take("iota_i", [NP, N], I32)
        iota_h = wr.take("iota_h", [NP, N], F16)
        RING = 4
        src_hot = [wr.take(f"src_hot{i}", [NP, N], BF16) for i in range(RING * GROUP)]
        dst_hot = [wr.take(f"dst_hot{i}", [NP, NP + 1], BF16) for i in range(RING * GROUP)]
        count_rows = [wr.take(f"count_rows{i}", [NP, N]) for i in range(2)]
        for half in range(2):
            for w, a in enumerate((src, dst)):
                t_e = dma("edges", sp, edges_i[:, half, w, :], a.rearrange("(h c p) -> h c p", h=2, p=NP)[half])
        t_g = dma("group_dst", sp, group_dst[:], dst.rearrange("(g e) -> g e", g=GROUPS))
        t = pool.do(lambda e: e.iota(iota_i[:], pattern=[[1, N]], base=0, channel_multiplier=0))
        t_iota = pool.do(lambda e: e.tensor_copy(iota_h[:], iota_i[:]), [t])
        t = dve.do(lambda e: e.tensor_copy(edges_f[:], edges_i[:]), [t_e])
        for half in range(2):
            for w in range(2):
                tt = pe.do(lambda e, half=half, w=w: e.transpose(
                    psum[0:NP, (2 * w + half) * HC:(2 * w + half + 1) * HC], edges_f[:, half, w, :], ident[0:HC, 0:HC]), [t, t_ident])
        t_col = dve.do(lambda e: e.tensor_copy(edge_col[:].rearrange("p w h c -> p (w h c)"), psum[0:NP, 0:4 * HC]), [tt])
        bank_free[0] = t_col
        t = dve.do(lambda e: e.tensor_copy(group_f[:], group_dst[:]), [t_g])
        t1 = dve.do(lambda e: e.tensor_reduce(group_low[:], group_f[:], AX.X, ALU.min), [t])
        t2 = dve.do(lambda e: e.tensor_reduce(group_high[:], group_f[:], AX.X, ALU.max))
        t3 = dve.do(lambda e: e.tensor_scalar(touches[:], iota_h[0:GROUPS, NP - 1:N:NP], group_low[:, 0:1], None, ALU.is_ge), [t1, t_iota])
        t4 = dve.do(lambda e: e.tensor_scalar(below[:], iota_h[0:GROUPS, 0:N:NP], group_high[:, 0:1], None, ALU.is_le), [t2])
        t = dve.do(lambda e: e.tensor_tensor(touches[:], touches[:], below[:], ALU.mult), [t4])
        tt = pe.do(lambda e: e.transpose(psum[0:NT, BANK:BANK + GROUPS], touches[:], ident[0:GROUPS, 0:GROUPS]), [t])
        dve.do(lambda e: e.tensor_copy(flags[:], psum[0:NT, BANK:BANK + GROUPS]), [tt])
        t_flags = bank_free[1] = dve.do(lambda e: e.tensor_reduce(
            block_flags[:], psum[0:NT, BANK:BANK + GROUPS].rearrange("p (b g) -> p b g", g=BLOCK), AX.X, ALU.max))
        t_zeros = dve.do(lambda e: e.memset(zeros[:], 0.0))

        def build_counts():
            rows_free = [None, None]
            registers = {}
            hot_ticks, used_ticks = [], []

            def load_flags(q, key, j):
                def load(e):
                    if key not in registers:
                        registers[key] = ([e.alloc_register(f"{key}_group{g}") for g in range(GROUPS)],
                                          [e.alloc_register(f"{key}_block{b}") for b in range(BLOCKS_E)])
                    e.reg_load(registers[key][0], flags[j:j + 1, :])
                    e.reg_load(registers[key][1], block_flags[j:j + 1, :])
                q.wait([t_flags])
                q.steps.append(load)

            def raw_wait(e, tick):
                e.wait_ge(tick.sem, tick.value)

            def over_block(q, key, block, group_body, tick_op, first, n0):
                def run(e):
                    groups, blocks = registers[key]
                    with e.If_ne(blocks[block], 0):
                        for i in range(BLOCK):
                            before, body, tick = group_body(block * BLOCK + i, n0 + i)
                            for w in before:
                                raw_wait(e, w)
                            with e.If_ne(groups[block * BLOCK + i], 0):
                                for make in body:
                                    make(e)
                            tick(e).then_inc(q.sem, 1)
                    with e.Else():
                        raw_wait(e, first)
                        tick_op(e).then_inc(q.sem, BLOCK)
                q.steps.append(run)

            counted = []

            def turn(j):
                rows, ready = counted[j]
                for s0 in range(0, NT, 4):
                    b = 6 + (s0 // 4) % 2
                    m = min(4, NT - s0)
                    view = bank(b, m * 128, NP).rearrange("p (k c) -> p k c", c=128)[:, :, 0:NP]
                    for k in range(m):
                        t5 = pe.do(lambda e, k=k, s0=s0, view=view: e.transpose(
                            view[:, k, :], rows[:, (s0 + k) * NP:(s0 + k + 1) * NP], ident[0:NP, 0:NP]), [ready, bank_free[b]])
                    bank_free[b] = act.do(lambda e, s0=s0, m=m, view=view: e.copy(
                        counts[:, s0:s0 + m, j * NP:(j + 1) * NP], view), [t5])
                return t5
            n = 0
            for j in range(NT):
                b0 = 3 * (j % 2)
                parts = [(q * BANK, min(BANK, N - q * BANK)) for q in range(3)]
                ps = psum[0:NP, b0 * BANK:b0 * BANK + N]
                load_flags(dve, "dve", j)
                load_flags(pe, "pe", j)
                for c0, w in parts:
                    pe.do(lambda e, ps=ps, c0=c0, w=w: e.matmul(ps[:, c0:c0 + w], zeros[:, 0:NP], zeros[:, 0:w], start=True, stop=False),
                          [t_zeros] + bank_free[b0:b0 + 3], quiet=True)
                dve.wait([t_col, t_iota])

                def make_hot(g, n, j=j):
                    body = []
                    for i in range(GROUP):
                        c, slot = g * GROUP + i, n % RING * GROUP + i
                        for w, target, nodes in ((0, src_hot[slot][:], iota_h[:]),
                                                 (1, dst_hot[slot][:, 0:NP], iota_h[:, j * NP:(j + 1) * NP])):
                            body.append(lambda e, w=w, c=c, target=target, nodes=nodes: e.tensor_scalar(
                                target, nodes, edge_col[:, w, c // HC, c % HC:c % HC + 1], None, ALU.is_equal))
                    return used_ticks[n - RING:n - RING + 1] if n >= RING else [], body, \
                        lambda e: e.memset(tally[:, n % RING:n % RING + 1], 0.0)

                def multiply(g, n, ps=ps, parts=parts):
                    body = [lambda e, slot=n % RING * GROUP + i, c0=c0, w=w: e.matmul(
                        ps[:, c0:c0 + w], dst_hot[slot][:, 0:NP], src_hot[slot][:, c0:c0 + w], start=False, stop=False)
                        for i in range(GROUP) for c0, w in parts]
                    return [hot_ticks[n]], body, lambda e: e.matmul(ps[:, 0:2], zeros[:, 0:NP], zeros[:, 0:2], start=False, stop=False)

                for block in range(BLOCKS_E):
                    for i in range(BLOCK):
                        hot_ticks.append(Tick(dve.sem, dve.count + 1 + i))
                        used_ticks.append(Tick(pe.sem, pe.count + 1 + i))
                    over_block(dve, "dve", block, make_hot, lambda e: e.memset(tally[:, 0:1], 0.0), used_ticks[n - 1] if n else Tick(pe.sem, 0), n)
                    over_block(pe, "pe", block, multiply, lambda e, ps=ps: e.matmul(ps[:, 0:2], zeros[:, 0:NP], zeros[:, 0:2], start=False, stop=False),
                               hot_ticks[n + BLOCK - 1], n)
                    n += BLOCK
                    dve.count += BLOCK
                    pe.count += BLOCK
                if j:
                    rows_free[(j - 1) % 2] = turn(j - 1)
                for c0, w in parts:
                    t2 = pe.do(lambda e, ps=ps, c0=c0, w=w: e.matmul(ps[:, c0:c0 + w], zeros[:, 0:NP], zeros[:, 0:w], start=False, stop=True))
                rows = count_rows[j % 2]
                t3 = act.do(lambda e, j=j, rows=rows, ps=ps: e.activation(rows[:], ps, ACT.Identity, accum_out=deg[:, j:j + 1]), [t2, rows_free[j % 2]])
                t4 = act.do(lambda e, j=j, rows=rows: e.copy(no_edge[:, j, :], rows[:]), [t3])
                bank_free[b0:b0 + 3] = [t3] * 3
                counted.append((rows, t3))
            rows_free[1] = turn(NT - 1)
            for j in range(NT):
                dve.do(lambda e, j=j: e.tensor_scalar(no_edge[:, j, :], no_edge[:, j, :], 0.0, MASKED, ALU.is_equal, ALU.mult), [t4])

        build_counts()
        fence()
        if stop_after == "counts":
            t = dve.do(lambda e: e.tensor_copy(X[:], counts[:, :, 0:D]), [t_x])
            return finish_program(nc, ctx, out, X, dma, (pe, dve, act, pool, sp), [t], NP)

        wr = Region(AT0, ARENA)
        H = wr.take("H", [NP, NT, D])
        WA = wr.take("WA", [128, KD, D])
        WB = wr.take("WB", [128, KD, D])
        STAGE0 = wr.at

        def attention_layer0():
            g = Region(STAGE0, ARENA)
            M = L0["proj"].shape[0]
            DH = L0["proj"].shape[1]
            HEADS = D // DH
            RT = 2
            ROWS = RT * 128
            h_in = g.take("h_in", [128, RT, D])
            hT = g.take("hT", [128, KD, ROWS])
            nat = {c: g.take(c + "_nat", [128, RT, D]) for c in "qkv"}
            tT = {c: g.take(c + "_T", [128, KD, ROWS]) for c in "qk"}
            squares = g.take("squares", [128, RT, D])
            half_norm = {c: g.take(c + "_halfnorm", [128, RT, HEADS]) for c in "qk"}
            proj_in = g.take("proj_in", [128, M // 128, DH])
            projT = g.take("projT", [128, M])
            umax = {c: g.take(c + "_umax", [128, RT, HEADS]) for c in "qk"}
            shift = {c: g.take(c + "_shift", [128, RT, HEADS]) for c in "qk"}
            row_max = g.take("row_max", [HEADS, 1])
            both = g.take("both_max", [128, HEADS])
            diag = g.take("diag", [HEADS, HEADS])
            feat = {c: [g.take(f"{c}_feat{i}", [128, RT, M]) for i in range(2)] for c in "qk"}
            qfT = [g.take(f"qfT{i}", [128, M // 128, ROWS]) for i in range(2)]
            v1 = g.take("v_and_one", [128, RT, HEADS, DH + 1])
            kv = [g.take(f"kv{i}", [128, M // 128, DH + 1]) for i in range(2)]
            z = g.take("z", [128, RT])
            o_nat = g.take("o_nat", [128, RT, D])
            TILES = 4
            oT = g.take("oT", [128, KD, TILES * NP])
            t_h = dma("h_in", sp, h_in[:], x[0:ROWS].rearrange("(r p) d -> p r d", p=128))
            t_pj = dma("proj", sp, proj_in[:], L0["proj"].rearrange("(r p) d -> p r d", p=128))
            for r in range(RT):
                b = r
                for k in range(KD):
                    t = pe.do(lambda e, r=r, k=k, b=b: e.transpose(bank(b)[:, k * 128:(k + 1) * 128],
                                                               h_in[:, r, k * 128:(k + 1) * 128], ident[:]), [t_h, bank_free[b]])
                th = act.do(lambda e, r=r, b=b: e.copy(hT[:, :, r * 128:(r + 1) * 128], bank(b).rearrange("p (k c) -> p k c", k=KD)), [t])
                bank_free[b] = th
            for m in range(M // 128):
                t = pe.do(lambda e, m=m: e.transpose(psum[0:DH, 2 * BANK + m * 128:2 * BANK + (m + 1) * 128], proj_in[:, m, :], ident[:]), [t_pj, bank_free[2]])
            act.do(lambda e: e.copy(projT[0:DH, :], psum[0:DH, 2 * BANK:2 * BANK + M]), [t])
            t_proj = bank_free[2] = act.do(lambda e: e.copy(projT[DH:2 * DH, :], psum[0:DH, 2 * BANK:2 * BANK + M]), [t])
            scale = DH ** -0.25
            free_w = [None, None]
            ready = {}
            for i, (c, name) in enumerate((("q", "Wq"), ("k", "Wk"), ("v", "Wv"))):
                W = (WA, WB)[i % 2]
                tw = dma(("wa", "wb")[i % 2], sp, W[:], L0[name].rearrange("(k p) n -> p k n", p=128), [free_w[i % 2]])
                for r in range(RT):
                    b = 4 + r
                    for k in range(KD):
                        t = pe.do(lambda e, r=r, k=k, b=b, W=W: e.matmul(bank(b), hT[:, k, r * 128:(r + 1) * 128], W[:, k, :],
                                                                     start=k == 0, stop=k == KD - 1), [th, tw, bank_free[b]])
                    s = scale if c != "v" else 1.0
                    ready[c] = bank_free[b] = act.do(lambda e, r=r, b=b, c=c, s=s: e.mul(nat[c][:, r, :], bank(b), s), [t])
                free_w[i % 2] = t
            for c in "qk":
                t = dve.do(lambda e, c=c: e.tensor_tensor(squares[:], nat[c][:], nat[c][:], ALU.mult), [ready[c], dve.last()])
                t = dve.do(lambda e, c=c: e.tensor_reduce(half_norm[c][:], squares[:].rearrange("p r (h d) -> p r h d", h=HEADS), AX.X, ALU.add), [t])
                for r in range(RT):
                    b = r
                    for k in range(KD):
                        t = pe.do(lambda e, r=r, k=k, b=b, c=c: e.transpose(bank(b)[:, k * 128:(k + 1) * 128],
                                                                        nat[c][:, r, k * 128:(k + 1) * 128], ident[:]), [ready[c], bank_free[b]])
                    ready[c + "T"] = bank_free[b] = act.do(lambda e, r=r, b=b, c=c: e.copy(
                        tT[c][:, :, r * 128:(r + 1) * 128], bank(b).rearrange("p (k c) -> p k c", k=KD)), [t])
            dve.do(lambda e: e.memset(v1[:], 1.0))
            t_v1 = dve.do(lambda e: e.tensor_copy(v1[:, :, :, 0:DH], nat["v"][:].rearrange("p r (h d) -> p r h d", h=HEADS)), [ready["v"], dve.last()])

            def scores(c, h, b):
                k, p0 = h // 2, DH * (h % 2)
                for r in range(RT):
                    t = pe.do(lambda e, r=r: e.matmul(bank(b)[:, r * M:(r + 1) * M], tT[c][p0:p0 + DH, k, r * 128:(r + 1) * 128],
                                                      projT[p0:p0 + DH, :], start=r == 0, stop=r == RT - 1, skip_group_check=True),
                              [ready[c + "T"], t_proj, bank_free[b]])
                return t
            for h in range(HEADS):
                b = h % 2
                t = scores("k", h, b)
                t_um = bank_free[b] = dve.do(lambda e, h=h, b=b: e.tensor_reduce(
                    umax["k"][:, :, h], bank(b).rearrange("p (r m) -> p r m", r=RT), AX.X, ALU.max), [t])
            t = dve.do(lambda e: e.tensor_tensor(both[:], umax["k"][:, 0, :], umax["k"][:, 1, :], ALU.max), [t_um])
            t = pe.do(lambda e: e.transpose(psum[0:HEADS, 3 * BANK:3 * BANK + 128], both[:], ident[:]), [t, bank_free[3]])
            t = dve.do(lambda e: e.tensor_reduce(row_max[:], psum[0:HEADS, 3 * BANK:3 * BANK + 128], AX.X, ALU.max), [t])
            t = dve.do(lambda e: e.tensor_scalar(diag[:], ident[0:HEADS, 0:HEADS], row_max[:, 0:1], None, ALU.mult), [t])
            t = pe.do(lambda e: e.matmul(psum[:, 3 * BANK:3 * BANK + HEADS], ones[0:HEADS, :], diag[:], start=True, stop=True), [t])
            for r in range(RT):
                t_sk = dve.do(lambda e, r=r: e.scalar_tensor_tensor(shift["k"][:, r, :], half_norm["k"][:, r, :], -0.5,
                                                                psum[:, 3 * BANK:3 * BANK + HEADS], ALU.mult, ALU.subtract), [t])
            bank_free[3] = t_sk
            inv = 1.0 / math.sqrt(M)
            for h in range(HEADS):
                i = h % 2
                for c in "kq":
                    b = 0 if c == "k" else 1
                    t = scores(c, h, b)
                    ready_shift = t_sk
                    if c == "q":
                        t2 = dve.do(lambda e, h=h, b=b: e.tensor_reduce(
                            umax["q"][:, :, h], bank(b).rearrange("p (r m) -> p r m", r=RT), AX.X, ALU.max), [t])
                        ready_shift = dve.do(lambda e, h=h: e.scalar_tensor_tensor(
                            shift["q"][:, :, h], half_norm["q"][:, :, h], -0.5, umax["q"][:, :, h], ALU.mult, ALU.subtract), [t2])
                    for r in range(RT):
                        t3 = act.do(lambda e, h=h, r=r, b=b, c=c, i=i: e.activation(
                            feat[c][i][:, r, :], bank(b)[:, r * M:(r + 1) * M], ACT.Exp, bias=shift[c][:, r, h:h + 1]),
                            [t, ready_shift, pe.last() if r == 0 else None])
                    bank_free[b] = t3
                    t4 = dve.do(lambda e, c=c, i=i: e.tensor_scalar(feat[c][i][:], feat[c][i][:], inv, KEPS, ALU.mult, ALU.add), [t3])
                    if c == "k":
                        for m in range(M // 128):
                            for r in range(RT):
                                t5 = pe.do(lambda e, h=h, m=m, r=r, i=i: e.matmul(
                                    psum[:, (2 + m) * BANK:(2 + m) * BANK + DH + 1], feat["k"][i][:, r, m * 128:(m + 1) * 128], v1[:, r, h, :],
                                    start=r == 0, stop=r == RT - 1), [t4, t_v1, bank_free[2 + m]])
                            t_kv = bank_free[2 + m] = dve.do(lambda e, m=m, i=i: e.tensor_copy(
                                kv[i][:, m, :], psum[:, (2 + m) * BANK:(2 + m) * BANK + DH + 1]), [t5])
                    else:
                        for m in range(M // 128):
                            for r in range(RT):
                                t5 = pe.do(lambda e, m=m, r=r, i=i: e.transpose(
                                    psum[:, 4 * BANK + (m * RT + r) * 128:4 * BANK + (m * RT + r + 1) * 128], feat["q"][i][:, r, m * 128:(m + 1) * 128], ident[:]),
                                    [t4, bank_free[4]])
                        t_qf = bank_free[4] = act.do(lambda e, i=i: e.copy(qfT[i][:].rearrange("p m n -> p (m n)"), bank(4)), [t5])
                for r in range(RT):
                    b = 5 + r
                    for m in range(M // 128):
                        t6 = pe.do(lambda e, r=r, m=m, i=i, b=b: e.matmul(
                            psum[:, b * BANK:b * BANK + DH + 1], qfT[i][:, m, r * 128:(r + 1) * 128], kv[i][:, m, :], start=m == 0, stop=m == M // 128 - 1),
                            [t_qf, t_kv, bank_free[b]])
                    t7 = dve.do(lambda e, r=r, b=b: e.tensor_scalar(z[:, r:r + 1], psum[:, b * BANK + DH:b * BANK + DH + 1], KEPS, None, ALU.add), [t6])
                    t7 = dve.do(lambda e, r=r: e.reciprocal(z[:, r:r + 1], z[:, r:r + 1]), [t7])
                    t_o = bank_free[b] = dve.do(lambda e, r=r, b=b, h=h: e.tensor_scalar(
                        o_nat[:, r, h * DH:(h + 1) * DH], psum[:, b * BANK:b * BANK + DH], z[:, r:r + 1], None, ALU.mult), [t7])
            for r in range(RT):
                b = r
                for k in range(KD):
                    t = pe.do(lambda e, r=r, k=k, b=b: e.transpose(bank(b)[:, k * 128:(k + 1) * 128], o_nat[:, r, k * 128:(k + 1) * 128], ident[:]), [t_o, bank_free[b]])
                t_oT = bank_free[b] = act.do(lambda e, r=r, b=b: e.copy(oT[:, :, r * 128:(r + 1) * 128], bank(b).rearrange("p (k c) -> p k c", k=KD)), [t])
            t_oT = dve.do(lambda e: e.tensor_copy(oT[:, :, ROWS:], oT[:, :, ROWS - 1:ROWS].to_broadcast([128, KD, TILES * NP - ROWS])), [t_oT])
            tw = dma("wb", sp, WB[:], L0["Wo"].rearrange("(k p) n -> p k n", p=128), [free_w[1]])

            def finish(j, ps, t):
                for jj in ([j] if j < TILES - 1 else range(TILES - 1, NT)):
                    t2 = dve.do(lambda e, jj=jj: e.tensor_tensor(H[:, jj, :], ps, X[:, jj, :], ALU.add), [t, t_x])
                return t2
            pe.wait([tw])
            done = dense(oT, WB, None, [t_oT] * TILES, finish, tiles=range(TILES))
            return done[-1]

        t_attn = attention_layer0()
        fence()
        if stop_after == "attn0":
            t = dve.do(lambda e: e.tensor_copy(X[:], H[:]), [t_attn])
            return finish_program(nc, ctx, out, X, dma, (pe, dve, act, pool, sp), [t], NP)

        def layer0():
            g = Region(STAGE0, ARENA)
            A = g.take("A", [NP, NT, D])
            T = g.take("T", [128, KD, N])
            inv_deg = g.take("inv_deg", [NP, NT])
            b_conv = g.take("b_conv", [1, D])
            tw = dma("wa", sp, WA[:], L0["W_conv"].rearrange("(k p) n -> p k n", p=128))
            tb = dma("b_conv", sp, b_conv[:], L0["b_conv"].rearrange("(a n) -> a n", a=1))
            save = g.at
            xn_ready = batch_norm(X, A, L0["norm1_g"], L0["norm1_b"], g, "bn1", [None] * NT)
            t = dve.do(lambda e: e.tensor_scalar(inv_deg[:], deg[:], 1.0, None, ALU.max))
            t_inv = dve.do(lambda e: e.reciprocal(inv_deg[:], inv_deg[:]), [t])
            AGG = nc.alloc_sbuf_tensor_at("AGG", [NP, NT, D], F32, offset=base + save)
            act.wait([xn_ready[-1]])
            agg_ready = gather_sum(A, xn_ready, lambda j, ps, t: act.do(
                lambda e: e.activation(AGG[:, j, :], ps, ACT.Identity, scale=inv_deg[:, j:j + 1]), [t, t_inv]))
            t_T = transpose_nodes(AGG, lambda j, v, t: [copy_out(j, T[:, :, j * NP:(j + 1) * NP], v, [t])], agg_ready)
            pe.wait([tw, tb])

            def add_conv(j, ps, t):
                return dve.do(lambda e: e.scalar_tensor_tensor(H[:, j, :], ps, 0.0, H[:, j, :], ALU.max, ALU.add), [t])
            h_ready = dense(T, WA, b_conv[0:1, :], t_T, add_conv)
            fence()
            g = Region(STAGE0, ARENA)
            A = g.take("A2", [NP, NT, D])
            bn_ready = batch_norm(H, A, L0["norm2_g"], L0["norm2_b"], g, "bn2", h_ready)
            x_ready = [dve.do(lambda e, j=j: e.tensor_tensor(X[:, j, :], X[:, j, :], A[:, j, :], ALU.add), [bn_ready[j]]) for j in range(NT)]
            x_ready = layer_norm(x_ready)
            fence()
            return x_ready

        x_ready = layer0()
        if stop_after == "L0":
            return finish_program(nc, ctx, out, X, dma, (pe, dve, act, pool, sp), x_ready, NP)

        def layer1(x_ready):
            HEADS1, _, DH1 = L1["Ws"].shape
            g = Region(AT0, ARENA)
            H = nc.alloc_sbuf_tensor_at("H1", [NP, NT, D], F32, offset=base + g.at)
            g.at += 4 * NT * D
            WH = g.take("WH", [NP, NT, HEADS1, DH1 + 1])
            SHIFT0 = g.at
            T = g.take("T1", [128, KD, N])
            W1 = g.take("W1", [128, KD, D])
            Wb = g.take("Wb1", [1, D])
            aw = g.take("aw", [NP, HEADS1, 2 * DH1])
            ab = g.take("ab", [NP, HEADS1])
            prod = [g.take(f"prod{i}", [NP, HEADS1, DH1]) for i in range(2)]
            SCORES_END = g.at
            tgt = g.take("tgt_score", [NP, NT, HEADS1])
            srcs = g.take("src_score", [NP, NT, HEADS1])
            srcs02 = g.take("src_score02", [NP, NT, HEADS1])
            nb_max = g.take("nb_max", [NP, NT, HEADS1])
            leak = g.take("leak", [NP, NT, HEADS1])
            rowT = {n: g.take("rowT_" + n, [HEADS1, N]) for n in ("src", "pos", "neg")}
            pick = g.take("pick", [HEADS1, HEADS1, 128])
            trash = g.take("trash", [NP, N], BF16)
            t_w = []
            for k in range(KD):
                t_w = dma("wa", sp, W1[:, k, :].rearrange("p (h d) -> p h d", h=HEADS1), L1["Ws"][:, k * 128:(k + 1) * 128, :].rearrange("h p d -> p h d"))
            t_wb = dma("b_conv", sp, Wb[:], L1["Wb"].rearrange("(a h) d -> a (h d)", a=1))
            t_aw = dma("aw", sp, aw[:], row_on_partitions(L1["a_w"]))
            t_ab = dma("aw", sp, ab[:], row_on_partitions(L1["a_b"]))
            t_pick = pool.do(lambda e: e.tensor_copy(pick[:], ident[0:HEADS1, 0:HEADS1].unsqueeze(2).to_broadcast([HEADS1, HEADS1, 128])))
            t_T = transpose_nodes(X, lambda j, v, t: [copy_out(j, T[:, :, j * NP:(j + 1) * NP], v, [t])], x_ready)
            t_one = pool.do(lambda e: e.memset(WH[:, :, :, DH1:DH1 + 1], 1.0))
            pe.wait([t_w, t_wb])
            wh_ready = dense(T, W1, Wb[0:1, :], t_T, lambda j, ps, t: copy_out(
                j, WH[:, j, :, 0:DH1], ps.rearrange("p (h d) -> p h d", h=HEADS1), [t]))
            for j in range(NT):
                for i, target in ((0, tgt), (1, srcs)):
                    t = dve.do(lambda e, j=j, i=i: e.tensor_tensor(prod[i][:], WH[:, j, :, 0:DH1], aw[:, :, i * DH1:(i + 1) * DH1], ALU.mult),
                               [wh_ready[j], t_ab, t_one, dve.last()])
                    t = dve.do(lambda e, j=j, i=i, target=target: e.tensor_reduce(target[:, j, :], prod[i][:], AX.X, ALU.add), [t])
                t_tgt = dve.do(lambda e, j=j: e.tensor_tensor(tgt[:, j, :], tgt[:, j, :], ab[:], ALU.add), [dve.last()])
            t_src02 = pool.do(lambda e: e.tensor_scalar(srcs02[:], srcs[:], 0.2, None, ALU.mult), [t_tgt])

            def to_rows(source, row, ready):
                view = psum[0:HEADS1, 0:NT * 128].rearrange("p (j c) -> p j c", c=128)
                for j in range(NT):
                    t = pe.do(lambda e, j=j: e.transpose(view[:, j, 0:NP], source[:, j, :], ident[0:NP, 0:NP]),
                              [ready, bank_free[0], bank_free[1], bank_free[2]])
                t = act.do(lambda e: e.copy(row[:].rearrange("p (j c) -> p j c", c=NP), view[:, :, 0:NP]), [t])
                bank_free[0] = bank_free[1] = bank_free[2] = t
                return t

            def spread_row(row, h, b0, ready):
                for q in range(3):
                    w = min(BANK, N - q * BANK)
                    t = pe.do(lambda e, q=q, w=w: e.matmul(psum[0:NP, (b0 + q) * BANK:(b0 + q) * BANK + w], pick[:, h, 0:NP],
                                                          row[:, q * BANK:q * BANK + w], start=True, stop=True),
                              [ready, t_pick] + bank_free[b0:b0 + 3])
                return t

            def spread_view(b0):
                return psum[0:NP, b0 * BANK:b0 * BANK + N]
            t_rows = to_rows(srcs, rowT["src"], t_tgt)
            for h in range(HEADS1):
                b0 = 3 * (h % 2)
                t = spread_row(rowT["src"], h, b0, t_rows)
                for j in range(NT):
                    t2 = dve.do(lambda e, h=h, j=j, b0=b0: e.tensor_tensor_reduce(
                        trash[:], spread_view(b0), no_edge[:, j, :], 1.0, 3 * MASKED, ALU.add, ALU.max, nb_max[:, j, h:h + 1]), [t, dve.last()])
                bank_free[b0] = bank_free[b0 + 1] = bank_free[b0 + 2] = t2
            t = dve.do(lambda e: e.tensor_tensor(nb_max[:], nb_max[:], tgt[:], ALU.add), [t2])
            t = dve.do(lambda e: e.scalar_tensor_tensor(nb_max[:], nb_max[:], 0.2, nb_max[:], ALU.mult, ALU.max), [t])
            t_neg = dve.do(lambda e: e.scalar_tensor_tensor(leak[:], tgt[:], 0.2, nb_max[:], ALU.mult, ALU.subtract), [t])
            t_pos = dve.do(lambda e: e.tensor_tensor(nb_max[:], tgt[:], nb_max[:], ALU.subtract), [t_neg])
            t_pos = to_rows(nb_max, rowT["pos"], t_pos)
            t_neg = to_rows(leak, rowT["neg"], t_neg)
            fence()
            s = Region(WORK, AT0)
            pos_row = [s.take(f"pos_row{i}", [NP, N]) for i in range(2)]
            neg_row = [s.take(f"neg_row{i}", [NP, N]) for i in range(2)]
            s = Region(SHIFT0, SCORES_END)
            LOWS, WEIGHTS = 2, 3
            low = [s.take(f"low{i}", [NP, N]) for i in range(LOWS)]
            weight = [s.take(f"weight{i}", [NP, N]) for i in range(WEIGHTS)]
            sumsT = s.take("sumsT", [DH1 + 1, N])
            recip = g.take("recip1", [NP, NT])
            PER_BANK = BANK // (DH1 + 1)
            steps = [(h, s_) for h in range(HEADS1) for s_ in range(NT)]
            t_row = {}
            row_read = {}
            t_low, t_score, t_exp = {}, {}, {}
            low_read, weight_read = {}, {}
            turned = {"sums": None}

            def spread_head(h, key):
                return spread_row(rowT[key], h, 3, t_pos if key == "pos" else t_neg)

            def keep_row(h, key, ready):
                out_ = (pos_row if key == "pos" else neg_row)[h % 2]
                t_row[h, key] = act.do(lambda e: e.copy(out_[:], spread_view(3)), [ready, row_read.get((h - 2, key))])
                bank_free[3:6] = [t_row[h, key]] * 3

            def make_low(n):
                h, s_ = steps[n]
                t_low[n] = row_read[h, "neg"] = act.do(lambda e: e.activation(
                    low[n % LOWS][:], neg_row[h % 2][:], ACT.Identity, bias=srcs02[:, s_, h:h + 1]),
                    [t_row[h, "neg"], t_src02, low_read.get(n - LOWS)])

            def make_score(n):
                h, s_ = steps[n]
                t_score[n] = row_read[h, "pos"] = low_read[n] = dve.do(lambda e: e.scalar_tensor_tensor(
                    weight[n % WEIGHTS][:], pos_row[h % 2][:], srcs[:, s_, h:h + 1], low[n % LOWS][:], ALU.add, ALU.max),
                    [t_low[n], t_row[h, "pos"], weight_read.get(n - WEIGHTS)])

            def make_exp(n):
                t_exp[n] = act.do(lambda e: e.activation(weight[n % WEIGHTS][:], weight[n % WEIGHTS][:], ACT.Exp), [t_score[n]])

            def weigh(n):
                h, s_ = steps[n]
                wt = weight[n % WEIGHTS]
                t = dve.do(lambda e: e.scalar_tensor_tensor(wt[:], wt[:], 1.0, counts[:, s_, :], ALU.min, ALU.mult), [t_exp[n]])
                for q in range(3):
                    w = min(BANK, N - q * BANK)
                    t2 = pe.do(lambda e, q=q, w=w: e.matmul(psum[0:DH1 + 1, q * BANK:q * BANK + w], WH[:, s_, h, :],
                                                           wt[:, q * BANK:q * BANK + w], start=s_ == 0, stop=s_ == NT - 1),
                               [t, bank_free[q] if s_ == 0 else None])
                weight_read[n] = t2
                return t2

            def take_sums(h, ready):
                t = act.do(lambda e: e.copy(sumsT[:], psum[0:DH1 + 1, 0:N]), [ready, turned["sums"]])
                bank_free[0:3] = [t] * 3
                return t

            def turn_sums(ready):
                for j in range(NT):
                    b, c = 6 + j // PER_BANK, j % PER_BANK * (DH1 + 1)
                    t = turned["sums"] = pe.do(lambda e, j=j, b=b, c=c: e.transpose(
                        psum[0:NP, b * BANK + c:b * BANK + c + DH1 + 1], sumsT[:, j * NP:(j + 1) * NP], ident[0:DH1 + 1, 0:DH1 + 1]),
                        [ready, bank_free[b]])
                return t

            def divide(h, ready):
                for j0, j1 in ((0, PER_BANK), (PER_BANK, NT)):
                    b = 6 + j0 // PER_BANK
                    v = psum[0:NP, b * BANK:b * BANK + (j1 - j0) * (DH1 + 1)].rearrange("p (j c) -> p j c", c=DH1 + 1)
                    t = dve.do(lambda e, v=v, j0=j0, j1=j1: e.tensor_scalar(recip[:, j0:j1], v[:, :, DH1], 1e-30, None, ALU.max), [ready])
                    t = dve.do(lambda e, j0=j0, j1=j1: e.reciprocal(recip[:, j0:j1], recip[:, j0:j1]), [t])
                    bank_free[b] = dve.do(lambda e, v=v, j0=j0, j1=j1: e.tensor_tensor(
                        H[:, j0:j1, h * DH1:(h + 1) * DH1], v[:, :, 0:DH1], recip[:, j0:j1].unsqueeze(2).to_broadcast([NP, j1 - j0, DH1]), ALU.mult), [t])

            for key in ("neg", "pos"):
                keep_row(0, key, spread_head(0, key))
            make_low(0)
            make_score(0)
            make_low(1)
            make_exp(0)
            sums, rows_of, turned_sums = None, None, None
            for n, (h, s_) in enumerate(steps):
                if n + 1 < len(steps):
                    make_score(n + 1)
                if n + 2 < len(steps):
                    make_low(n + 2)
                if n + 1 < len(steps):
                    make_exp(n + 1)
                if s_ == 0 and h:
                    sums = take_sums(h - 1, sums)
                if s_ == 1 and h:
                    turned_sums = turn_sums(sums)
                if s_ == 3 and h:
                    divide(h - 1, turned_sums)
                if h + 1 < HEADS1:
                    if s_ in (3, 6):
                        rows_of = spread_head(h + 1, "neg" if s_ == 3 else "pos")
                    if s_ in (4, 7):
                        keep_row(h + 1, "neg" if s_ == 4 else "pos", rows_of)
                t = weigh(n)
                if s_ == NT - 1:
                    sums = t
            divide(HEADS1 - 1, turn_sums(take_sums(HEADS1 - 1, sums)))
            out_free = bank_free[7]
            x_ready = [dve.do(lambda e, j=j: e.tensor_tensor(X[:, j, :], X[:, j, :], H[:, j, :], ALU.add), [out_free]) for j in range(NT)]
            x_ready = layer_norm(x_ready)
            fence()
            return x_ready

        x_ready = layer1(x_ready)
        if stop_after == "L1":
            return finish_program(nc, ctx, out, X, dma, (pe, dve, act, pool, sp), x_ready, NP)

        def layer2(x_ready):
            g = Region(WORK, ARENA)
            Y = g.take("Y2", [NP, NT, D])
            H = g.take("H2", [NP, NT, D])
            T = g.take("T2", [128, KD, N])
            W_in = g.take("W2_in", [128, KD, D])
            WT = g.take("W2_T", [128, KD, D])
            b2 = g.take("b2", [NP, D])
            dinv = g.take("dinv", [NP, NT])
            t_w = dma("wa", sp, W_in[:], L2["W"].rearrange("(m p) n -> p m n", p=128))
            t_b2 = dma("b_conv", sp, b2[:], row_on_partitions(L2["b"]))
            t = dve.do(lambda e: e.tensor_scalar(dinv[:], deg[:], 1.0, None, ALU.add))
            t_dinv = pool.do(lambda e: e.tensor_tensor(dinv[:], dinv[:], minus_half[0:NP, :], ALU.pow), [t])
            for k in range(KD):
                b = k
                for m in range(KD):
                    t = pe.do(lambda e, k=k, m=m, b=b: e.transpose(bank(b)[:, m * 128:(m + 1) * 128], W_in[:, m, k * 128:(k + 1) * 128], ident[:]), [t_w, bank_free[b]])
                t_WT = bank_free[b] = act.do(lambda e, k=k, b=b: e.copy(WT[:, k, :], bank(b)), [t])
            t_T = transpose_nodes(X, lambda j, v, t: [copy_out(j, T[:, :, j * NP:(j + 1) * NP], v, [t])], x_ready)
            pe.wait([t_WT])
            y_ready = dense(T, WT, None, t_T, lambda j, ps, t: act.do(
                lambda e: e.activation(Y[:, j, :], ps, ACT.Identity, scale=dinv[:, j:j + 1]), [t, t_dinv]))
            h_ready = [dve.do(lambda e, j=j: e.scalar_tensor_tensor(H[:, j, :], Y[:, j, :], dinv[:, j:j + 1], b2[:], ALU.mult, ALU.add),
                              [y_ready[j], t_b2]) for j in range(NT)]
            h_ready = gather_sum(Y, y_ready, lambda j, ps, t: dve.do(
                lambda e: e.scalar_tensor_tensor(H[:, j, :], ps, dinv[:, j:j + 1], H[:, j, :], ALU.mult, ALU.add), [t, h_ready[j]]))
            dve.wait([pe.last()])
            bn_ready = batch_norm(H, Y, L2["gamma"], L2["beta"], g, "bn3", h_ready)
            x_ready = []
            for j in range(NT):
                t = act.do(lambda e, j=j: e.activation(Y[:, j, :], Y[:, j, :], ACT.Gelu), [bn_ready[j]])
                t = dve.do(lambda e, j=j: e.scalar_tensor_tensor(X[:, j, :], X[:, j, :], 2.0, Y[:, j, :], ALU.mult, ALU.add), [t])
                x_ready.append(t)
            x_ready = layer_norm(x_ready)
            fence()
            return x_ready

        x_ready = layer2(x_ready)
        if stop_after == "L2":
            return finish_program(nc, ctx, out, X, dma, (pe, dve, act, pool, sp), x_ready, NP)

        def layer3(x_ready):
            BLOCKS, COND = L3["s1_w"].shape[0], L3["s1_w"].shape[1]
            HEADS = 4
            DH = D // HEADS
            SCALE = DH ** -0.5
            FREQS = L3["f_w1"].shape[0] // 2
            TWO_PI = 2 * math.pi
            x_in = nc.dram_tensor("x_in", [N, D], F32, kind="Internal").ap()
            tiles_of = lambda ap: ap.rearrange("(j p) d -> p j d", p=NP)
            t_save = dma("x_in", sp, tiles_of(x_in), X[:], x_ready)
            g = Region(WORK, ARENA)
            cond3 = g.take("cond3", [96, N], F32R)
            yT = [g.take(f"yT_{p}", [128, KD, N], F32R) for p in ("hi", "lo")]
            bias_out = g.take("bias_out", [NP, D])
            has_edge = g.take("has_edge", [NP, NT])
            shift = g.take("ln_shift", [NP, NT])
            bias_cols = g.take("bias_cols", [128, 4, BLOCKS, KD])
            cond_in = g.take("cond_in", [96, 2, D])
            PHASE = g.at

            def load_bias_columns():
                rows = Region(PHASE, ARENA).take("bias_rows", [4 * BLOCKS * KD, 128])
                for n, name in enumerate(("bq", "bk", "bv", "m_b1")):
                    t = dma("bias_rows", sp, rows[n * BLOCKS * KD:(n + 1) * BLOCKS * KD, :], L3[name].rearrange("i (k p) -> (i k) p", p=128))
                R = 4 * BLOCKS * KD
                t = pe.do(lambda e: e.transpose(psum[:, 7 * BANK:7 * BANK + R], rows[:], ident[0:R, 0:R]), [t, bank_free[7]])
                bank_free[7] = act.do(lambda e: e.copy(bias_cols[:].rearrange("p n i k -> p (n i k)"), psum[:, 7 * BANK:7 * BANK + R]), [t])
            load_bias_columns()
            fence()

            def split_lo(q, lo, exact, hi, after):
                return q.do(lambda e: e.tensor_tensor(lo, exact, hi.bitcast(F32), ALU.subtract), after)

            def condition():
                g = Region(PHASE, ARENA)
                R = 2 * FREQS
                angle = g.take("angle", [R, N])
                turns = g.take("turns", [R, N])
                freq_i = g.take("freq_i", [R, 1], I32)
                freq = g.take("freq", [R, 1])
                quarter = g.take("quarter", [R, 1])
                hidden = g.take("hidden", [COND, N])
                sig = g.take("sig", [COND, N])
                f_w1 = g.take("f_w1", [R, COND])
                f_b1 = g.take("f_b1", [COND, 1])
                f_w2x3 = g.take("f_w2x3", [COND, 96])
                f_b2x3 = g.take("f_b2x3", [96, 1])
                exact = g.take("cond_exact", [96, N])
                t_n = dma("noise", sp, angle[:], noise.rearrange("n o -> (n o)").partition_broadcast(R))
                dma("cond_w", sp, f_w1[:], L3["f_w1"])
                dma("cond_w", sp, f_b1[:], L3["f_b1"].rearrange("(p o) -> p o", o=1))
                t0 = dve.do(lambda e: e.memset(f_w2x3[:], 0.0))
                t0 = dve.do(lambda e: e.tensor_tensor(f_b2x3[:], ident[0:96, COND:COND + 1], ident[0:96, 32 + COND:33 + COND], ALU.add))
                t0 = dve.do(lambda e: e.tensor_tensor(f_b2x3[:], f_b2x3[:], ident[0:96, 64 + COND:65 + COND], ALU.add), [t0])
                for i in range(3):
                    dma("cond_w", sp, f_w2x3[:, 32 * i:32 * i + COND], L3["f_w2"], [t0])
                    t_w = dma("cond_w", sp, f_b2x3[32 * i:32 * i + COND, :], L3["f_b2"].rearrange("(p o) -> p o", o=1))
                pool.do(lambda e: e.iota(freq_i[0:FREQS, :], pattern=[[0, 1]], base=1, channel_multiplier=1))
                t = pool.do(lambda e: e.iota(freq_i[FREQS:R, :], pattern=[[0, 1]], base=1, channel_multiplier=1))
                dve.do(lambda e: e.memset(quarter[0:FREQS, :], 0.0))
                t_q = dve.do(lambda e: e.memset(quarter[FREQS:R, :], 0.25))
                t = dve.do(lambda e: e.tensor_copy(freq[:], freq_i[:]), [t])
                t = dve.do(lambda e: e.tensor_scalar(freq[:], freq[:], TWO_PI / 16, None, ALU.mult), [t])
                t = dve.do(lambda e: e.tensor_scalar(angle[:], angle[:], freq[:, 0:1], None, ALU.mult), [t, t_n])
                t = dve.do(lambda e: e.tensor_scalar(turns[:], angle[:], 1 / TWO_PI, quarter[:, 0:1], ALU.mult, ALU.add), [t, t_q])
                ROUND = 1.5 * 2 ** 23
                t = dve.do(lambda e: e.tensor_scalar(turns[:], turns[:], ROUND, None, ALU.add), [t])
                t = dve.do(lambda e: e.tensor_scalar(turns[:], turns[:], ROUND, None, ALU.subtract), [t])
                part1 = 6.28125
                part2 = math.ldexp(round(math.ldexp(TWO_PI - part1, 21)), -21)
                part3 = TWO_PI - part1 - part2
                for part in (part1, part2, part3):
                    t = dve.do(lambda e, part=part: e.scalar_tensor_tensor(angle[:], turns[:], -part, angle[:], ALU.mult, ALU.add), [t])
                t = dve.do(lambda e: e.tensor_scalar(quarter[:], quarter[:], TWO_PI, None, ALU.mult), [t])
                t = dve.do(lambda e: e.tensor_scalar(angle[:], angle[:], quarter[:, 0:1], None, ALU.add), [t])
                PI = 3.1415925
                t = dve.do(lambda e: e.tensor_scalar(angle[:], angle[:], PI, -PI, ALU.min, ALU.max), [t])
                t = act.do(lambda e: e.activation(angle[:], angle[:], ACT.Sin), [t])

                def product(rows, lhsT, rhs, b0, after):
                    for q in range(3):
                        w = min(BANK, N - q * BANK)
                        t = pe.do(lambda e, q=q, w=w: e.matmul(psum[0:rows, (b0 + q) * BANK:(b0 + q) * BANK + w], lhsT,
                                                          rhs[:, q * BANK:q * BANK + w], start=True, stop=True), after)
                    return psum[0:rows, b0 * BANK:b0 * BANK + N], t
                ps, t = product(COND, f_w1[:], angle, 0, [t, t_w])
                t1 = act.do(lambda e: e.activation(hidden[:], ps, ACT.Identity, bias=f_b1[:, 0:1]), [t])
                t = act.do(lambda e: e.activation(sig[:], hidden[:], ACT.Exp, scale=-1.0), [t1])
                t = dve.do(lambda e: e.tensor_scalar(sig[:], sig[:], 1.0, None, ALU.add), [t])
                t = dve.do(lambda e: e.reciprocal(sig[:], sig[:]), [t])
                t = dve.do(lambda e: e.tensor_tensor(hidden[:], hidden[:], sig[:], ALU.mult), [t])
                ps2, t = product(96, f_w2x3[:], hidden, 3, [t])
                t = act.do(lambda e: e.activation(exact[:], ps2, ACT.Identity, bias=f_b2x3[:, 0:1]), [t])
                t = act.do(lambda e: e.copy(cond3[:], exact[:]), [t])
                return split_lo(dve, cond3[32:64, :], exact[32:64, :], cond3[32:64, :], [t])
            condition()
            fence()
            g = Region(PHASE, ARENA)
            absent = [g.take(f"absent{i}", [NP, N]) for i in range(2)]
            free = [None, None]
            for s in range(NT):
                a = absent[s % 2]
                t1 = dve.do(lambda e, s=s, a=a: e.tensor_scalar(a[:], counts[:, s, :], 0.0, MASKED, ALU.is_equal, ALU.mult), [free[s % 2]])
                t = dve.do(lambda e, s=s: e.tensor_reduce(has_edge[:, s:s + 1], counts[:, s, :], AX.X, ALU.max))
                t = dve.do(lambda e, s=s: e.tensor_scalar(counts[:, s, :], counts[:, s, :], 1.0, None, ALU.max), [t, t1])
                t = act.do(lambda e, s=s: e.activation(counts[:, s, :], counts[:, s, :], ACT.Ln), [t])
                free[s % 2] = dve.do(lambda e, s=s, a=a: e.scalar_tensor_tensor(counts[:, s, :], counts[:, s, :], 1 / SCALE, a[:], ALU.mult, ALU.add), [t])
            dve.do(lambda e: e.tensor_scalar(has_edge[:], has_edge[:], 1.0, None, ALU.min), [dve.last()])
            edge_term = counts

            def split_weight(name, stage, hi, lo, source, free):
                t = dma(name, sp, stage[:], source, [pool_done.get(name)])
                t = pool.do(lambda e: e.tensor_copy(hi[:], stage[:]), [t] + free)
                t = pool_done[name] = split_lo(pool, lo[:], stage[:], hi[:], [t])
                return t
            pool_done = {}

            def norm_stats(j, t):
                t = dve.do(lambda e: e.bn_stats(stats[:, j, :], X[:, j, :]), [t])
                return dve.do(lambda e: e.bn_aggr(mean_var[:, j, :], stats[:, j, :]), [t])

            norm_scale, cond_loaded = {}, {}

            def finish_stats():
                t = dve.do(lambda e: e.tensor_scalar(rstd[:], mean_var[:, :, 1], EPS, None, ALU.add), [dve.last()])
                t = pool.do(lambda e: e.tensor_tensor(rstd[:], rstd[:], minus_half[0:NP, :], ALU.pow), [t])
                norm_scale["t"] = dve.do(lambda e: e.scalar_tensor_tensor(shift[:], mean_var[:, :, 0], -1.0, rstd[:], ALU.mult, ALU.mult), [t])

            def load_condition(i, a, used):
                for n, c in enumerate("sb"):
                    for r in range(3):
                        dma("cw", sp, cond_in[32 * r:32 * r + COND, n, :], L3[f"{c}{a}_w"][i], [used])
                        cond_loaded["t"] = dma("cw", sp, cond_in[32 * r + COND:32 * r + COND + 1, n, :], L3[f"{c}{a}_b"][i:i + 1, :])

            def cond_norm(i, a, g, t_bias):
                w3 = g.take(f"cw3_{i}{a}", [96, 2, D], F32R)
                xn = [g.take(f"xn{i}{a}{n}", [NP, D]) for n in range(3)]
                t = act.do(lambda e: e.copy(w3[:], cond_in[:]), [cond_loaded["t"]])
                t_w = split_lo(dve, w3[64:96, :, :], cond_in[64:96, :, :], w3[64:96, :, :], [t])
                if a == 1:
                    load_condition(i, 2, t_w)
                elif i + 1 < BLOCKS:
                    load_condition(i + 1, 1, t_w)
                t_shift = norm_scale["t"]
                xn_free = [None] * 3
                normed, turned = {}, {}

                def modulate(j):
                    b0 = 2 * (j % 2)
                    for n in range(2):
                        t = pe.do(lambda e, n=n: e.matmul(bank(b0 + n, D, NP), cond3[:, j * NP:(j + 1) * NP], w3[:, n, :],
                                                          start=True, stop=True), [t_w, bank_free[b0 + n]])
                    return t

                def norm_tile(j):
                    x_, b0 = xn[j % 3], 2 * (j % 2)
                    t1 = normed[j] = act.do(lambda e: e.activation(x_[:], X[:, j, :], ACT.Identity, bias=shift[:, j:j + 1], scale=rstd[:, j:j + 1]),
                                            [t_shift, xn_free[j % 3]])
                    t2 = modulated[j]
                    t3 = bank_free[b0] = dve.do(lambda e: e.scalar_tensor_tensor(x_[:], bank(b0, D, NP), 1.0, x_[:], ALU.add, ALU.mult), [t1, t2])
                    t4 = bank_free[b0 + 1] = dve.do(lambda e: e.tensor_tensor(x_[:], bank(b0 + 1, D, NP), x_[:], ALU.add), [t3])
                    if j + 1 < NT:
                        modulated[j + 1] = modulate(j + 1)
                    b = 4 + j % 2
                    v = bank(b).rearrange("p (k c) -> p k c", k=KD)
                    for k in range(KD):
                        t5 = pe.do(lambda e, k=k: e.transpose(v[:, k, 0:NP], x_[:, k * 128:(k + 1) * 128], ident[0:NP, 0:NP]), [t4, bank_free[b]], quiet=k < KD - 1)
                    xn_free[j % 3] = turned[j] = t5

                def store_tile(j):
                    b, c = 4 + j % 2, slice(j * NP, (j + 1) * NP)
                    v = bank(b).rearrange("p (k c) -> p k c", k=KD)[:, :, 0:NP]
                    t6 = act.do(lambda e: e.copy(yT[0][:, :, c], v), [turned[j]])
                    bank_free[b] = split_lo(dve, yT[1][:, :, c], v, yT[0][:, :, c], [t6])
                modulated = {0: modulate(0)}
                for j in range(NT + 1):
                    if j < NT:
                        norm_tile(j)
                    if j:
                        store_tile(j - 1)
                for j in range(NT):
                    t_b = pool.do(lambda e, j=j: e.tensor_tensor(X[:, j, :], X[:, j, :], bias_out[:], ALU.add), [t_bias, normed[j]])
                return bank_free[4 + (NT - 1) % 2], t_b

            def three_products(out_, lhs, rhs, first, last, after, quiet=False):
                for n, (a, b) in enumerate(((0, 0), (0, 1), (1, 0))):
                    t = pe.do(lambda e, a=a, b=b, n=n: e.matmul(out_, lhs[a], rhs[b], start=first and n == 0, stop=last and n == 2),
                              after, quiet=quiet or n < 2)
                return t

            def attention_block(i):
                fence()
                g = Region(PHASE, ARENA)
                PAIR = 2 * NP
                qk = {c: [g.take(f"{c}{i}_{p}", [128, N], F32R) for p in ("hi", "lo")] for c in "qk"}
                v2 = [g.take(f"v{i}_{p}", [NP, NT, DH], F32R) for p in ("hi", "lo")]
                oT = [g.take(f"oT{i}_{p}", [128, PAIR], F32R) for p in ("hi", "lo")]
                pT = [g.take(f"pT{i}_{p}", [NP, NT, PAIR], F32R) for p in ("hi", "lo")]
                prob = [g.take(f"prob{i}_{n}", [128, N]) for n in range(4)]
                w_in = g.take(f"w_in{i}", [128, KD, DH])
                w2 = [[g.take(f"w{i}_{n}_{p}", [128, KD, DH], F32R) for p in ("hi", "lo")] for n in range(2)]
                wo_in = g.take(f"wo_in{i}", [128, D])
                wo2 = [g.take(f"wo{i}_{p}", [128, D], F32R) for p in ("hi", "lo")]
                row_max = g.take(f"row_max{i}", [NP, NT])
                row_sum = g.take(f"row_sum{i}", [NP, NT])
                t_bo = dma("bias_out", sp, bias_out[:], row_on_partitions(L3["bo"][i]))
                w_ready, w_used, n_load = {}, [None, None], [0]

                def load_head(c, h):
                    n = n_load[0] % 2
                    n_load[0] += 1
                    t = split_weight("w_in", w_in, w2[n][0], w2[n][1],
                                     L3["w" + c][i].rearrange("(k p) n -> p k n", p=128)[:, :, h * DH:(h + 1) * DH], [w_used[n]])
                    w_ready[c, h] = (n, t)

                def load_wo(h, used):
                    w_ready["o", h] = split_weight("w_o", wo_in, wo2[0], wo2[1], L3["wo"][i][h * DH:(h + 1) * DH, :], [used])

                def project(c, h, b0, t_y, store):
                    buf, t_w = w_ready[c, h]
                    for q in range(3):
                        cols = slice(q * BANK, min((q + 1) * BANK, N))
                        ps = psum[:, (b0 + q) * BANK:(b0 + q) * BANK + cols.stop - cols.start]
                        for k in range(KD):
                            t = three_products(ps, [p[:, k, :] for p in w2[buf]], [p[:, k, cols] for p in yT], k == 0, k == KD - 1,
                                               [t_w, t_y, bank_free[b0 + q]])
                        bank_free[b0 + q] = store(cols, ps, t)
                    w_used[buf] = t

                def project_qk(c, h, b0, t_y):
                    bias = bias_cols[:, "qk".index(c), i, h:h + 1]

                    def store(cols, ps, t):
                        hi, lo = (p[:, cols] for p in qk[c])
                        t = act.do(lambda e: e.activation(hi, ps, ACT.Identity, bias=bias), [t])
                        return dve.do(lambda e: e.scalar_tensor_tensor(lo, ps, bias, hi.bitcast(F32), ALU.add, ALU.subtract), [t])
                    project(c, h, b0, t_y, store)
                    t_qk[c] = bank_free[b0 + 2]

                prob_free, n_prob = [None] * 4, [0]

                def next_prob():
                    n_prob[0] += 1
                    return (n_prob[0] - 1) % 4
                t_qk = {}
                load_head("q", 0)
                load_head("k", 0)
                load_wo(0, None)
                t_y, t_b = cond_norm(i, 1, Region(PHASE, PHASE + 20000), t_bo)
                project_qk("q", 0, 0, t_y)
                load_head("v", 0)
                project_qk("k", 0, 3, t_y)
                if HEADS > 1:
                    load_head("q", 1)

                def head(h):
                    t_q, t_k = t_qk["q"], t_qk["k"]
                    soft, turned = {}, {}
                    v_ready = []

                    def scores(n):
                        for q in range(3):
                            w = min(BANK, N - q * BANK)
                            t = three_products(psum[0:NP, q * BANK:q * BANK + w], [p[:, n * NP:(n + 1) * NP] for p in qk["q"]],
                                               [p[:, q * BANK:q * BANK + w] for p in qk["k"]], True, True, [t_q, t_k, bank_free[q]])
                        p = next_prob()
                        P, mx = prob[p][0:NP, :], row_max[:, n:n + 1]
                        t = dve.do(lambda e: e.tensor_tensor_reduce(P, psum[0:NP, 0:N], edge_term[:, n, :], 1.0, 3 * MASKED,
                                                                    ALU.add, ALU.max, mx), [t, prob_free[p]])
                        bank_free[0:3] = [t] * 3
                        t = dve.do(lambda e: e.tensor_scalar(mx, mx, -SCALE, None, ALU.mult), [t])
                        soft[n] = (p, t)

                    def exponentials(n):
                        p, t = soft[n]
                        P, mx, sm = prob[p][0:NP, :], row_max[:, n:n + 1], row_sum[:, n:n + 1]
                        t = act.do(lambda e: e.activation(P, P, ACT.Exp, bias=mx, scale=SCALE, accum_out=sm), [t])
                        soft[n] = (p, t)

                    def normalise(n):
                        p, t = soft[n]
                        P, sm = prob[p][0:NP, :], row_sum[:, n:n + 1]
                        t = dve.do(lambda e: e.reciprocal(sm, sm), [t])
                        t = dve.do(lambda e: e.tensor_tensor(sm, sm, has_edge[:, n:n + 1], ALU.mult), [t])
                        t = act.do(lambda e: e.activation(P, P, ACT.Identity, scale=sm), [t])
                        soft[n] = (p, t)

                    def turn(n):
                        p, t0 = soft[n]
                        turned[n] = []
                        for q in range(3):
                            m = min(4, NT - 4 * q)
                            b = 3 + q
                            v = bank(b, m * 128, NP).rearrange("p (k c) -> p k c", c=128)
                            for k in range(m):
                                d = 4 * q + k
                                t = pe.do(lambda e, k=k, d=d, v=v: e.transpose(v[:, k, 0:NP], prob[p][0:NP, d * NP:(d + 1) * NP], ident[0:NP, 0:NP]),
                                          [t0, bank_free[b]], quiet=k < m - 1)
                            half = slice((n % 2) * NP, (n % 2 + 1) * NP)
                            hi, lo = (x_[:, 4 * q:4 * q + m, half] for x_ in pT)
                            t1 = act.do(lambda e, v=v, hi=hi: e.copy(hi, v[:, :, 0:NP]), [t])
                            bank_free[b] = split_lo(dve, lo, v[:, :, 0:NP], hi, [t1])
                            turned[n].append(bank_free[b])
                        prob_free[p] = t

                    def mix(g):
                        for d in range(NT):
                            t = three_products(bank(6, PAIR), [v[:, d, :] for v in v2], [x_[:, d, :] for x_ in pT], d == 0, d == NT - 1,
                                               [turned[2 * g][d // 4], turned[2 * g + 1][d // 4], v_ready[d // 4], bank_free[6]])
                        t = act.do(lambda e: e.copy(oT[0][:], bank(6, PAIR)), [t])
                        bank_free[6] = split_lo(dve, oT[1][:], bank(6, PAIR), oT[0][:], [t])
                        return bank_free[6]

                    def output_product(g, t_o):
                        for n, b in ((2 * g, 7), (2 * g + 1, 6)):
                            half = slice((n % 2) * NP, (n % 2 + 1) * NP)
                            t = three_products(bank(b, D, NP), [p[:, half] for p in oT], [p[:] for p in wo2], True, True,
                                               [w_ready["o", h], t_o, bank_free[b]])
                            bank_free[b] = dve.do(lambda e, n=n, b=b: e.tensor_tensor(X[:, n, :], bank(b, D, NP), X[:, n, :], ALU.add), [t, t_b])
                            if h == HEADS - 1:
                                norm_stats(n, bank_free[b])
                        return t

                    def make_v():
                        p = next_prob()
                        vT = prob[p]
                        bias = bias_cols[:, 2, i, h:h + 1]
                        free = prob_free[p]
                        ready = {}

                        def store(cols, ps, t):
                            ready["t"] = act.do(lambda e: e.activation(vT[:, cols], ps, ACT.Identity, bias=bias), [t, free])
                            return ready["t"]
                        project("v", h, 0, t_y, store)
                        return p, ready["t"]

                    def turn_v(p, t0):
                        for q in range(3):
                            m, b = min(4, NT - 4 * q), 3 + q
                            v = bank(b, m * 128, NP).rearrange("p (k c) -> p k c", c=128)
                            for k in range(m):
                                d = 4 * q + k
                                t = pe.do(lambda e, k=k, d=d, v=v: e.transpose(v[:, k, :], prob[p][:, d * NP:(d + 1) * NP], ident[:]),
                                          [t0, bank_free[b]], quiet=k < m - 1)
                            hi, lo = (x_[:, 4 * q:4 * q + m, :] for x_ in v2)
                            t1 = act.do(lambda e, v=v, hi=hi: e.copy(hi, v), [t])
                            bank_free[b] = split_lo(dve, lo, v, hi, [t1])
                            v_ready.append(bank_free[b])
                        prob_free[p] = t
                    last = h + 1 == HEADS
                    v_at = make_v()
                    if not last:
                        load_head("k", h + 1)
                    scores(0)
                    exponentials(0)
                    turn_v(*v_at)
                    normalise(0)
                    scores(1)
                    exponentials(1)
                    PAIRS = NT // 2
                    for g in range(PAIRS):
                        more = 2 * g + 2 < NT
                        turn(2 * g)
                        normalise(2 * g + 1)
                        if g:
                            output_product(g - 1, t_o)
                        if more:
                            scores(2 * g + 2)
                        elif not last:
                            project_qk("q", h + 1, 0, t_y)
                            load_head("v", h + 1)
                        turn(2 * g + 1)
                        if more:
                            exponentials(2 * g + 2)
                            normalise(2 * g + 2)
                            scores(2 * g + 3)
                            exponentials(2 * g + 3)
                        elif not last:
                            project_qk("k", h + 1, 3, t_y)
                            if h + 2 < HEADS:
                                load_head("q", h + 2)
                        t_o = mix(g)
                    t = output_product(PAIRS - 1, t_o)
                    if not last:
                        load_wo(h + 1, t)
                for h in range(HEADS):
                    head(h)

            def mlp_block(i):
                fence()
                g = Region(PHASE, ARENA)
                hT = [g.take(f"hT{i}_{p}", [128, KD, N], F32R) for p in ("hi", "lo")]
                m_in = g.take(f"m_in{i}", [128, KD, D])
                m1 = [g.take(f"m1_{i}_{p}", [128, KD, D], F32R) for p in ("hi", "lo")]
                m2 = [g.take(f"m2_{i}_{p}", [128, KD, D], F32R) for p in ("hi", "lo")]
                relu = g.take(f"relu{i}", [128, N])
                t_b2 = dma("bias_out", sp, bias_out[:], row_on_partitions(L3["m_b2"][i]))
                t_m1 = split_weight("m_in", m_in, m1[0], m1[1], L3["m_w1"][i].rearrange("(k p) n -> p k n", p=128), [])
                t_y, t_b = cond_norm(i, 2, Region(PHASE, PHASE + 20000), t_b2)
                t_m2 = split_weight("m_in", m_in, m2[0], m2[1], L3["m_w2"][i].rearrange("(k p) n -> p k n", p=128), [])
                relu_free = None
                for m in range(KD):
                    b0 = 3 * (m % 2)
                    for q in range(3):
                        w = min(BANK, N - q * BANK)
                        for k in range(KD):
                            t = three_products(psum[:, (b0 + q) * BANK:(b0 + q) * BANK + w], [p[:, k, m * 128:(m + 1) * 128] for p in m1],
                                               [p[:, k, q * BANK:q * BANK + w] for p in yT], k == 0, k == KD - 1,
                                               [t_m1, t_y] + bank_free[b0:b0 + 3])
                    ps = psum[:, b0 * BANK:b0 * BANK + N]
                    t1 = act.do(lambda e, m=m, ps=ps: e.activation(relu[:], ps, ACT.Relu, bias=bias_cols[:, 3, i, m:m + 1]), [t, relu_free])
                    bank_free[b0:b0 + 3] = [t1] * 3
                    t2 = act.do(lambda e, m=m: e.copy(hT[0][:, m, :], relu[:]), [t1])
                    relu_free = split_lo(dve, hT[1][:, m, :], relu[:], hT[0][:, m, :], [t2])
                for j in range(NT):
                    b = 6 + j % 2
                    for k in range(KD):
                        t = three_products(bank(b, D, NP), [p[:, k, j * NP:(j + 1) * NP] for p in hT], [p[:, k, :] for p in m2],
                                           k == 0, k == KD - 1, [relu_free, t_m2, bank_free[b]])
                    bank_free[b] = dve.do(lambda e, j=j, b=b: e.tensor_tensor(X[:, j, :], bank(b, D, NP), X[:, j, :], ALU.add), [t, t_b])
                    norm_stats(j, bank_free[b])

            load_condition(0, 1, pool.do(lambda e: e.memset(cond_in[:], 0.0)))
            for j in range(NT):
                norm_stats(j, x_ready[j])
            finish_stats()
            for i in range(BLOCKS):
                attention_block(i)
                finish_stats()
                if stop_after == f"xa{i}":
                    return [dve.last(), cond_loaded["t"]]
                mlp_block(i)
                if i + 1 < BLOCKS:
                    finish_stats()
                if stop_after == f"xb{i}":
                    return [dve.last(), cond_loaded["t"]]
            fence()
            before = Region(PHASE, ARENA).take("x_before", [NP, NT, D])
            t = dma("x_in", sp, before[:], tiles_of(x_in), [t_save])
            ready = [dve.do(lambda e, j=j: e.tensor_tensor(X[:, j, :], X[:, j, :], before[:, j, :], ALU.add), [t]) for j in range(NT)]
            return layer_norm(ready)

        x_ready = layer3(x_ready)
        finish_program(nc, ctx, out, X, dma, (pe, dve, act, pool, sp), x_ready, NP)


def finish_program(nc, ctx, out, X, dma, queues, ready, NP):
    pe, dve, act, pool, sp = queues
    t = dma("out", sp, out.rearrange("(j p) d -> p j d", p=NP), X[:], ready)
    sp.wait([t])
    block = ctx.enter_context(nc.Block())
    block.tensor(lambda e: pe.run(e))
    block.vector(lambda e: dve.run(e))
    block.scalar(lambda e: act.run(e))
    block.gpsimd(lambda e: pool.run(e))
    block.sync(lambda e: sp.run(e))


_INS = ['x', 'src', 'dst', 'node_vec1', 'L0_gnn_norm1_g', 'L0_gnn_norm1_b', 'L0_gnn_norm2_g', 'L0_gnn_norm2_b', 'L0_gnn_W_conv',
        'L0_gnn_b_conv', 'L0_gnn_Wq', 'L0_gnn_Wk', 'L0_gnn_Wv', 'L0_gnn_Wo', 'L0_gnn_proj', 'L1_gnn_Ws', 'L1_gnn_Wb', 'L1_gnn_a_w',
        'L1_gnn_a_b', 'L2_gnn_W', 'L2_gnn_b', 'L2_gnn_gamma', 'L2_gnn_beta', 'L3_gnn_f_w1', 'L3_gnn_f_b1', 'L3_gnn_f_w2',
        'L3_gnn_f_b2', 'L3_gnn_s1_w', 'L3_gnn_s1_b', 'L3_gnn_b1_w', 'L3_gnn_b1_b', 'L3_gnn_wq', 'L3_gnn_bq', 'L3_gnn_wk',
        'L3_gnn_bk', 'L3_gnn_wv', 'L3_gnn_bv', 'L3_gnn_wo', 'L3_gnn_bo', 'L3_gnn_s2_w', 'L3_gnn_s2_b', 'L3_gnn_b2_w',
        'L3_gnn_b2_b', 'L3_gnn_m_w1', 'L3_gnn_m_b1', 'L3_gnn_m_w2', 'L3_gnn_m_b2']


def build(nc, args, out, stop_after=None):
    layer = lambda p: {k[len(p):]: v for k, v in args.items() if k.startswith(p)}
    build_layers(nc, args["x"], args["src"], args["dst"], args["node_vec1"], layer("L0_gnn_"), layer("L1_gnn_"),
                 layer("L2_gnn_"), layer("L3_gnn_"), out, stop_after)


def kernel(**inputs):
    import numpy as _np
    import concourse.bacc as _bacc
    from concourse import mybir as _mybir
    from concourse.bass_utils import run_bass_kernel_spmd as _run

    nc = _bacc.Bacc("TRN2", target_bir_lowering=False, num_devices=1)
    arrays, args = {}, {}
    for name in _INS:
        a = _np.ascontiguousarray(inputs[name])
        arrays[f"in_{name}"] = a
        args[name] = nc.dram_tensor(f"in_{name}", a.shape, _mybir.dt.from_np(a.dtype), kind="ExternalInput").ap()
    out = nc.dram_tensor("out", inputs["x"].shape, _mybir.dt.float32, kind="ExternalOutput").ap()
    build(nc, args, out)
    return _run(nc, [arrays], core_ids=[0]).results[0]["out"]
```
